# Optimizing a Trainium2 kernel written in Bass

```python
import numpy as np
import jax
import jax.numpy as jnp

def _softmax(x, axis=-1):
    return jax.nn.softmax(x, axis=axis)

def _gelu(x):
    return jax.nn.gelu(x, approximate=True)

def _silu(x):
    return jax.nn.silu(x)

def _sigmoid(x):
    return jax.nn.sigmoid(x)

def _layernorm(x, axis=-1, eps=1e-05):
    m = jnp.mean(x, axis=axis, keepdims=True)
    v = jnp.var(x, axis=axis, keepdims=True)
    return (x - m) / jnp.sqrt(v + eps)

def _scatter_add(tgt, idx, src, axis=0):
    return tgt.at[idx].add(src)

def _segment_sum(src, seg, n):
    return jax.ops.segment_sum(src, seg, n)
kernel_name = 'mk_flamingo_gated_d4_seqx_r8_74ab02'

def setup_inputs(seed: int=0):
    np.random.seed(seed)
    _w = jnp.asarray

    def _rec_inputs():
        import jax
        import jax.numpy as jnp
        _rk = jax.random.key(seed)
        x = 2.818e-05 + 1 * jax.random.normal(jax.random.fold_in(_rk, 1), (32, 128, 128), jnp.float32)
        _lenS = 128 - jax.random.randint(jax.random.fold_in(_rk, 7), (32,), 0, max(1, 128 // 4) + 1, jnp.int32)
        _lenS2 = 128 - jax.random.randint(jax.random.fold_in(_rk, 8), (32,), 0, max(1, 128 // 4) + 1, jnp.int32)
        _ctx_2048P = jax.random.normal(jax.random.fold_in(_rk, 11), (32, 16, 256), jnp.float32)
        _ctx_2048c = jax.random.dirichlet(jax.random.fold_in(_rk, 511), 0.3 * jnp.ones((16,), jnp.float32), (32, 128))
        _ctx_2048t = jnp.einsum('bsk,bkd->bsd', _ctx_2048c, _ctx_2048P)
        _ctx_2048t = _ctx_2048t * jax.lax.rsqrt(jnp.mean(jnp.square(_ctx_2048t)) + 1e-12) * 0.953939
        ctx_2048 = -0.000125008 + 0.999885 * (_ctx_2048t + 0.3 * jax.random.normal(jax.random.fold_in(_rk, 611), (32, 128, 256), jnp.float32))
        itok_Bx1_68_817 = jax.random.randint(jax.random.fold_in(_rk, 14), (32, 1), 68, 818, jnp.int32)
        _validS = jnp.arange(128)[None, :] < _lenS[:, None]
        _validS2 = jnp.arange(128)[None, :] < _lenS2[:, None]
        _causal = jnp.tril(jnp.ones((128, 128), dtype=bool))
        mask_BxS2_fk1 = jnp.where(jnp.broadcast_to(_validS2[:, :], (32, 128)), 1.0, 0.0).astype(jnp.float32)
        mask_BxS2_if0 = jnp.where(jnp.ones((32, 128), dtype=bool), 4, 0).astype(jnp.int32)
        _g = jax.random.normal(jax.random.fold_in(_rk, 9001), (2, 4), jnp.float32)
        _g = jnp.sign(_g) * jnp.maximum(jnp.abs(_g), 1.0) + (_g == 0) * 1.0
        g_xattn = _g[0]
        g_ffn = _g[1]
        return (x, ctx_2048, itok_Bx1_68_817, mask_BxS2_fk1, mask_BxS2_if0, g_xattn, g_ffn)
    x, ctx_2048, itok_Bx1_68_817, mask_BxS2_fk1, mask_BxS2_if0, g_xattn, g_ffn = _rec_inputs()

    def _L0_xattn_setup():
        import jax, jax.numpy as jnp
        import numpy as np
        B, S, T = (32, 64, 64)
        SRC_SIZE, TGT_SIZE, OUT_SIZE, NUM_HEAD = (256, 128, 128, 8)
        HEAD_DIM = OUT_SIZE // NUM_HEAD
        key = jax.random.key(seed)
        ks = jax.random.split(key, 12)
        src = jax.random.normal(ks[0], (B, S, SRC_SIZE), dtype=jnp.float32)
        tgt = jax.random.normal(ks[1], (B, T, TGT_SIZE), dtype=jnp.float32)
        src_mask = (jax.random.uniform(ks[2], (B, S)) > 0.3).astype(jnp.float32)
        src_mask = src_mask.at[:, 0].set(1.0)
        tgt_mask = (jax.random.uniform(ks[3], (B, T)) > 0.3).astype(jnp.float32)
        tgt_mask = tgt_mask.at[:, 0].set(1.0)

        def lin(k, out_f, in_f):
            return jax.random.normal(k, (out_f, in_f), dtype=jnp.float32) / np.sqrt(in_f)
        W_src = lin(ks[4], 2 * OUT_SIZE, SRC_SIZE)
        b_src = jnp.zeros((2 * OUT_SIZE,), jnp.float32)
        W_tgt = lin(ks[5], OUT_SIZE, TGT_SIZE)
        b_tgt = jnp.zeros((OUT_SIZE,), jnp.float32)
        W_out = lin(ks[6], OUT_SIZE, OUT_SIZE + TGT_SIZE)
        b_out = jnp.zeros((OUT_SIZE,), jnp.float32)
        return {'src': src, 'tgt': tgt, 'src_mask': src_mask, 'tgt_mask': tgt_mask, 'W_src': W_src, 'b_src': b_src, 'W_tgt': W_tgt, 'b_tgt': b_tgt, 'W_out': W_out, 'b_out': b_out}
    _L0_xattn_all = _L0_xattn_setup()
    _L0_xattn_in = {k: v for k, v in _L0_xattn_all.items() if k in ('W_src', 'b_src', 'W_tgt', 'b_tgt', 'W_out', 'b_out')}
    del _L0_xattn_all

    def _L0_ffn_setup():
        import jax, jax.numpy as jnp
        import numpy as np
        D_MODEL = 128
        N_EXPERTS = 8
        TOP_K = 2
        key = jax.random.key(seed)
        ks = jax.random.split(key, 8)
        d, e = (D_MODEL, N_EXPERTS)
        s = 1.0 / np.sqrt(d)
        return {'x': jax.random.normal(ks[0], (4, 256, d), dtype=jnp.float32), 'W_gate': jax.random.uniform(ks[1], (d, e), jnp.float32, -s, s), 'b_gate': jax.random.uniform(ks[2], (e,), jnp.float32, -s, s), 'W1': jax.random.uniform(ks[3], (e, d, d), jnp.float32, -s, s), 'b1': jax.random.uniform(ks[4], (e, d), jnp.float32, -s, s), 'W2': jax.random.uniform(ks[5], (e, d, d), jnp.float32, -s, s), 'b2': jax.random.uniform(ks[6], (e, d), jnp.float32, -s, s)}
    _L0_ffn_all = _L0_ffn_setup()
    _L0_ffn_in = {k: v for k, v in _L0_ffn_all.items() if k in ('W_gate', 'b_gate', 'W1', 'b1', 'W2', 'b2')}
    del _L0_ffn_all

    def _L1_xattn_setup():
        import jax, jax.numpy as jnp
        import numpy as np
        B, L, P = (4, 512, 128)
        D_MODEL = 128
        D_GLOBAL = 256
        HEADDIM = 32
        EPSILON = 0.001
        RMS_EPS = 1e-05

        def rmsnorm(x, g, eps=RMS_EPS):
            var = jnp.mean(jnp.square(x), axis=-1, keepdims=True)
            return x * jax.lax.rsqrt(var + eps) * g

        def _hnet_depool(h, h_patch_full, patch_lens):
            h_patch = h_patch_full[..., :D_MODEL]
            bsz, plen = (h_patch.shape[0], h_patch.shape[1])
            seqlen = h.shape[1]
            logp = jnp.full((bsz, plen), -EPSILON, dtype=jnp.float32)
            bidx = jnp.cumsum(patch_lens, axis=1) - 1
            boundary_mask = jnp.zeros((bsz, seqlen), dtype=jnp.int32)
            boundary_mask = boundary_mask.at[jnp.arange(bsz)[:, None], bidx].set(1)
            dt = (-jnp.log(-jnp.expm1(logp))).astype(h_patch.dtype)
            x = h_patch / dt[..., None]
            n_heads = D_MODEL // HEADDIM
            A = -jnp.ones((n_heads,), dtype=jnp.float32)
            bcoef = jnp.exp(logp).astype(h_patch.dtype)
            x4 = x.reshape(bsz, plen, n_heads, HEADDIM)
            a = jnp.exp(dt[:, :, None] * A[None, None, :])
            u = (dt * bcoef)[:, :, None, None] * x4
            a_b = jnp.broadcast_to(a[..., None], u.shape)

            def comb(lft, rgt):
                aL, uL = lft
                aR, uR = rgt
                return (aL * aR, uL * aR + uR)
            _, s = jax.lax.associative_scan(comb, (a_b, u), axis=1)
            depool = s.reshape(bsz, plen, D_MODEL)
            plug = jnp.clip(jnp.cumsum(boundary_mask, axis=1) - 1, 0, plen - 1)
            depool_out = depool[jnp.arange(bsz)[:, None], plug]
            return depool_out + h
        key = jax.random.key(seed)
        k1, k2, k3, k4 = jax.random.split(key, 4)
        embeds = jax.random.normal(k1, (B, L, D_MODEL), dtype=jnp.float32)
        patch_embeds = jax.random.normal(k2, (B, P, D_GLOBAL), dtype=jnp.float32)
        patch_lens = jnp.full((B, P), L // P, dtype=jnp.int64)
        W_in = jax.random.normal(k3, (D_MODEL, D_MODEL), dtype=jnp.float32) * 0.02
        b_in = jnp.zeros((D_MODEL,), dtype=jnp.float32)
        g_res = jnp.ones((D_MODEL,), dtype=jnp.float32)
        g_init = jnp.ones((D_GLOBAL,), dtype=jnp.float32)
        return {'embeds': embeds, 'patch_embeds': patch_embeds, 'patch_lens': patch_lens, 'W_in': W_in, 'b_in': b_in, 'g_res': g_res, 'g_init': g_init}
    _L1_xattn_all = _L1_xattn_setup()
    _L1_xattn_in = {k: v for k, v in _L1_xattn_all.items() if k in ('W_in', 'b_in', 'g_res', 'g_init')}
    del _L1_xattn_all

    def _L1_ffn_setup():
        import jax, jax.numpy as jnp
        import numpy as np
        HIDDEN = 128
        N_ROUTED = 16
        N_SHARED = 2
        TOP_K = 2
        MID_R = HIDDEN // 4
        MID_S = HIDDEN // 2
        key = jax.random.key(seed)
        ks = jax.random.split(key, 8)
        s = 0.02
        return {'x': jax.random.normal(ks[0], (2, 128, HIDDEN), dtype=jnp.float32), 'router_w': jax.random.normal(ks[1], (HIDDEN, N_ROUTED), dtype=jnp.float32) * s, 'wg_r': jax.random.normal(ks[2], (N_ROUTED, HIDDEN, MID_R), dtype=jnp.float32) * s, 'wu_r': jax.random.normal(ks[3], (N_ROUTED, HIDDEN, MID_R), dtype=jnp.float32) * s, 'wd_r': jax.random.normal(ks[4], (N_ROUTED, MID_R, HIDDEN), dtype=jnp.float32) * s, 'wg_s': jax.random.normal(ks[5], (N_SHARED, HIDDEN, MID_S), dtype=jnp.float32) * s, 'wu_s': jax.random.normal(ks[6], (N_SHARED, HIDDEN, MID_S), dtype=jnp.float32) * s, 'wd_s': jax.random.normal(ks[7], (N_SHARED, MID_S, HIDDEN), dtype=jnp.float32) * s}
    _L1_ffn_all = _L1_ffn_setup()
    _L1_ffn_in = {k: v for k, v in _L1_ffn_all.items() if k in ('router_w', 'wg_r', 'wu_r', 'wd_r', 'wg_s', 'wu_s', 'wd_s')}
    del _L1_ffn_all

    def _L2_xattn_setup():
        import jax, jax.numpy as jnp
        import numpy as np
        B, N, DIM = (8, 512, 128)
        M, CTX = (32, 256)
        HEADS, DH = (16, 64)
        INNER = HEADS * DH
        EPS = 1e-06

        def _split_heads(t):
            b, n, _ = t.shape
            return t.reshape(b, n, HEADS, DH).transpose(0, 2, 1, 3)
        key = jax.random.key(seed)
        ks = jax.random.split(key, 6)
        x = jax.random.normal(ks[0], (B, N, DIM), dtype=jnp.float32)
        context = jax.random.normal(ks[1], (B, M, CTX), dtype=jnp.float32)
        Wq = jax.random.normal(ks[2], (DIM, INNER), dtype=jnp.float32) / np.sqrt(DIM)
        Wkv = jax.random.normal(ks[3], (CTX, 2 * INNER), dtype=jnp.float32) / np.sqrt(CTX)
        null_kv = jax.random.normal(ks[4], (2, DH), dtype=jnp.float32) / np.sqrt(2.0)
        Wout = jax.random.normal(ks[5], (INNER, DIM), dtype=jnp.float32) / np.sqrt(INNER)
        ln_scale = jnp.ones((DIM,), dtype=jnp.float32)
        ln_bias = jnp.zeros((DIM,), dtype=jnp.float32)
        return {'x': x, 'context': context, 'Wq': Wq, 'Wkv': Wkv, 'null_kv': null_kv, 'Wout': Wout, 'ln_scale': ln_scale, 'ln_bias': ln_bias}
    _L2_xattn_all = _L2_xattn_setup()
    _L2_xattn_in = {k: v for k, v in _L2_xattn_all.items() if k in ('Wq', 'Wkv', 'null_kv', 'Wout', 'ln_scale', 'ln_bias')}
    del _L2_xattn_all

    def _L2_ffn_setup():
        import jax, jax.numpy as jnp
        import numpy as np
        B, S, D, H, F = (4, 512, 128, 16, 512)
        CAP = 0.125
        ROPE_BASE = 10000.0

        def rmsnorm(x, g):
            return x * jax.lax.rsqrt(jnp.mean(x * x, -1, keepdims=True) + 1e-06) * g

        def rope(t, pos):
            hd = t.shape[-1]
            inv = 1.0 / ROPE_BASE ** (jnp.arange(0, hd, 2, dtype=jnp.float32) / hd)
            f = pos[:, None, :, None].astype(jnp.float32) * inv
            emb = jnp.concatenate([f, f], axis=-1)
            cos, sin = (jnp.cos(emb), jnp.sin(emb))
            rot = jnp.concatenate([-t[..., hd // 2:], t[..., :hd // 2]], axis=-1)
            return t * cos + rot * sin
        key = jax.random.key(seed)
        ks = jax.random.split(key, 9)
        scale = 0.02
        x = jax.random.normal(ks[0], (B, S, D), jnp.float32)
        causal = jnp.where(jnp.tril(jnp.ones((S, S), bool)), 0.0, -1000000000.0).astype(jnp.float32)
        attention_mask = jnp.broadcast_to(causal[None, None], (B, 1, S, S))
        position_ids = jnp.broadcast_to(jnp.arange(S, dtype=jnp.int32), (B, S))
        return {'x': x, 'attention_mask': attention_mask, 'position_ids': position_ids, 'router_w': jax.random.normal(ks[1], (D, 1), jnp.float32) * scale, 'router_b': jnp.zeros((1,), jnp.float32), 'wq': jax.random.normal(ks[2], (D, D), jnp.float32) * scale, 'wk': jax.random.normal(ks[3], (D, D), jnp.float32) * scale, 'wv': jax.random.normal(ks[4], (D, D), jnp.float32) * scale, 'wo': jax.random.normal(ks[5], (D, D), jnp.float32) * scale, 'w1': jax.random.normal(ks[6], (D, F), jnp.float32) * scale, 'w2': jax.random.normal(ks[7], (F, D), jnp.float32) * scale, 'ln1': jnp.ones((D,), jnp.float32), 'ln2': jnp.ones((D,), jnp.float32)}
    _L2_ffn_all = _L2_ffn_setup()
    _L2_ffn_in = {k: v for k, v in _L2_ffn_all.items() if k in ('attention_mask', 'position_ids', 'router_w', 'router_b', 'wq', 'wk', 'wv', 'wo', 'w1', 'w2', 'ln1', 'ln2')}
    del _L2_ffn_all

    def _L3_xattn_setup():
        import jax, jax.numpy as jnp
        import numpy as np
        UNITS = 128
        NUM_HEADS = 16
        MASK_VALUE = -1000000000000.0

        def _split_heads(x, n):
            B, S, D = x.shape
            return x.reshape(B, S, n, D // n).transpose(0, 2, 1, 3)
        key = jax.random.key(seed)
        k1, k2, k3, k4 = jax.random.split(key, 4)
        B, S = (8, 128)
        memory = jax.random.normal(k1, (B, S, 2 * UNITS), dtype=jnp.float32)
        query = jax.random.normal(k2, (B, S, UNITS), dtype=jnp.float32)
        b = jax.random.normal(k3, (S,), dtype=jnp.float32)
        seq_len = jax.random.randint(k4, (B, 1), 0, S, dtype=jnp.int32)
        return {'memory': memory, 'query': query, 'b': b, 'seq_len': seq_len}
    _L3_xattn_all = _L3_xattn_setup()
    _L3_xattn_in = {k: v for k, v in _L3_xattn_all.items() if k in ('b',)}
    del _L3_xattn_all

    def _L3_ffn_setup():
        import jax, jax.numpy as jnp
        import numpy as np
        D_MODEL = 128
        EXPANSION = 4
        D_HIDDEN = D_MODEL * EXPANSION
        NUM_STAGES = int(np.log2(D_HIDDEN))

        def butterfly(y, weights, dim):
            lead = y.shape[:-1]
            for stage in range(weights.shape[0]):
                s = 2 ** stage
                nb = dim // (2 * s)
                yr = y.reshape(*lead, nb, 2, s)
                a = yr[..., 0, :]
                b = yr[..., 1, :]
                w = weights[stage].reshape(nb, s, 2, 2)
                na = w[..., 0, 0] * a + w[..., 0, 1] * b
                nb2 = w[..., 1, 0] * a + w[..., 1, 1] * b
                y = jnp.stack([na, nb2], axis=-2).reshape(*lead, dim)
            return y
        key = jax.random.key(seed)
        ks = jax.random.split(key, 6)
        B, S = (4, 256)
        x = jax.random.normal(ks[0], (B, S, D_MODEL), jnp.float32)
        W_exp = jax.random.normal(ks[1], (D_MODEL, D_HIDDEN), jnp.float32) * 0.02
        b_exp = jnp.zeros((D_HIDDEN,), jnp.float32)
        up_weights = jax.random.normal(ks[2], (NUM_STAGES, D_HIDDEN // 2, 2, 2), jnp.float32) * 0.02
        up_bias = jnp.zeros((D_HIDDEN,), jnp.float32)
        down_weights = jax.random.normal(ks[3], (NUM_STAGES, D_HIDDEN // 2, 2, 2), jnp.float32) * 0.02
        W_con = jax.random.normal(ks[4], (D_HIDDEN, D_MODEL), jnp.float32) * 0.02
        b_con = jnp.zeros((D_MODEL,), jnp.float32)
        down_bias = jnp.zeros((D_MODEL,), jnp.float32)
        return dict(x=x, W_exp=W_exp, b_exp=b_exp, up_weights=up_weights, up_bias=up_bias, down_weights=down_weights, W_con=W_con, b_con=b_con, down_bias=down_bias)
    _L3_ffn_all = _L3_ffn_setup()
    _L3_ffn_in = {k: v for k, v in _L3_ffn_all.items() if k in ('W_exp', 'b_exp', 'up_weights', 'up_bias', 'down_weights', 'W_con', 'b_con', 'down_bias')}
    del _L3_ffn_all
    return {'x': x, 'ctx_2048': ctx_2048, 'itok_Bx1_68_817': itok_Bx1_68_817, 'mask_BxS2_fk1': mask_BxS2_fk1, 'mask_BxS2_if0': mask_BxS2_if0, 'g_xattn': g_xattn, 'g_ffn': g_ffn, 'L0_xattn_W_src': _L0_xattn_in['W_src'], 'L0_xattn_b_src': _L0_xattn_in['b_src'], 'L0_xattn_W_tgt': _L0_xattn_in['W_tgt'], 'L0_xattn_b_tgt': _L0_xattn_in['b_tgt'], 'L0_xattn_W_out': _L0_xattn_in['W_out'], 'L0_xattn_b_out': _L0_xattn_in['b_out'], 'L0_ffn_W_gate': _L0_ffn_in['W_gate'], 'L0_ffn_b_gate': _L0_ffn_in['b_gate'], 'L0_ffn_W1': _L0_ffn_in['W1'], 'L0_ffn_b1': _L0_ffn_in['b1'], 'L0_ffn_W2': _L0_ffn_in['W2'], 'L0_ffn_b2': _L0_ffn_in['b2'], 'L1_xattn_W_in': _L1_xattn_in['W_in'], 'L1_xattn_b_in': _L1_xattn_in['b_in'], 'L1_xattn_g_res': _L1_xattn_in['g_res'], 'L1_xattn_g_init': _L1_xattn_in['g_init'], 'L1_ffn_router_w': _L1_ffn_in['router_w'], 'L1_ffn_wg_r': _L1_ffn_in['wg_r'], 'L1_ffn_wu_r': _L1_ffn_in['wu_r'], 'L1_ffn_wd_r': _L1_ffn_in['wd_r'], 'L1_ffn_wg_s': _L1_ffn_in['wg_s'], 'L1_ffn_wu_s': _L1_ffn_in['wu_s'], 'L1_ffn_wd_s': _L1_ffn_in['wd_s'], 'L2_xattn_Wq': _L2_xattn_in['Wq'], 'L2_xattn_Wkv': _L2_xattn_in['Wkv'], 'L2_xattn_null_kv': _L2_xattn_in['null_kv'], 'L2_xattn_Wout': _L2_xattn_in['Wout'], 'L2_xattn_ln_scale': _L2_xattn_in['ln_scale'], 'L2_xattn_ln_bias': _L2_xattn_in['ln_bias'], 'L2_ffn_attention_mask': _L2_ffn_in['attention_mask'], 'L2_ffn_position_ids': _L2_ffn_in['position_ids'], 'L2_ffn_router_w': _L2_ffn_in['router_w'], 'L2_ffn_router_b': _L2_ffn_in['router_b'], 'L2_ffn_wq': _L2_ffn_in['wq'], 'L2_ffn_wk': _L2_ffn_in['wk'], 'L2_ffn_wv': _L2_ffn_in['wv'], 'L2_ffn_wo': _L2_ffn_in['wo'], 'L2_ffn_w1': _L2_ffn_in['w1'], 'L2_ffn_w2': _L2_ffn_in['w2'], 'L2_ffn_ln1': _L2_ffn_in['ln1'], 'L2_ffn_ln2': _L2_ffn_in['ln2'], 'L3_xattn_b': _L3_xattn_in['b'], 'L3_ffn_W_exp': _L3_ffn_in['W_exp'], 'L3_ffn_b_exp': _L3_ffn_in['b_exp'], 'L3_ffn_up_weights': _L3_ffn_in['up_weights'], 'L3_ffn_up_bias': _L3_ffn_in['up_bias'], 'L3_ffn_down_weights': _L3_ffn_in['down_weights'], 'L3_ffn_W_con': _L3_ffn_in['W_con'], 'L3_ffn_b_con': _L3_ffn_in['b_con'], 'L3_ffn_down_bias': _L3_ffn_in['down_bias']}

def reference(x, ctx_2048, itok_Bx1_68_817, mask_BxS2_fk1, mask_BxS2_if0, g_xattn, g_ffn, L0_xattn_W_src, L0_xattn_b_src, L0_xattn_W_tgt, L0_xattn_b_tgt, L0_xattn_W_out, L0_xattn_b_out, L0_ffn_W_gate, L0_ffn_b_gate, L0_ffn_W1, L0_ffn_b1, L0_ffn_W2, L0_ffn_b2, L1_xattn_W_in, L1_xattn_b_in, L1_xattn_g_res, L1_xattn_g_init, L1_ffn_router_w, L1_ffn_wg_r, L1_ffn_wu_r, L1_ffn_wd_r, L1_ffn_wg_s, L1_ffn_wu_s, L1_ffn_wd_s, L2_xattn_Wq, L2_xattn_Wkv, L2_xattn_null_kv, L2_xattn_Wout, L2_xattn_ln_scale, L2_xattn_ln_bias, L2_ffn_attention_mask, L2_ffn_position_ids, L2_ffn_router_w, L2_ffn_router_b, L2_ffn_wq, L2_ffn_wk, L2_ffn_wv, L2_ffn_wo, L2_ffn_w1, L2_ffn_w2, L2_ffn_ln1, L2_ffn_ln2, L3_xattn_b, L3_ffn_W_exp, L3_ffn_b_exp, L3_ffn_up_weights, L3_ffn_up_bias, L3_ffn_down_weights, L3_ffn_W_con, L3_ffn_b_con, L3_ffn_down_bias):
    import jax
    import jax.numpy as jnp

    def _L0_xattn_ref(src, tgt, src_mask, tgt_mask, W_src, b_src, W_tgt, b_tgt, W_out, b_out):
        import jax, jax.numpy as jnp
        import numpy as np
        B, S, T = (32, 64, 64)
        SRC_SIZE, TGT_SIZE, OUT_SIZE, NUM_HEAD = (256, 128, 128, 8)
        HEAD_DIM = OUT_SIZE // NUM_HEAD
        b, s, _ = src.shape
        t = tgt.shape[1]
        src_trans = jnp.einsum('bsf,of->bso', src, W_src) + b_src
        tgt_trans = jnp.einsum('btf,of->bto', tgt, W_tgt) + b_tgt
        src_trans = src_trans * src_mask[:, :, None]
        tgt_trans = tgt_trans * tgt_mask[:, :, None]
        src_key, src_val = jnp.split(src_trans, 2, axis=2)
        k = src_key.reshape(b, s, NUM_HEAD, HEAD_DIM)
        v = src_val.reshape(b, s, NUM_HEAD, HEAD_DIM)
        q = tgt_trans.reshape(b, t, NUM_HEAD, HEAD_DIM)
        scores = jnp.einsum('bthd,bshd->bhts', q, k) / np.sqrt(HEAD_DIM)
        scores = jnp.where(src_mask[:, None, None, :] == 0, -jnp.inf, scores)
        attn = jax.nn.softmax(scores, axis=-1)
        tgt_update = jnp.einsum('bhts,bshd->bthd', attn, v).reshape(b, t, OUT_SIZE)
        cat_tgt = jnp.concatenate([tgt, tgt_update], axis=2)
        return jnp.einsum('btf,of->bto', cat_tgt, W_out) + b_out

    def _L0_ffn_ref(x, W_gate, b_gate, W1, b1, W2, b2):
        import jax, jax.numpy as jnp
        import numpy as np
        D_MODEL = 128
        N_EXPERTS = 8
        TOP_K = 2
        B, T, d = x.shape
        xf = x.reshape(-1, d)
        scores = xf @ W_gate + b_gate
        topk_val, topk_idx = jax.lax.top_k(scores, TOP_K)
        onehot = jax.nn.one_hot(topk_idx, N_EXPERTS, dtype=xf.dtype)
        w = jnp.einsum('nk,nke->ne', topk_val, onehot)
        h = jax.nn.relu(jnp.einsum('nd,edh->neh', xf, W1) + b1)
        y = jnp.einsum('neh,ehd->ned', h, W2) + b2
        out = jnp.einsum('ned,ne->nd', y, w)
        return out.reshape(B, T, d)

    def _L1_xattn_ref(embeds, patch_embeds, patch_lens, W_in, b_in, g_res, g_init):
        import jax, jax.numpy as jnp
        import numpy as np
        B, L, P = (4, 512, 128)
        D_MODEL = 128
        D_GLOBAL = 256
        HEADDIM = 32
        EPSILON = 0.001
        RMS_EPS = 1e-05

        def rmsnorm(x, g, eps=RMS_EPS):
            var = jnp.mean(jnp.square(x), axis=-1, keepdims=True)
            return x * jax.lax.rsqrt(var + eps) * g

        def _hnet_depool(h, h_patch_full, patch_lens):
            h_patch = h_patch_full[..., :D_MODEL]
            bsz, plen = (h_patch.shape[0], h_patch.shape[1])
            seqlen = h.shape[1]
            logp = jnp.full((bsz, plen), -EPSILON, dtype=jnp.float32)
            bidx = jnp.cumsum(patch_lens, axis=1) - 1
            boundary_mask = jnp.zeros((bsz, seqlen), dtype=jnp.int32)
            boundary_mask = boundary_mask.at[jnp.arange(bsz)[:, None], bidx].set(1)
            dt = (-jnp.log(-jnp.expm1(logp))).astype(h_patch.dtype)
            x = h_patch / dt[..., None]
            n_heads = D_MODEL // HEADDIM
            A = -jnp.ones((n_heads,), dtype=jnp.float32)
            bcoef = jnp.exp(logp).astype(h_patch.dtype)
            x4 = x.reshape(bsz, plen, n_heads, HEADDIM)
            a = jnp.exp(dt[:, :, None] * A[None, None, :])
            u = (dt * bcoef)[:, :, None, None] * x4
            a_b = jnp.broadcast_to(a[..., None], u.shape)

            def comb(lft, rgt):
                aL, uL = lft
                aR, uR = rgt
                return (aL * aR, uL * aR + uR)
            _, s = jax.lax.associative_scan(comb, (a_b, u), axis=1)
            depool = s.reshape(bsz, plen, D_MODEL)
            plug = jnp.clip(jnp.cumsum(boundary_mask, axis=1) - 1, 0, plen - 1)
            depool_out = depool[jnp.arange(bsz)[:, None], plug]
            return depool_out + h
        h = rmsnorm(embeds, g_res)
        h = jnp.einsum('bld,ed->ble', h, W_in) + b_in
        h_patch = rmsnorm(patch_embeds, g_init)
        return _hnet_depool(h, h_patch, patch_lens)

    def _L1_ffn_ref(x, router_w, wg_r, wu_r, wd_r, wg_s, wu_s, wd_s):
        import jax, jax.numpy as jnp
        import numpy as np
        HIDDEN = 128
        N_ROUTED = 16
        N_SHARED = 2
        TOP_K = 2
        MID_R = HIDDEN // 4
        MID_S = HIDDEN // 2
        orig_shape = x.shape
        flat = x.reshape(-1, orig_shape[-1])
        gs = jnp.einsum('td,ndm->tnm', flat, wg_s)
        us = jnp.einsum('td,ndm->tnm', flat, wu_s)
        out = jnp.einsum('tnm,nmd->td', jax.nn.silu(gs) * us, wd_s)
        logits = (flat @ router_w).astype(jnp.float32)
        probs = jax.nn.softmax(logits, axis=-1)
        weights, indices = jax.lax.top_k(probs, TOP_K)
        weights = weights / (weights.sum(axis=-1, keepdims=True) + 1e-09)
        weights = weights.astype(x.dtype)
        comb = jnp.sum(jax.nn.one_hot(indices, N_ROUTED, dtype=x.dtype) * weights[..., None], axis=1)
        g = jnp.einsum('td,edm->tem', flat, wg_r)
        u = jnp.einsum('td,edm->tem', flat, wu_r)
        h = jax.nn.silu(g) * u
        h = h * comb[:, :, None]
        out = out + jnp.einsum('tem,emd->td', h, wd_r)
        return out.reshape(orig_shape)

    def _L2_xattn_ref(x, context, Wq, Wkv, null_kv, Wout, ln_scale, ln_bias):
        import jax, jax.numpy as jnp
        import numpy as np
        B, N, DIM = (8, 512, 128)
        M, CTX = (32, 256)
        HEADS, DH = (16, 64)
        INNER = HEADS * DH
        EPS = 1e-06

        def _split_heads(t):
            b, n, _ = t.shape
            return t.reshape(b, n, HEADS, DH).transpose(0, 2, 1, 3)
        scale = DH ** (-0.5)
        b = x.shape[0]
        q = _split_heads(jnp.einsum('bnd,df->bnf', x, Wq))
        kv = jnp.einsum('bmc,cf->bmf', context, Wkv)
        k, v = jnp.split(kv, 2, axis=-1)
        k, v = (_split_heads(k), _split_heads(v))
        nk = jnp.broadcast_to(null_kv[0], (b, HEADS, 1, DH))
        nv = jnp.broadcast_to(null_kv[1], (b, HEADS, 1, DH))
        k = jnp.concatenate((nk, k), axis=-2)
        v = jnp.concatenate((nv, v), axis=-2)
        q = q * scale
        sim = jnp.einsum('bhid,bhjd->bhij', q, k)
        attn = jax.nn.softmax(sim, axis=-1)
        out = jnp.einsum('bhij,bhjd->bhid', attn, v)
        out = out.transpose(0, 2, 1, 3).reshape(b, -1, INNER)
        out = jnp.einsum('bnf,fd->bnd', out, Wout)
        mu = jnp.mean(out, axis=-1, keepdims=True)
        var = jnp.var(out, axis=-1, keepdims=True)
        out = (out - mu) * jax.lax.rsqrt(var + EPS) * ln_scale + ln_bias
        return out

    def _L2_ffn_ref(x, attention_mask, position_ids, router_w, router_b, wq, wk, wv, wo, w1, w2, ln1, ln2):
        import jax, jax.numpy as jnp
        import numpy as np
        B, S, D, H, F = (4, 512, 128, 16, 512)
        CAP = 0.125
        ROPE_BASE = 10000.0

        def rmsnorm(x, g):
            return x * jax.lax.rsqrt(jnp.mean(x * x, -1, keepdims=True) + 1e-06) * g

        def rope(t, pos):
            hd = t.shape[-1]
            inv = 1.0 / ROPE_BASE ** (jnp.arange(0, hd, 2, dtype=jnp.float32) / hd)
            f = pos[:, None, :, None].astype(jnp.float32) * inv
            emb = jnp.concatenate([f, f], axis=-1)
            cos, sin = (jnp.cos(emb), jnp.sin(emb))
            rot = jnp.concatenate([-t[..., hd // 2:], t[..., :hd // 2]], axis=-1)
            return t * cos + rot * sin
        b, s, d = x.shape
        hd = d // H
        weights = (x @ router_w)[..., 0] + router_b[0]
        k = int(CAP * s)
        topv, topi = jax.lax.top_k(weights, k)
        thr = topv[:, -1]
        sel_mask = (weights > thr[:, None]).astype(x.dtype)
        kc = k - 1
        sel_idx = jnp.sort(topi[:, :kc], axis=1)
        bidx = jnp.arange(b)[:, None]
        x_sel = x[bidx, sel_idx]
        pos_sel = position_ids[bidx, sel_idx]
        w_sel = weights[bidx, sel_idx]
        m = attention_mask[:, 0]
        m_sel = m[bidx[:, :, None], sel_idx[:, :, None], sel_idx[:, None, :]]
        hn = rmsnorm(x_sel, ln1)

        def heads(t):
            return t.reshape(b, kc, H, hd).transpose(0, 2, 1, 3)
        q = rope(heads(hn @ wq), pos_sel)
        kk = rope(heads(hn @ wk), pos_sel)
        v = heads(hn @ wv)
        sc = jnp.einsum('bhqd,bhkd->bhqk', q, kk) / np.sqrt(hd).astype(np.float32)
        sc = sc + m_sel[:, None]
        a = jax.nn.softmax(sc, axis=-1)
        o = jnp.einsum('bhqk,bhkd->bhqd', a, v).transpose(0, 2, 1, 3).reshape(b, kc, d) @ wo
        x1 = x_sel + o
        x2 = x1 + jax.nn.gelu(rmsnorm(x1, ln2) @ w1) @ w2
        proc = x2 * w_sel[..., None]
        out = jnp.zeros_like(x).at[bidx, sel_idx].set(proc)
        return out + x * (1.0 - sel_mask)[..., None]

    def _L3_xattn_ref(memory, query, b, seq_len):
        import jax, jax.numpy as jnp
        import numpy as np
        UNITS = 128
        NUM_HEADS = 16
        MASK_VALUE = -1000000000000.0

        def _split_heads(x, n):
            B, S, D = x.shape
            return x.reshape(B, S, n, D // n).transpose(0, 2, 1, 3)
        B, S, _ = query.shape
        dh = UNITS // NUM_HEADS
        k_mem, v_mem = jnp.split(memory, 2, axis=2)
        Q = _split_heads(query, NUM_HEADS) * dh ** (-0.5)
        Kh = _split_heads(k_mem, NUM_HEADS)
        Vh = _split_heads(v_mem, NUM_HEADS)
        logits = jnp.einsum('bhqd,bhkd->bhqk', Q, Kh) + b
        valid = (jnp.arange(S)[None, :] < seq_len[:, 0:1]).astype(jnp.float32)
        logits = logits + MASK_VALUE * (1.0 - valid)[:, None, None, :]
        weights = jax.nn.softmax(logits, axis=-1)
        out = jnp.einsum('bhqk,bhkd->bhqd', weights, Vh)
        return out.transpose(0, 2, 1, 3).reshape(B, S, UNITS)

    def _L3_ffn_ref(x, W_exp, b_exp, up_weights, up_bias, down_weights, W_con, b_con, down_bias):
        import jax, jax.numpy as jnp
        import numpy as np
        D_MODEL = 128
        EXPANSION = 4
        D_HIDDEN = D_MODEL * EXPANSION
        NUM_STAGES = int(np.log2(D_HIDDEN))

        def butterfly(y, weights, dim):
            lead = y.shape[:-1]
            for stage in range(weights.shape[0]):
                s = 2 ** stage
                nb = dim // (2 * s)
                yr = y.reshape(*lead, nb, 2, s)
                a = yr[..., 0, :]
                b = yr[..., 1, :]
                w = weights[stage].reshape(nb, s, 2, 2)
                na = w[..., 0, 0] * a + w[..., 0, 1] * b
                nb2 = w[..., 1, 0] * a + w[..., 1, 1] * b
                y = jnp.stack([na, nb2], axis=-2).reshape(*lead, dim)
            return y
        h = jnp.einsum('bsd,dh->bsh', x, W_exp) + b_exp
        h = butterfly(h, up_weights, D_HIDDEN)
        h = jax.nn.gelu(h + up_bias, approximate=False)
        h = butterfly(h, down_weights, D_HIDDEN)
        y = jnp.einsum('bsh,hd->bsd', h, W_con) + b_con
        return y + down_bias
    x = x + jnp.tanh(g_xattn[0]) * _L0_xattn_ref(ctx_2048, _layernorm(x, axis=-1), mask_BxS2_fk1, mask_BxS2_fk1, L0_xattn_W_src, L0_xattn_b_src, L0_xattn_W_tgt, L0_xattn_b_tgt, L0_xattn_W_out, L0_xattn_b_out)
    x = x + jnp.tanh(g_ffn[0]) * _L0_ffn_ref(_layernorm(x, axis=-1), L0_ffn_W_gate, L0_ffn_b_gate, L0_ffn_W1, L0_ffn_b1, L0_ffn_W2, L0_ffn_b2)
    x = x + jnp.tanh(g_xattn[1]) * _L1_xattn_ref(_layernorm(x, axis=-1), ctx_2048, mask_BxS2_if0, L1_xattn_W_in, L1_xattn_b_in, L1_xattn_g_res, L1_xattn_g_init)
    x = x + jnp.tanh(g_ffn[1]) * _L1_ffn_ref(_layernorm(x, axis=-1), L1_ffn_router_w, L1_ffn_wg_r, L1_ffn_wu_r, L1_ffn_wd_r, L1_ffn_wg_s, L1_ffn_wu_s, L1_ffn_wd_s)
    x = x + jnp.tanh(g_xattn[2]) * _L2_xattn_ref(_layernorm(x, axis=-1), ctx_2048, L2_xattn_Wq, L2_xattn_Wkv, L2_xattn_null_kv, L2_xattn_Wout, L2_xattn_ln_scale, L2_xattn_ln_bias)
    x = x + jnp.tanh(g_ffn[2]) * _L2_ffn_ref(_layernorm(x, axis=-1), L2_ffn_attention_mask, L2_ffn_position_ids, L2_ffn_router_w, L2_ffn_router_b, L2_ffn_wq, L2_ffn_wk, L2_ffn_wv, L2_ffn_wo, L2_ffn_w1, L2_ffn_w2, L2_ffn_ln1, L2_ffn_ln2)
    x = x + jnp.tanh(g_xattn[3]) * _L3_xattn_ref(ctx_2048, _layernorm(x, axis=-1), L3_xattn_b, itok_Bx1_68_817)
    x = x + jnp.tanh(g_ffn[3]) * _L3_ffn_ref(_layernorm(x, axis=-1), L3_ffn_W_exp, L3_ffn_b_exp, L3_ffn_up_weights, L3_ffn_up_bias, L3_ffn_down_weights, L3_ffn_W_con, L3_ffn_b_con, L3_ffn_down_bias)
    return x

_drawn_inputs = setup_inputs


def setup_inputs(seed=0):
    import zlib

    import numpy as np

    out = dict(_drawn_inputs(seed))
    spreads = {'L0_xattn_b_src': (0.0, 0.1),
     'L0_xattn_b_tgt': (0.0, 0.291),
     'L0_xattn_b_out': (0.0, 0.1),
     'L1_xattn_b_in': (0.0, 0.1),
     'L1_xattn_g_res': (1.0, 0.2),
     'L1_xattn_g_init': (1.0, 0.2),
     'L2_xattn_ln_scale': (1.0, 0.2),
     'L2_xattn_ln_bias': (0.0, 0.1),
     'L2_ffn_ln1': (1.0, 0.6),
     'L2_ffn_ln2': (1.0, 0.6),
     'L3_ffn_b_exp': (0.0, 0.1),
     'L3_ffn_up_bias': (0.0, 0.1),
     'L3_ffn_b_con': (0.0, 0.1),
     'L3_ffn_down_bias': (0.0, 0.1)}
    factors = {'g_ffn': 8.0,
     'L1_ffn_router_w': 7.641,
     'L1_ffn_wg_r': 4.788,
     'L1_ffn_wu_r': 7.636,
     'L1_ffn_wd_r': 6.107,
     'L1_ffn_wg_s': 4.346,
     'L1_ffn_wu_s': 4.347,
     'L1_ffn_wd_s': 4.212,
     'L2_xattn_null_kv': 3.552,
     'L2_ffn_wq': 8.0,
     'L2_ffn_wk': 8.0,
     'L2_ffn_wv': 8.0,
     'L2_ffn_wo': 8.0,
     'L2_ffn_w1': 8.0,
     'L2_ffn_w2': 8.0}
    for name, (base, spread) in spreads.items():
        noise = np.random.default_rng([zlib.crc32(name.encode()), seed]).standard_normal(out[name].shape)
        drawn = base * np.exp(spread * noise) if base else spread * noise
        out[name] = jnp.asarray(drawn.astype(out[name].dtype))
    for name, factor in factors.items():
        out[name] = (out[name] * factor).astype(out[name].dtype)
    return out
```

```python
from contextlib import ExitStack

import concourse.bass as bass
from concourse import mybir

F32 = mybir.dt.float32
BF16 = mybir.dt.bfloat16
I32 = mybir.dt.int32
ALU = mybir.AluOpType
ACT = mybir.ActivationFunctionType
AX = mybir.AxisListType

P = 128
NB = 32
D = 128
DC = 256
G4 = 4
TURNS4 = NB // G4
TURNS2 = NB // 2
EPS_LN = 1e-5
BIG = 1e30
BASE = 9
EXPERTS0 = 8
EXPERTS1 = 16
SEL = 16
KEEP = 15


def done(n):
    return n + BASE


def bc(ap, shape):
    return ap.broadcast_to(shape)


def setup_block(nc, K, A):
    with ExitStack() as c:
        def sb(name, shape, dt=F32):
            return c.enter_context(nc.sbuf_tensor(name, shape, dt))

        def sem(name):
            return c.enter_context(nc.semaphore(name))

        gates = sb("gates", [P, 8])
        mask32 = sb("mask32", [NB, P])
        len32i = sb("len32i", [NB, 1], I32)
        len32 = sb("len32", [NB, 1])
        iota32 = sb("iota32", [NB, P])
        kb32 = sb("kb32", [NB, P])
        sum32 = sb("sum32", [NB, P])
        rest32 = sb("rest32", [NB, P])
        x_loaded = [sem(f"x_loaded{i}") for i in range(4)]
        small_loaded = sem("small_loaded")
        chain = sem("setup_chain")

        with nc.Block() as block:
            @block.sync
            def _(sp):
                sp.dma_start(gates[:, 0:4], bc(A["g_xattn"].rearrange("(o g) -> o g", o=1), [P, 4])).then_inc(small_loaded, 16)
                sp.dma_start(gates[:, 4:8], bc(A["g_ffn"].rearrange("(o g) -> o g", o=1), [P, 4])).then_inc(small_loaded, 16)
                sp.dma_start(mask32[:, :], A["mask_BxS2_fk1"]).then_inc(small_loaded, 16)
                sp.dma_start(len32i[:, :], A["itok_Bx1_68_817"]).then_inc(small_loaded, 16)
                sp.dma_start(iota32[:, :], bc(A["c_iota"], [NB, P])).then_inc(small_loaded, 16)
                sp.dma_start(kb32[:, :], bc(A["L3_xattn_b"].rearrange("(o k) -> o k", o=1), [NB, P])).then_inc(small_loaded, 16)
                xv = A["x"].rearrange("b t f -> t b f")
                for i in range(4):
                    sp.dma_start(K.x[:, 8 * i:8 * i + 8, :], xv[:, 8 * i:8 * i + 8, :]).then_inc(x_loaded[i], 16)

            @block.scalar
            def _(act):
                K.load_weights(act)
                act.wait_ge(small_loaded, 96)
                nc.scalar.activation(K.tg[:, :], gates[:, :], ACT.Tanh).then_inc(K.gates_ready, 1)

            @block.vector
            def _(v):
                n = [0]

                def link(ins):
                    n[0] += 1
                    ins.then_inc(chain, 1)
                    v.wait_ge(chain, n[0])
                nc.vector.memset(K.ones_row[:, :], 1.0)
                nc.vector.memset(K.ones_bf[:, :], 1.0)
                nc.vector.memset(K.ones_f[:, :], 1.0)
                nc.vector.memset(K.neg_half[:, :], -0.5)
                v.wait_ge(small_loaded, 96)
                nc.vector.tensor_scalar(K.neg32[:, :], mask32[:, :], 0.0, -BIG, ALU.is_equal, ALU.mult)
                link(nc.vector.tensor_copy(len32[:, :], len32i[:, :]))
                link(nc.vector.tensor_scalar(rest32[:, :], iota32[:, :], len32[:, 0:1], -1e12, ALU.is_ge, ALU.mult))
                link(nc.vector.tensor_tensor(sum32[:, :], kb32[:, :], rest32[:, :], ALU.add))
                link(nc.vector.tensor_copy(K.part32[:, 0, :], sum32[:, :]))
                link(nc.vector.tensor_tensor(rest32[:, :], sum32[:, :], K.part32[:, 0, :], ALU.subtract))
                link(nc.vector.tensor_copy(K.part32[:, 1, :], rest32[:, :]))
                link(nc.vector.tensor_tensor(sum32[:, :], rest32[:, :], K.part32[:, 1, :], ALU.subtract))
                link(nc.vector.tensor_copy(K.part32[:, 2, :], sum32[:, :]))
                for i in range(4):
                    v.wait_ge(x_loaded[i], 16)
                    with v.Fori(8 * i, 8 * i + 8) as b:
                        nc.vector.bn_stats(K.st6[:, b, :], K.x[:, b, :])


def ln_statistics(nc, K, v, chain):
    even_mean, odd_mean = K.st6[:, :, 1], K.st6[:, :, 4]
    even_m2, odd_m2 = K.st6[:, :, 2], K.st6[:, :, 5]
    a, b2 = K.lna, K.lnb
    nc.vector.tensor_tensor(K.mean[:, :], even_mean, odd_mean, ALU.add).then_inc(chain, 1)
    nc.vector.tensor_tensor(a[:, :], even_mean, odd_mean, ALU.subtract).then_inc(chain, 1)
    nc.vector.tensor_tensor(b2[:, :], even_m2, odd_m2, ALU.add).then_inc(chain, 1)
    v.wait_ge(chain, 3)
    nc.vector.tensor_scalar(K.mean[:, :], K.mean[:, :], 0.5, None, ALU.mult).then_inc(chain, 1)
    nc.vector.tensor_tensor(a[:, :], a[:, :], a[:, :], ALU.mult).then_inc(chain, 1)
    nc.vector.tensor_scalar(b2[:, :], b2[:, :], 1.0 / D, EPS_LN, ALU.mult, ALU.add).then_inc(chain, 1)
    v.wait_ge(chain, 6)
    nc.vector.scalar_tensor_tensor(out=K.var[:, :], in0=a[:, :], scalar=0.25, in1=b2[:, :],
                                   op0=ALU.mult, op1=ALU.add).then_inc(chain, 1)
    v.wait_ge(chain, 7)


class Attention:

    def __init__(self, nc, c, tag, groups, seqs, first, extra, psum_steps, shared=()):
        self.groups, self.seqs, self.tag = groups, seqs, tag
        self.units = seqs * groups
        self.turns = NB // seqs
        self.sched, self.copies_first = [], []
        for i in range(first, first + self.units):
            steps, others = [], []
            for kind, j in (("T", i), ("S", i + 2), ("V", i - 1)):
                unit = j % self.units
                steps.append((j // self.units, (kind, unit // groups, unit % groups)))
            for kind, at in extra:
                for k in range(seqs):
                    slot = groups * k + at
                    assert first - self.units <= slot < first + self.units
                    if slot in (i, i - self.units):
                        others.append((int(slot != i), (kind, k)))
            self.sched += steps + others
            self.copies_first += [steps[0], steps[2]] + others + [steps[1]]

        def sem(name):
            return c.enter_context(nc.semaphore(f"{tag}_{name}"))
        self.scores_ready = sem("scores_ready")
        self.max_ready = sem("max_ready")
        self.shifted = sem("shifted")
        self.exp_ready = sem("exp_ready")
        self.turned = sem("turned")
        self.turned_copied = sem("turned_copied")
        self.summed = sem("summed")
        self.recip_ready = sem("recip_ready")
        self.null_ready = sem("null_ready")
        self.normed = sem("normed")
        self.ln_chain = sem("ln_chain")
        self.rstd_ready = sem("rstd_ready")
        self.centred_ready = sem("centred_ready")
        self.xn_ready = sem("xn_ready")
        self.wait_carried = sem("wait_carried")
        self.x_done = sem("x_done")
        self.j_steps = [(ahead, s) for ahead, s in self.sched if s[0] in psum_steps]
        assert len(self.j_steps) % 2 == 0
        self.j_ready = {s: sem(f"ready_{s}") for s in psum_steps}
        self.copied = {s: sem(f"copied_{s}") for s in psum_steps}
        self.shared = shared

    def run(self, engine, step_of, copies_first=False):
        sched = self.copies_first if copies_first else self.sched
        for ahead, step in sched:
            if ahead:
                step_of(0, step)
        with engine.Fori(0, self.turns - 1) as it:
            for ahead, step in sched:
                step_of(it + ahead, step)
        for ahead, step in sched:
            if not ahead:
                step_of(self.turns - 1, step)

    def unit(self, it, k, g):
        return self.units * it + self.groups * k + g

    def j_index(self, kind, k):
        return [s for _, s in self.j_steps].index((kind, k))

    def j_bank(self, kind, k):
        return self.j_index(kind, k) % 2

    def wait_bank(self, pe, it, kind, k):
        n = len(self.j_steps)
        i = self.j_index(kind, k)
        own_ahead = self.j_steps[i][0]
        peeled = isinstance(it, int)
        for back in range(i - 2, i - n - 2, -2):
            ahead0, (kind0, k0) = self.j_steps[back % n]
            turn = it + (ahead0 - own_ahead - (1 if back < 0 else 0))
            if peeled and not 0 <= turn < self.turns:
                continue
            pe.wait_ge(self.copied[kind0], self.copied_at(kind0, self.seqs * turn + k0 + 1))
            if peeled or back >= 0 or ahead0:
                break

    def copied_at(self, kind, n):
        return done((2 if kind in self.shared else 1) * n)


def start_counts(engine, sems):
    for s in sems:
        engine.sem_inc(s, BASE)


class Buffers:
    pass


def attn_buffers(nc, c, tag):
    def sb(name, shape, dt=F32):
        return c.enter_context(nc.sbuf_tensor(f"{tag}_{name}", shape, dt))
    B = Buffers()
    B.shift = sb("shift", [P, 2, 4, P])
    B.exp = sb("exp", [P, 2, 4, P])
    B.expT = sb("expT", [P, 2, 4, P])
    B.max = sb("max", [P, 2, 4])
    B.rec = sb("rec", [P, 2, 4])
    B.null = sb("null", [P, 4, 4])
    return B


def pe_turn(nc, K, pe, a, B, it, k, g):
    u = a.unit(it, k, g)
    s = (a.groups * k + g) % 2
    pe.wait_ge(a.exp_ready, done(u + 1))
    pe.wait_ge(a.turned_copied, done(u - 1))
    for h in range(4):
        m = nc.tensor.transpose(K.T[:, s, h * P:(h + 1) * P], B.exp[:, s, h, :], K.w["ident"][:, :])
    m.then_inc(a.turned, 1)


def pe_values(nc, K, pe, a, B, it, k, g, values, width):
    u = a.unit(it, k, g)
    s = (a.groups * k + g) % 2
    pe.wait_ge(a.turned_copied, done(u + 1))
    pe.wait_ge(a.normed, done(u - 1))
    for h in range(4):
        m = nc.tensor.matmul(K.O[:, s, h * width:(h + 1) * width], B.expT[:, s, h, :], values(h),
                             start=True, stop=True)
    m.then_inc(a.summed, 1)


def dve_shift(nc, K, v, a, B, it, k, g, clamp=False):
    u = a.unit(it, k, g)
    s = (a.groups * k + g) % 2
    scores = K.S[:, s, :].rearrange("p (h k) -> p h k", h=4)
    per = 2 if clamp else 1
    v.wait_ge(a.scores_ready, done(u + 1))
    if clamp:
        v.wait_ge(a.exp_ready, done(u - 1))
    nc.vector.tensor_reduce(B.max[:, s, :], scores, AX.X, ALU.max).then_inc(a.max_ready, 1)
    v.wait_ge(a.max_ready, done(per * u + 1))
    if clamp:
        nc.vector.tensor_scalar(B.max[:, s, :], B.max[:, s, :], 0.0, None, ALU.max).then_inc(a.max_ready, 1)
        v.wait_ge(a.max_ready, done(per * u + 2))
    v.wait_ge(a.exp_ready, done(u - 1))
    nc.vector.tensor_tensor(B.shift[:, s, :, :], scores, bc(B.max[:, s, :].unsqueeze(2), [P, 4, P]),
                            ALU.subtract).then_inc(a.shifted, 1)


def act_exp(nc, K, act, a, B, it, k, g, scale, null=False):
    u = a.unit(it, k, g)
    s = (a.groups * k + g) % 2
    act.wait_ge(a.shifted, done(u + 1))
    if null:
        act.wait_ge(a.normed, done(u - 3))
        nc.scalar.activation(B.null[:, g, :], B.max[:, s, :], ACT.Exp, scale=-scale).then_inc(a.null_ready, 1)
    act.wait_ge(a.turned, done(u - 1))
    nc.scalar.activation(B.exp[:, s, :, :], B.shift[:, s, :, :], ACT.Exp, scale=scale).then_inc(a.exp_ready, 1)


def act_copy_turned(nc, K, act, a, B, it, k, g):
    u = a.unit(it, k, g)
    s = (a.groups * k + g) % 2
    act.wait_ge(a.turned, done(u + 1))
    act.wait_ge(a.summed, done(u - 1))
    nc.scalar.copy(B.expT[:, s, :, :], K.T[:, s, :].rearrange("p (h k) -> p h k", h=4)).then_inc(a.turned_copied, 1)


def dve_norm(nc, K, v, a, B, it, k, g, out, width, null=False):
    u = a.unit(it, k, g)
    s = (a.groups * k + g) % 2
    o = K.O[:, s, 0:4 * width].rearrange("p (h w) -> p h w", h=4)
    v.wait_ge(a.summed, done(u + 1))
    if null:
        v.wait_ge(a.null_ready, done(u + 1))
        nc.vector.tensor_tensor(B.rec[:, s, :].unsqueeze(2), o[:, :, width - 1:width], B.null[:, g, :].unsqueeze(2), ALU.add)\
            .then_inc(a.recip_ready, 1)
        v.wait_ge(a.recip_ready, done(2 * u + 1))
        nc.vector.reciprocal(B.rec[:, s, :], B.rec[:, s, :]).then_inc(a.recip_ready, 1)
        v.wait_ge(a.recip_ready, done(2 * u + 2))
    else:
        nc.vector.reciprocal(B.rec[:, s, :].unsqueeze(2), o[:, :, width - 1:width]).then_inc(a.recip_ready, 1)
        v.wait_ge(a.recip_ready, done(u + 1))
    nc.vector.tensor_tensor(out, o[:, :, 0:width - 1], bc(B.rec[:, s, :].unsqueeze(2), [P, 4, width - 1]),
                            ALU.mult).then_inc(a.normed, 1)


def pool_rstd(nc, K, pool, ln_chain, rstd_ready):
    pool.wait_ge(ln_chain, 7)
    nc.gpsimd.tensor_tensor(K.rstd[:, :], K.var[:, :], K.neg_half[:, :], ALU.pow).then_inc(rstd_ready, 1)


def pool_normalise(nc, K, pool, a, xn, b, k):
    k = k % 2
    own = bass.ds(b, 1)
    pool.wait_ge(a.copied["x"], done(b - 1))
    pool.sem_inc(a.wait_carried, 1)
    nc.gpsimd.tensor_tensor(xn[:, k, :], K.x[:, b, :], bc(K.mean[:, own], [P, D]), ALU.subtract).then_inc(a.centred_ready, 1)
    pool.wait_ge(a.centred_ready, done(b + 1))
    pool.sem_inc(a.wait_carried, 1)
    nc.gpsimd.tensor_tensor(xn[:, k, :], xn[:, k, :], bc(K.rstd[:, own], [P, D]), ALU.mult).then_inc(a.xn_ready, 1)




def layer0_attention(nc, K, A):
    H, HD = 8, 16
    W = HD + 1
    with ExitStack() as c:
        def sb(name, shape, dt=F32):
            return c.enter_context(nc.sbuf_tensor(f"l0_{name}", shape, dt))

        def sem(name):
            return c.enter_context(nc.semaphore(f"l0_{name}"))

        extra = (("u", 3), ("v", -1), ("k", -5), ("q", -3), ("o", 4), ("x", -4))
        a = Attention(nc, c, "l0", 2, 4, 3, extra, ("k", "v", "x", "q", "u", "o"))
        B = attn_buffers(nc, c, "l0")
        ctxT = sb("ctxT", [P, 4, 2, P])
        mask_bc = sb("mask_bc", [P, NB, P])
        mask_col = sb("mask_col", [P, NB])
        xn = sb("xn", [P, 2, D])
        xnT = sb("xnT", [P, 4, P])
        qT = sb("qT", [P, 2, P])
        kT = sb("kT", [P, 2, P])
        kz = sb("kz", [P, 2, H, P])
        vx = sb("vx", [P, 2, H, W])
        upd = sb("upd", [P, 2, D])
        updT = sb("updT", [P, 2, D])
        ctx_loaded = [sem(f"ctx_loaded{k}") for k in range(4)]
        neg_row = sb("neg_row", [1, NB * P], BF16)
        mask_loaded = sem("mask_loaded")
        neg_moved = sem("neg_moved")
        keys_ready = sem("keys_ready")
        ones_set = sem("ones_set")

        with nc.Block() as block:
            @block.sync
            def _(sp):
                mv = A["mask_BxS2_fk1"].rearrange("(o b) k -> o b k", o=1)
                sp.dma_start(mask_bc[:, :, :], bc(mv, [P, NB, P])).then_inc(mask_loaded, 16)
                sp.dma_start(mask_col[:, :], A["maskT"]).then_inc(mask_loaded, 16)
                sp.dma_start(neg_row[0:1, :].rearrange("o (b k) -> o b k", b=NB), K.neg32[:, :]).then_inc(neg_moved, 16)
                with sp.Fori(0, TURNS4) as it:
                    for k in range(4):
                        sp.wait_ge(a.copied["v"], done(4 * it + k - 3))
                        sp.dma_start(ctxT[:, k, :, :], A["ctxT"].rearrange("b (c p) t -> p b c t", p=P)[:, 4 * it + k, :, :])\
                            .then_inc(ctx_loaded[k], 16)

            @block.tensor
            def _(pe):
                start_counts(pe, [a.scores_ready, a.turned, a.summed, *a.j_ready.values()])
                pe.wait_ge(K.w_loaded[0], K.w_count[0])
                pe.wait_ge(neg_moved, 16)

                def step_of(it, step):
                    kind, k = step[0], step[1]
                    b = 4 * it + k
                    if kind in a.copied:
                        a.wait_bank(pe, it, kind, k)
                        J = K.J[:, a.j_bank(kind, k), 0:P]
                    if kind == "k":
                        pe.wait_ge(ctx_loaded[k], 16 * it + 16)
                        for j in range(2):
                            m = nc.tensor.matmul(J, K.w["w_src"][:, j, 0:D], ctxT[:, k, j, :], start=(j == 0), stop=(j == 1))
                    elif kind == "v":
                        for j in range(2):
                            nc.tensor.matmul(J, ctxT[:, k, j, :], K.w["w_src"][:, j, D:2 * D], start=(j == 0), stop=False)
                        m = nc.tensor.matmul(J, K.ones_row[0:1, :], K.w["b_srcv"][0:1, :], start=False, stop=True)
                    elif kind == "x":
                        pe.wait_ge(a.xn_ready, done(b + 1))
                        m = nc.tensor.transpose(J, xn[:, k % 2, :], K.w["ident"][:, :])
                    elif kind == "q":
                        pe.wait_ge(a.copied["x"], done(4 * it + k + 1))
                        m = nc.tensor.matmul(J, K.w["w_tgt"][:, :], xnT[:, k, :], start=True, stop=True)
                    elif kind == "u":
                        pe.wait_ge(a.normed, done(a.unit(it, k, 1) + 1))
                        m = nc.tensor.transpose(J, upd[:, k % 2, :], K.w["ident"][:, :])
                    elif kind == "o":
                        pe.wait_ge(a.copied["u"], done(4 * it + k + 1))
                        nc.tensor.matmul(J, xnT[:, k, :], K.w["w_out0"][:, 0, :], start=True, stop=False)
                        nc.tensor.matmul(J, K.ones_row[0:1, :], K.w["b_out0"][0:1, :], start=False, stop=False)
                        m = nc.tensor.matmul(J, updT[:, k % 2, :], K.w["w_out0"][:, 1, :], start=False, stop=True)
                    elif kind == "S":
                        g = step[2]
                        u = a.unit(it, k, g)
                        s = (2 * k + g) % 2
                        if g == 0:
                            pe.wait_ge(a.copied["q"], done(4 * it + k + 1))
                            pe.wait_ge(keys_ready, done(4 * it + k + 1))
                        pe.wait_ge(a.shifted, done(u - 1))
                        neg = bc(neg_row[0:1, bass.ds((4 * it + k) * P, P)].unsqueeze(1), [1, 4, P])
                        nc.tensor.matmul(K.S[:, s, :], qT[:, k % 2, :], kz[:, k % 2, 4 * g:4 * g + 4, :],
                                         start=True, stop=False)
                        nc.tensor.matmul(K.S[:, s, :], K.ones_bf[0:1, :], neg, start=False, stop=True)\
                            .then_inc(a.scores_ready, 1)
                    elif kind == "T":
                        pe_turn(nc, K, pe, a, B, it, k, step[2])
                    elif kind == "V":
                        g = step[2]
                        if g == 0:
                            pe.wait_ge(a.copied["v"], done(4 * it + k + 1))
                        pe_values(nc, K, pe, a, B, it, k, g, lambda h: vx[:, k % 2, 4 * g + h, :], W)
                    if kind in a.copied:
                        m.then_inc(a.j_ready[kind], 1)
                a.run(pe, step_of)

            @block.vector
            def _(v):
                start_counts(v, [a.max_ready, a.shifted, a.recip_ready, a.normed, a.x_done,
                                 a.copied["k"], a.copied["q"], a.copied["o"]])
                nc.vector.memset(vx[:, :, :, HD:W], 1.0).then_inc(ones_set, 1)
                ln_statistics(nc, K, v, a.ln_chain)
                v.wait_ge(K.w_loaded[0], K.w_count[0])
                v.wait_ge(mask_loaded, 32)
                v.wait_ge(K.gates_ready, 1)

                def step_of(it, step):
                    kind, k = step[0], step[1]
                    b = 4 * it + k
                    if kind in ("k", "q"):
                        v.wait_ge(a.j_ready[kind], done(b + 1))
                        if kind == "k":
                            v.wait_ge(keys_ready, done(b - 1))
                        else:
                            v.wait_ge(a.scores_ready, done(a.unit(it, k, 1) + 1 - 4))
                        dst, bias = (kT, K.w["b_srck"]) if kind == "k" else (qT, K.w["b_tgt"])
                        nc.vector.scalar_tensor_tensor(
                            out=dst[:, k % 2, :], in0=K.J[:, a.j_bank(kind, k), 0:P], scalar=bias[:, 0:1],
                            in1=mask_bc[:, b, :], op0=ALU.add, op1=ALU.mult).then_inc(a.copied[kind], 1)
                    elif kind == "S":
                        dve_shift(nc, K, v, a, B, it, k, step[2])
                    elif kind == "V":
                        g = step[2]
                        if g == 0:
                            v.wait_ge(a.copied["u"], done(b - 1))
                        dve_norm(nc, K, v, a, B, it, k, g,
                                 upd[:, k % 2, 64 * g:64 * g + 64].rearrange("p (h d) -> p h d", h=4), W)
                    elif kind == "o":
                        v.wait_ge(a.j_ready[kind], done(b + 1))
                        nc.vector.scalar_tensor_tensor(
                            out=K.x[:, b, :], in0=K.J[:, a.j_bank(kind, k), 0:P], scalar=K.tg[:, 0:1],
                            in1=K.x[:, b, :], op0=ALU.mult, op1=ALU.add).then_inc(a.copied["o"], 1)
                        v.wait_ge(a.copied["o"], done(b + 1))
                        nc.vector.bn_stats(K.st6[:, b, :], K.x[:, b, :])
                a.run(v, step_of)

            @block.scalar
            def _(act):
                start_counts(act, [a.exp_ready, a.turned_copied, a.copied["x"], a.copied["v"], a.copied["u"]])
                act.wait_ge(mask_loaded, 32)
                act.wait_ge(ones_set, 1)

                def step_of(it, step):
                    kind, k = step[0], step[1]
                    b = 4 * it + k
                    if kind in ("x", "u"):
                        act.wait_ge(a.j_ready[kind], done(b + 1))
                        act.wait_ge(a.copied["o"], done(b - 3 if kind == "x" else b - 1))
                        nc.scalar.copy(xnT[:, k, :] if kind == "x" else updT[:, k % 2, :], K.J[:, a.j_bank(kind, k), 0:P])\
                            .then_inc(a.copied[kind], 1)
                    elif kind == "v":
                        act.wait_ge(a.j_ready[kind], done(b + 1))
                        act.wait_ge(a.summed, done(a.unit(it, k, 1) + 1 - 4))
                        nc.scalar.mul(vx[:, k % 2, :, 0:HD], K.J[:, a.j_bank(kind, k), 0:P].rearrange("p (h d) -> p h d", h=H),
                                      mask_col[:, bass.ds(b, 1)]).then_inc(a.copied["v"], 1)
                    elif kind == "S":
                        act_exp(nc, K, act, a, B, it, k, step[2], float(HD) ** -0.5)
                    elif kind == "T":
                        act_copy_turned(nc, K, act, a, B, it, k, step[2])
                a.run(act, step_of, copies_first=True)

            @block.gpsimd
            def _(pool):
                start_counts(pool, [keys_ready, a.centred_ready, a.xn_ready])
                pool_rstd(nc, K, pool, a.ln_chain, a.rstd_ready)
                pool.wait_ge(a.rstd_ready, 1)
                pool.wait_ge(K.w_loaded[0], K.w_count[0])
                pool_normalise(nc, K, pool, a, xn, 0, 0)

                def keys_and_rows(it, k):
                    b = 4 * it + k
                    pool.wait_ge(a.copied["k"], done(b + 1))
                    pool.wait_ge(a.scores_ready, done(2 * b - 2))
                    nc.gpsimd.tensor_tensor(kz[:, k % 2, :, :], bc(kT[:, k % 2, :].unsqueeze(1), [P, H, P]),
                                            bc(K.w["head16"][:, :].unsqueeze(2), [P, H, P]), ALU.mult).then_inc(keys_ready, 1)
                    if not (isinstance(b, int) and b == NB - 1):
                        pool_normalise(nc, K, pool, a, xn, b + 1, k + 1)
                with pool.Fori(0, a.turns - 1) as it:
                    for k in range(4):
                        keys_and_rows(it, k)
                for k in range(4):
                    keys_and_rows(a.turns - 1, k)


def normalise4(nc, K, v, it, xn, rstd_ready, xn_ready, used):
    v.wait_ge(rstd_ready, done(it + 1))
    v.wait_ge(used, done(it))
    for j in range(G4):
        b = 4 * it + j
        n = nc.vector.tensor_scalar(xn[:, j, :], K.x[:, b, :], K.mean[:, bass.ds(b, 1)], K.rstd[:, bass.ds(b, 1)],
                                    ALU.subtract, ALU.mult)
    n.then_inc(xn_ready, 1)


def pool_rstd4(nc, K, it, rstd_ready):
    nc.gpsimd.tensor_tensor(K.rstd[:, bass.ds(4 * it, 4)], K.var[:, bass.ds(4 * it, 4)], K.neg_half[:, 0:4],
                            ALU.pow).then_inc(rstd_ready, 1)


def layer0_ffn(nc, K, A):
    E = EXPERTS0
    with ExitStack() as c:
        def sb(name, shape, dt=F32):
            return c.enter_context(nc.sbuf_tensor(f"f0_{name}", shape, dt))

        def sem(name):
            return c.enter_context(nc.semaphore(f"f0_{name}"))

        xn = sb("xn", [P, G4, D])
        xnT = sb("xnT", [P, G4 * P])
        score = sb("score", [P, G4, E])
        above = sb("above", [P, G4, E, E])
        equal = sb("equal", [P, G4, E, E])
        rank = sb("rank", [P, G4, E])
        weight = sb("weight", [P, G4, E])
        weightT = sb("weightT", [E, G4, P])
        hidden = sb("hidden", [P, 2, G4 * P])
        acc = sb("acc", [P, G4, D])
        fold_rows = sb("fold_rows", [P, 3, 512])
        up_w = sb("up_w", [P, 9, 2, 2, 256])
        ln_chain = sem("ln_chain")
        rstd_ready = sem("rstd_ready")
        xn_ready = sem("xn_ready")
        xn_used = sem("xn_used")
        xnT_ready = sem("xnT_ready")
        gate_ready = sem("gate_ready")
        dve_step = sem("dve_step")
        weight_ready = sem("weight_ready")
        weight_turned = sem("weight_turned")
        weightT_ready = sem("weightT_ready")
        bias_ready = sem("bias_ready")
        acc_started = sem("acc_started")
        h_ready = sem("h_ready")
        relu_ready = sem("relu_ready")
        y_ready = sem("y_ready")
        y_added = sem("y_added")
        up_loaded = sem("up_loaded")
        fold = sem("fold")

        with nc.Block() as block:
            @block.sync
            def _(sp):
                sp.dma_start(up_w[:, :, :, :, :], bc(A["up_w"], [P, 9, 2, 2, 256])).then_inc(up_loaded, 16)
                sp.wait_ge(up_loaded, 16)

            @block.gpsimd
            def _(pool):
                start_counts(pool, [rstd_ready])
                pool.wait_ge(ln_chain, 7)
                for t in range(TURNS4):
                    pool_rstd4(nc, K, t, rstd_ready)
                pool.wait_ge(up_loaded, 16)
                pool.wait_ge(K.w_loaded[7], K.w_count[7])
                butterfly(nc, pool, K.w["up_rows"], fold_rows, up_w, fold, False)

            @block.tensor
            def _(pe):
                start_counts(pe, [xn_used, gate_ready, weight_turned, bias_ready, h_ready, y_ready])
                pe.wait_ge(K.w_loaded[1], K.w_count[1])
                with pe.Fori(0, TURNS4) as it:
                    pe.wait_ge(xn_ready, done(it + 1))
                    pe.wait_ge(xnT_ready, done(it))
                    for j in range(G4):
                        m = nc.tensor.transpose(K.T[:, 0, j * P:(j + 1) * P], xn[:, j, :], K.w["ident"][:, :])
                    m.then_inc(xn_used, 1)
                    pe.wait_ge(xnT_ready, done(it + 1))
                    pe.wait_ge(weight_ready, done(it))
                    for j in range(G4):
                        J = K.J[:, 0, j * E:(j + 1) * E]
                        nc.tensor.matmul(J, xnT[:, j * P:(j + 1) * P], K.w["w_gate"][:, :], start=True, stop=False)
                        m = nc.tensor.matmul(J, K.ones_row[0:1, :], K.w["b_gate"][0:1, :], start=False, stop=True)
                    m.then_inc(gate_ready, 1)

                    def first(e):
                        pe.wait_ge(relu_ready, done(E * it + e - 1))
                        nc.tensor.matmul(K.S[:, e % 2, :], K.w["w1_0"][:, e, :], xnT[:, :], start=True, stop=True)\
                            .then_inc(h_ready, 1)
                    first(0)
                    first(1)
                    pe.wait_ge(weight_ready, done(it + 1))
                    pe.wait_ge(weightT_ready, done(it))
                    for j in range(G4):
                        m = nc.tensor.transpose(K.J[0:E, 1, j * P:(j + 1) * P], weight[:, j, :], K.w["ident"][:, :])
                    m.then_inc(weight_turned, 1)
                    pe.wait_ge(weightT_ready, done(it + 1))
                    pe.wait_ge(acc_started, done(it))
                    for j in range(G4):
                        m = nc.tensor.matmul(K.T[:, 1, j * P:(j + 1) * P], weightT[0:E, j, :], K.w["b2_0"][0:E, :],
                                             start=True, stop=True)
                    m.then_inc(bias_ready, 1)
                    for e in range(E):
                        pe.wait_ge(relu_ready, done(E * it + e + 1))
                        pe.wait_ge(y_added, done(G4 * (E * it + e - 1)))
                        for j in range(G4):
                            m = nc.tensor.matmul(K.O[:, e % 2, j * P:(j + 1) * P], hidden[:, e % 2, j * P:(j + 1) * P],
                                                 K.w["w2_0"][:, e, :], start=True, stop=True)
                        m.then_inc(y_ready, 1)
                        if e + 2 < E:
                            first(e + 2)

            @block.scalar
            def _(act):
                start_counts(act, [xnT_ready, weightT_ready, relu_ready])
                with act.Fori(0, TURNS4) as it:
                    act.wait_ge(xn_used, done(it + 1))
                    act.wait_ge(h_ready, done(E * it))
                    nc.scalar.copy(xnT[:, :], K.T[:, 0, :]).then_inc(xnT_ready, 1)

                    def relu(e):
                        act.wait_ge(h_ready, done(E * it + e + 1))
                        act.wait_ge(y_ready, done(E * it + e - 1))
                        nc.scalar.activation(hidden[:, e % 2, :], K.S[:, e % 2, :], ACT.Relu, bias=K.w["b1_0"][:, e:e + 1])\
                            .then_inc(relu_ready, 1)
                    relu(0)
                    relu(1)
                    act.wait_ge(weight_turned, done(it + 1))
                    act.wait_ge(bias_ready, done(it))
                    nc.scalar.copy(weightT[:, :, :], K.J[0:E, 1, :].rearrange("p (j t) -> p j t", j=G4))\
                        .then_inc(weightT_ready, 1)
                    for e in range(2, E):
                        relu(e)

            @block.vector
            def _(v):
                ln_statistics(nc, K, v, ln_chain)
                start_counts(v, [xn_ready, dve_step, weight_ready, acc_started, y_added])
                with v.Fori(0, TURNS4) as it:
                    normalise4(nc, K, v, it, xn, rstd_ready, xn_ready, xn_used)
                    STEPS = 6
                    v.wait_ge(gate_ready, done(it + 1))
                    nc.vector.tensor_copy(score[:, :, :], K.J[:, 0, 0:G4 * E].rearrange("p (j e) -> p j e", j=G4))\
                        .then_inc(dve_step, 1)
                    v.wait_ge(dve_step, done(STEPS * it + 1))
                    for j in range(G4):
                        other = bc(score[:, j, :].unsqueeze(1), [P, E, E])
                        own = bc(score[:, j, :].unsqueeze(2), [P, E, E])
                        nc.vector.tensor_tensor(above[:, j, :, :], other, own, ALU.is_gt)
                        m = nc.vector.tensor_tensor(equal[:, j, :, :], other, own, ALU.is_equal)
                    m.then_inc(dve_step, 1)
                    v.wait_ge(dve_step, done(STEPS * it + 2))
                    nc.vector.tensor_tensor(equal[:, :, :, :], equal[:, :, :, :],
                                            bc(K.w["before8"][:, :, :].unsqueeze(1), [P, G4, E, E]), ALU.mult).then_inc(dve_step, 1)
                    v.wait_ge(dve_step, done(STEPS * it + 3))
                    nc.vector.tensor_tensor(above[:, :, :, :], above[:, :, :, :], equal[:, :, :, :], ALU.add).then_inc(dve_step, 1)
                    v.wait_ge(dve_step, done(STEPS * it + 4))
                    nc.vector.tensor_reduce(rank[:, :, :], above[:, :, :, :], AX.X, ALU.add).then_inc(dve_step, 1)
                    v.wait_ge(dve_step, done(STEPS * it + 5))
                    nc.vector.scalar_tensor_tensor(out=rank[:, :, :], in0=rank[:, :, :], scalar=2.0, in1=score[:, :, :],
                                                   op0=ALU.is_lt, op1=ALU.mult).then_inc(dve_step, 1)
                    v.wait_ge(dve_step, done(STEPS * it + 6))
                    v.wait_ge(y_added, done(G4 * E * it))
                    nc.vector.tensor_scalar(weight[:, :, :], rank[:, :, :], K.tg[:, 4:5], None, ALU.mult).then_inc(weight_ready, 1)
                    v.wait_ge(bias_ready, done(it + 1))
                    nc.vector.tensor_tensor(acc[:, :, :], K.T[:, 1, :].rearrange("p (j d) -> p j d", j=G4),
                                            K.x[:, bass.ds(G4 * it, G4), :], ALU.add).then_inc(acc_started, 1)
                    v.wait_ge(acc_started, done(it + 1))
                    v.wait_ge(weight_ready, done(it + 1))
                    for e in range(E):
                        v.wait_ge(y_ready, done(E * it + e + 1))
                        for j in range(G4):
                            if e > 0:
                                v.wait_ge(y_added, done(G4 * (E * it + e - 1) + j + 1))
                            to = K.x[:, G4 * it + j, :] if e == E - 1 else acc[:, j, :]
                            nc.vector.scalar_tensor_tensor(out=to, in0=K.O[:, e % 2, j * P:(j + 1) * P],
                                                           scalar=weight[:, j, e:e + 1], in1=acc[:, j, :],
                                                           op0=ALU.mult, op1=ALU.add).then_inc(y_added, 1)
                    for j in range(G4):
                        v.wait_ge(y_added, done(G4 * (E * it + E - 1) + j + 1))
                        nc.vector.bn_stats(K.st6[:, G4 * it + j, :], K.x[:, G4 * it + j, :])


def butterfly(nc, pool, rows, spare, w, fold, transposed):
    R = rows.shape[1]
    n = 0
    for r in range(R):
        src, dst = rows[:, r, :], spare[:, r, :]
        for stage in (reversed(range(9)) if transposed else range(9)):
            s = 2 ** stage
            x = src.rearrange("p (n two s) -> p two n s", two=2, s=s)
            y = dst.rearrange("p (n two s) -> p two n s", two=2, s=s)
            part = spare[:, R, 0:256].rearrange("p (n s) -> p n s", s=s)
            for o in range(2):
                pick = lambda i: (w[:, stage, i, o, :] if transposed else w[:, stage, o, i, :]).rearrange("p (n s) -> p n s", s=s)
                if n:
                    pool.wait_ge(fold, n)
                nc.gpsimd.tensor_tensor(part, x[:, 1, :, :], pick(1), ALU.mult).then_inc(fold, 1)
                nc.gpsimd.tensor_tensor(y[:, o, :, :], x[:, 0, :, :], pick(0), ALU.mult).then_inc(fold, 1)
                n += 2
                pool.wait_ge(fold, n)
                nc.gpsimd.tensor_tensor(y[:, o, :, :], y[:, o, :, :], part, ALU.add).then_inc(fold, 1)
                n += 1
            src, dst = dst, src
        pool.wait_ge(fold, n)
        nc.gpsimd.tensor_copy(rows[:, r, :], spare[:, r, :]).then_inc(fold, 1)
        n += 1
    pool.wait_ge(fold, n)


def layer1_attention(nc, K, A):
    import math
    import numpy as np
    dt = float(-np.log(-np.expm1(np.float32(-1e-3))))
    keep = math.exp(-1e-3)
    with ExitStack() as c:
        def sb(name, shape, dt=F32):
            return c.enter_context(nc.sbuf_tensor(f"l1_{name}", shape, dt))

        def sem(name):
            return c.enter_context(nc.semaphore(f"l1_{name}"))

        lens_i = sb("lens_i", [P, NB], I32)
        lens = sb("lens", [P, NB])
        ends = sb("ends", [P, NB])
        wrap = sb("wrap", [P, NB])
        plug = sb("plug", [P, NB])
        hot = sb("hot", [P, NB, P], BF16)
        st6c = sb("st6c", [P, NB, 6])
        m1 = sb("m1", [P, NB])
        m2 = sb("m2", [P, NB])
        rctx = sb("rctx", [P, NB])
        row_scale = sb("row_scale", [P, NB])
        w_in = sb("w_in", [P, P])
        hn = sb("hn", [P, G4, D])
        hT = sb("hT", [P, G4 * P])
        lag = sb("lag", [P, G4 * P])
        decay = sb("decay", [P, G4 * P])
        pick = sb("pick", [P, G4, P])
        u = sb("u", [P, G4, D])
        lens_loaded = sem("lens_loaded")
        ln_chain = sem("ln_chain")
        pre = sem("pre")
        pre_pe = sem("pre_pe")
        ctx_stats = sem("ctx_stats")
        powers = sem("powers")
        plug_ready = sem("plug_ready")
        lag_ready = sem("lag_ready")
        decay_ready = sem("decay_ready")
        pick_ready = sem("pick_ready")
        hn_ready = sem("hn_ready")
        turned = sem("turned")
        hT_ready = sem("hT_ready")
        sum_ready = sem("sum_ready")
        x_done = sem("x_done")

        with nc.Block() as block:
            @block.sync
            def _(sp):
                sp.dma_start(lens_i[:, :], A["lensT"]).then_inc(lens_loaded, 16)
                sp.wait_ge(lens_loaded, 16)

            @block.vector
            def _(v):
                n = [0]

                def link(ins):
                    n[0] += 1
                    ins.then_inc(pre, 1)
                    v.wait_ge(pre, n[0])
                ln_statistics(nc, K, v, ln_chain)
                v.wait_ge(K.w_loaded[2], K.w_count[2])
                v.wait_ge(lens_loaded, 16)
                link(nc.vector.tensor_copy(lens[:, :], lens_i[:, :]))
                link(nc.vector.reciprocal(K.lna[:, :], K.var[:, :]))
                link(nc.vector.scalar_tensor_tensor(out=K.lnb[:, :], in0=K.var[:, :], scalar=-EPS_LN, in1=K.lna[:, :],
                                                    op0=ALU.add, op1=ALU.mult))
                link(nc.vector.tensor_scalar(K.lnb[:, :], K.lnb[:, :], 1e-5, None, ALU.add))
                link(nc.vector.tensor_scalar(w_in[:, :], K.w["w_in"][:, :], K.w["g_res"][:, 0:1], None, ALU.mult))
                v.wait_ge(pre_pe, 1)
                link(nc.vector.tensor_scalar(ends[:, :], K.J[:, 0, 0:NB], -1.0, None, ALU.add))
                link(nc.vector.tensor_scalar(wrap[:, :], ends[:, :], 0.0, float(P), ALU.is_lt, ALU.mult))
                link(nc.vector.tensor_tensor(ends[:, :], ends[:, :], wrap[:, :], ALU.add))
                link(nc.vector.tensor_tensor(hot[:, :, :], bc(K.w["iota_row"][:, :].unsqueeze(1), [P, NB, P]),
                                             bc(ends[:, :].unsqueeze(2), [P, NB, P]), ALU.is_equal))
                v.wait_ge(pre_pe, 2)
                link(nc.vector.tensor_scalar(ends[:, :], K.J[:, 1, 0:NB], 1.0, None, ALU.min))
                with v.Fori(0, NB) as b:
                    nc.vector.bn_stats(st6c[:, b, :], K.w["ctx"][:, b, :]).then_inc(ctx_stats, 1)
                v.wait_ge(ctx_stats, NB)
                link(nc.vector.tensor_tensor(m1[:, :], st6c[:, :, 1], st6c[:, :, 1], ALU.mult))
                link(nc.vector.tensor_tensor(m2[:, :], st6c[:, :, 4], st6c[:, :, 4], ALU.mult))
                link(nc.vector.tensor_tensor(m1[:, :], m1[:, :], m2[:, :], ALU.add))
                link(nc.vector.tensor_tensor(m2[:, :], st6c[:, :, 2], st6c[:, :, 5], ALU.add))
                link(nc.vector.tensor_scalar(m2[:, :], m2[:, :], 1.0 / DC, 1e-5, ALU.mult, ALU.add))
                link(nc.vector.scalar_tensor_tensor(out=m1[:, :], in0=m1[:, :], scalar=0.5, in1=m2[:, :],
                                                    op0=ALU.mult, op1=ALU.add))
                v.wait_ge(pre_pe, 3)
                link(nc.vector.tensor_scalar(plug[:, :], K.J[:, 0, 0:NB], -1.0, 0.0, ALU.add, ALU.max))
                link(nc.vector.tensor_scalar(plug[:, :], plug[:, :], float(P - 1), None, ALU.min))
                link(nc.vector.tensor_tensor(hot[:, :, :], bc(K.w["ident"][:, :].unsqueeze(1), [P, NB, P]),
                                             bc(plug[:, :].unsqueeze(2), [P, NB, P]), ALU.mult))
                v.wait_ge(powers, 3)
                link(nc.vector.tensor_tensor(row_scale[:, :], K.rstd[:, :], row_scale[:, :], ALU.mult))
                link(nc.vector.tensor_scalar(rctx[:, :], rctx[:, :], keep, None, ALU.mult))
                start_counts(v, [lag_ready, pick_ready, hn_ready, x_done])
                with v.Fori(0, TURNS4) as it:
                    v.wait_ge(turned, done(it))
                    for j in range(G4):
                        b = G4 * it + j
                        m = nc.vector.tensor_scalar(hn[:, j, :], K.x[:, b, :], K.mean[:, bass.ds(b, 1)],
                                                    row_scale[:, bass.ds(b, 1)], ALU.subtract, ALU.mult)
                    m.then_inc(hn_ready, 1)
                    v.wait_ge(plug_ready, done(it + 1))
                    nc.vector.tensor_scalar(lag[:, :], K.S[:, 0, :], K.w["iota_col"][:, 0:1], 0.0, ALU.subtract, ALU.max)\
                        .then_inc(lag_ready, 1)
                    v.wait_ge(sum_ready, done(it))
                    for j in range(G4):
                        b = G4 * it + j
                        nc.vector.scalar_tensor_tensor(out=u[:, j, :], in0=K.w["ctx"][:, b, 0:D], scalar=rctx[:, bass.ds(b, 1)],
                                                       in1=K.w["g_init"][:, :], op0=ALU.mult, op1=ALU.mult)
                    v.wait_ge(decay_ready, done(it + 1))
                    nc.vector.scalar_tensor_tensor(out=pick[:, :, :].rearrange("p j t -> p (j t)"), in0=K.S[:, 0, :],
                                                   scalar=K.w["iota_col"][:, 0:1], in1=decay[:, :],
                                                   op0=ALU.is_ge, op1=ALU.mult).then_inc(pick_ready, 1)
                    v.wait_ge(sum_ready, done(it + 1))
                    xs = K.x[:, bass.ds(G4 * it, G4), :]
                    nc.vector.scalar_tensor_tensor(out=xs, in0=K.O[:, 0, :].rearrange("p (j d) -> p j d", j=G4),
                                                   scalar=K.tg[:, 1:2], in1=xs, op0=ALU.mult, op1=ALU.add).then_inc(x_done, 1)
                    v.wait_ge(x_done, done(it + 1))
                    for j in range(G4):
                        nc.vector.bn_stats(K.st6[:, G4 * it + j, :], K.x[:, G4 * it + j, :])

            @block.gpsimd
            def _(pool):
                pool.wait_ge(ln_chain, 7)
                nc.gpsimd.tensor_tensor(K.rstd[:, :], K.var[:, :], K.neg_half[:, :], ALU.pow).then_inc(powers, 1)
                pool.wait_ge(pre, 4)
                nc.gpsimd.tensor_tensor(row_scale[:, :], K.lnb[:, :], K.neg_half[:, :], ALU.pow).then_inc(powers, 1)
                pool.wait_ge(pre, 16)
                nc.gpsimd.tensor_tensor(rctx[:, :], m1[:, :], K.neg_half[:, :], ALU.pow).then_inc(powers, 1)

            @block.scalar
            def _(act):
                start_counts(act, [decay_ready, hT_ready])
                with act.Fori(0, TURNS4) as it:
                    act.wait_ge(turned, done(it + 1))
                    act.wait_ge(sum_ready, done(it))
                    nc.scalar.copy(hT[:, :], K.T[:, 0, :]).then_inc(hT_ready, 1)
                    act.wait_ge(lag_ready, done(it + 1))
                    act.wait_ge(pick_ready, done(it))
                    nc.scalar.activation(decay[:, :], lag[:, :], ACT.Exp, scale=-dt).then_inc(decay_ready, 1)

            @block.tensor
            def _(pe):
                pe.wait_ge(pre, 1)
                pe.wait_ge(K.w_loaded[2], K.w_count[2])
                nc.tensor.matmul(K.J[:, 0, 0:NB], K.w["upto"][:, :], lens[:, :], start=True, stop=True).then_inc(pre_pe, 1)
                pe.wait_ge(pre, 9)
                for b in range(NB):
                    m = nc.tensor.matmul(K.J[:, 1, b:b + 1], hot[:, b, :], K.ones_bf[:, 0:1], start=True, stop=True)
                m.then_inc(pre_pe, 1)
                pe.wait_ge(pre, 10)
                nc.tensor.matmul(K.J[:, 0, 0:NB], K.w["upto"][:, :], ends[:, :], start=True, stop=True).then_inc(pre_pe, 1)
                start_counts(pe, [plug_ready, turned, sum_ready])
                pe.wait_ge(pre, 20)
                with pe.Fori(0, TURNS4) as it:
                    pe.wait_ge(pick_ready, done(it))
                    nc.tensor.matmul(K.S[:, 0, :], K.ones_bf[:, :], hot[:, bass.ds(G4 * it, G4), :],
                                     start=True, stop=True).then_inc(plug_ready, 1)
                    pe.wait_ge(hn_ready, done(it + 1))
                    pe.wait_ge(hT_ready, done(it))
                    for j in range(G4):
                        m = nc.tensor.transpose(K.T[:, 0, j * P:(j + 1) * P], hn[:, j, :], K.w["ident"][:, :])
                    m.then_inc(turned, 1)
                    pe.wait_ge(hT_ready, done(it + 1))
                    pe.wait_ge(x_done, done(it))
                    pe.wait_ge(pick_ready, done(it + 1))
                    for j in range(G4):
                        o = K.O[:, 0, j * P:(j + 1) * P]
                        nc.tensor.matmul(o, hT[:, j * P:(j + 1) * P], w_in[:, :], start=True, stop=False)
                        nc.tensor.matmul(o, K.ones_row[0:1, :], K.w["b_in"][0:1, :], start=False, stop=False)
                        m = nc.tensor.matmul(o, pick[:, j, :], u[:, j, :], start=False, stop=True)
                    m.then_inc(sum_ready, 1)


def layer1_ffn(nc, K, A):
    E = EXPERTS1
    CH = 5
    with ExitStack() as c:
        def sb(name, shape, dt=F32):
            return c.enter_context(nc.sbuf_tensor(f"f1_{name}", shape, dt))

        def sem(name):
            return c.enter_context(nc.semaphore(f"f1_{name}"))

        xn = sb("xn", [P, G4, D])
        xnT = sb("xnT", [P, G4 * P])
        prob = sb("prob", [P, G4, E])
        best = sb("best", [P, G4])
        total = sb("total", [P, G4])
        above = sb("above", [P, G4, E, E])
        equal = sb("equal", [P, G4, E, E])
        rank = sb("rank", [P, G4, E])
        comb = sb("comb", [P, G4, E])
        combT = sb("combT", [E, G4 * P])
        tanh = sb("tanh", [P, 2, G4 * P])
        gated = sb("gated", [P, 2, G4 * P])
        hidden = sb("hidden", [P, 2, G4 * P])
        half_gate = sb("half_gate", [P, 1])
        fold_rows = sb("fold_rows", [P, 2, 512])
        down_w = sb("down_w", [P, 9, 2, 2, 256])
        ln_chain = sem("ln_chain")
        rstd_ready = sem("rstd_ready")
        xn_ready = sem("xn_ready")
        xn_used = sem("xn_used")
        xnT_ready = sem("xnT_ready")
        logits_ready = sem("logits_ready")
        dve_step = sem("dve_step")
        exp_ready = sem("exp_ready")
        comb_ready = sem("comb_ready")
        comb_turned = sem("comb_turned")
        combT_ready = sem("combT_ready")
        gu_ready = sem("gu_ready")
        tanh_ready = sem("tanh_ready")
        mul_step = sem("mul_step")
        hidden_ready = sem("hidden_ready")
        y_ready = sem("y_ready")
        x_done = sem("x_done")
        down_loaded = sem("down_loaded")
        fold = sem("fold")
        step2_done = sem("step2_done")
        MUL = 1 + 2 * (CH - 1)

        with nc.Block() as block:
            @block.sync
            def _(sp):
                sp.dma_start(down_w[:, :, :, :, :], bc(A["down_w"], [P, 9, 2, 2, 256])).then_inc(down_loaded, 16)
                sp.wait_ge(down_loaded, 16)

            @block.gpsimd
            def _(pool):
                start_counts(pool, [rstd_ready])
                pool.wait_ge(ln_chain, 7)
                for t in range(TURNS4):
                    pool_rstd4(nc, K, t, rstd_ready)
                pool.wait_ge(down_loaded, 16)
                pool.wait_ge(K.w_loaded[7], K.w_count[7])
                butterfly(nc, pool, K.w["down_rows"], fold_rows, down_w, fold, True)

            @block.tensor
            def _(pe):
                start_counts(pe, [xn_used, logits_ready, comb_turned, gu_ready, y_ready])
                pe.wait_ge(K.w_loaded[3], K.w_count[3])
                with pe.Fori(0, TURNS4) as it:
                    def down(ch):
                        pe.wait_ge(hidden_ready, done(CH * it + ch + 1))
                        if ch == 0:
                            pe.wait_ge(x_done, done(it))
                        for j in range(G4):
                            m = nc.tensor.matmul(K.J[:, 1, j * P:(j + 1) * P], hidden[:, ch % 2, j * P:(j + 1) * P],
                                                 K.w["wd1"][:, ch, :], start=(ch == 0 and j == 0), stop=(ch == CH - 1),
                                                 skip_group_check=True)
                        m.then_inc(y_ready, 1)

                    pe.wait_ge(xn_ready, done(it + 1))
                    pe.wait_ge(xnT_ready, done(it))
                    for j in range(G4):
                        m = nc.tensor.transpose(K.J[:, 0, j * P:(j + 1) * P], xn[:, j, :], K.w["ident"][:, :])
                    m.then_inc(xn_used, 1)
                    pe.wait_ge(xnT_ready, done(it + 1))
                    pe.wait_ge(hidden_ready, done(CH * it))
                    for j in range(G4):
                        m = nc.tensor.matmul(K.T[:, 0, j * E:(j + 1) * E], xnT[:, j * P:(j + 1) * P], K.w["router1"][:, :],
                                             start=True, stop=True)
                    m.then_inc(logits_ready, 1)
                    for ch in range(CH):
                        s = ch % 2
                        pe.wait_ge(hidden_ready, done(CH * it + ch - 1))
                        nc.tensor.matmul(K.S[:, s, :], K.w["wg1"][:, ch, :], xnT[:, :], start=True, stop=True)
                        m = nc.tensor.matmul(K.O[:, s, :], K.w["wu1"][:, ch, :], xnT[:, :], start=True, stop=True)
                        if ch == 1:
                            pe.wait_ge(comb_ready, done(it + 1))
                            for j in range(G4):
                                t = nc.tensor.transpose(K.T[0:E, 0, j * P:(j + 1) * P], comb[:, j, :], K.w["ident"][:, :])
                            t.then_inc(comb_turned, 1)
                            pe.wait_ge(combT_ready, done(it + 1))
                        if ch > 0:
                            m = nc.tensor.matmul(K.T[:, s, :], K.w["spread"][0:E, ch - 1, :], combT[0:E, :], start=True, stop=True)
                        m.then_inc(gu_ready, 1)
                        if ch > 0:
                            down(ch - 1)
                    down(CH - 1)

            @block.scalar
            def _(act):
                start_counts(act, [xnT_ready, exp_ready, combT_ready, tanh_ready])
                with act.Fori(0, TURNS4) as it:
                    def tanh_of(ch):
                        act.wait_ge(gu_ready, done(CH * it + ch + 1))
                        act.wait_ge(mul_step, done(MUL * it + (0, 0, 1, 2, 4)[ch]))
                        nc.scalar.activation(tanh[:, ch % 2, :], K.S[:, ch % 2, :], ACT.Tanh, scale=0.5).then_inc(tanh_ready, 1)
                    act.wait_ge(xn_used, done(it + 1))
                    act.wait_ge(gu_ready, done(CH * it))
                    nc.scalar.copy(xnT[:, :], K.J[:, 0, :]).then_inc(xnT_ready, 1)
                    act.wait_ge(dve_step, done(9 * it + 2))
                    nc.scalar.activation(prob[:, :, :], prob[:, :, :], ACT.Exp).then_inc(exp_ready, 1)
                    tanh_of(0)
                    act.wait_ge(comb_turned, done(it + 1))
                    nc.scalar.copy(combT[:, :], K.T[0:E, 0, :]).then_inc(combT_ready, 1)
                    for ch in range(1, CH):
                        tanh_of(ch)

            @block.vector
            def _(v):
                ln_statistics(nc, K, v, ln_chain)
                nc.vector.tensor_scalar(half_gate[:, :], K.tg[:, 5:6], 0.5, None, ALU.mult).then_inc(ln_chain, 1)
                v.wait_ge(ln_chain, 8)
                start_counts(v, [xn_ready, dve_step, step2_done, comb_ready, mul_step, hidden_ready, x_done])
                with v.Fori(0, TURNS4) as it:
                    n = [0]

                    def step(ins):
                        n[0] += 1
                        ins.then_inc(dve_step, 1)
                        v.wait_ge(dve_step, done(9 * it + n[0]))

                    def gate(ch):
                        s = ch % 2
                        first = MUL * it + (0 if ch == 0 else 2 * ch - 1)
                        v.wait_ge(tanh_ready, done(CH * it + ch + 1))
                        nc.vector.scalar_tensor_tensor(out=gated[:, s, :], in0=tanh[:, s, :], scalar=1.0, in1=K.S[:, s, :],
                                                       op0=ALU.add, op1=ALU.mult).then_inc(mul_step, 1)
                        v.wait_ge(mul_step, done(first + 1))
                        v.wait_ge(y_ready, done(CH * it + ch - 1))
                        if ch == 0:
                            nc.vector.tensor_tensor(hidden[:, s, :], gated[:, s, :], K.O[:, s, :], ALU.mult).then_inc(hidden_ready, 1)
                        else:
                            nc.vector.tensor_tensor(gated[:, s, :], gated[:, s, :], K.O[:, s, :], ALU.mult).then_inc(mul_step, 1)
                            v.wait_ge(mul_step, done(first + 2))
                            nc.vector.tensor_tensor(hidden[:, s, :], gated[:, s, :], K.T[:, s, :], ALU.mult).then_inc(hidden_ready, 1)

                    normalise4(nc, K, v, it, xn, rstd_ready, xn_ready, xn_used)
                    v.wait_ge(logits_ready, done(it + 1))
                    logits = K.T[:, 0, 0:G4 * E].rearrange("p (j e) -> p j e", j=G4)
                    step(nc.vector.tensor_reduce(best[:, :], logits, AX.X, ALU.max))
                    step(nc.vector.tensor_tensor(prob[:, :, :], logits, bc(best[:, :].unsqueeze(2), [P, G4, E]), ALU.subtract))
                    v.wait_ge(exp_ready, done(it + 1))
                    step(nc.vector.tensor_reduce(total[:, :], prob[:, :, :], AX.X, ALU.add))
                    step(nc.vector.reciprocal(total[:, :], total[:, :]))
                    step(nc.vector.tensor_tensor(prob[:, :, :], prob[:, :, :], bc(total[:, :].unsqueeze(2), [P, G4, E]), ALU.mult))
                    for j in range(G4):
                        other = bc(prob[:, j, :].unsqueeze(1), [P, E, E])
                        own = bc(prob[:, j, :].unsqueeze(2), [P, E, E])
                        nc.vector.tensor_tensor(above[:, j, :, :], other, own, ALU.is_gt)
                        m = nc.vector.tensor_tensor(equal[:, j, :, :], other, own, ALU.is_equal)
                    step(m)
                    step(nc.vector.tensor_tensor(equal[:, :, :, :], equal[:, :, :, :],
                                                 bc(K.w["before16"][:, :, :].unsqueeze(1), [P, G4, E, E]), ALU.mult))
                    step(nc.vector.tensor_tensor(above[:, :, :, :], above[:, :, :, :], equal[:, :, :, :], ALU.add))
                    step(nc.vector.tensor_reduce(rank[:, :, :], above[:, :, :, :], AX.X, ALU.add))
                    n[0] = 0

                    def step2(ins):
                        n[0] += 1
                        ins.then_inc(step2_done, 1)
                        v.wait_ge(step2_done, done(4 * it + n[0]))
                    step2(nc.vector.scalar_tensor_tensor(out=comb[:, :, :], in0=rank[:, :, :], scalar=2.0, in1=prob[:, :, :],
                                                         op0=ALU.is_lt, op1=ALU.mult))
                    step2(nc.vector.tensor_reduce(total[:, :], comb[:, :, :], AX.X, ALU.add))
                    step2(nc.vector.tensor_scalar(total[:, :], total[:, :], 1e-9, None, ALU.add))
                    step2(nc.vector.reciprocal(total[:, :], total[:, :]))
                    nc.vector.tensor_tensor(comb[:, :, :], comb[:, :, :], bc(total[:, :].unsqueeze(2), [P, G4, E]), ALU.mult)\
                        .then_inc(comb_ready, 1)
                    for ch in range(CH):
                        gate(ch)
                    v.wait_ge(y_ready, done(CH * (it + 1)))
                    xs = K.x[:, bass.ds(G4 * it, G4), :]
                    nc.vector.scalar_tensor_tensor(out=xs, in0=K.J[:, 1, :].rearrange("p (j d) -> p j d", j=G4),
                                                   scalar=half_gate[:, 0:1], in1=xs, op0=ALU.mult, op1=ALU.add).then_inc(x_done, 1)
                    v.wait_ge(x_done, done(it + 1))
                    for j in range(G4):
                        nc.vector.bn_stats(K.st6[:, G4 * it + j, :], K.x[:, G4 * it + j, :])


def layer2_attention(nc, K, A):
    H, HD, NT = 16, 64, 8
    W = HD + 1
    with ExitStack() as c:
        def sb(name, shape, dt=F32):
            return c.enter_context(nc.sbuf_tensor(f"l2_{name}", shape, dt))

        def sem(name):
            return c.enter_context(nc.semaphore(f"l2_{name}"))

        extra = (("o", 6), ("n", -5), ("x", -4), ("k0", -4), ("q0", -3), ("k1", -2), ("q1", -1), ("v0", 0), ("v1", 1),
                 ("a0", 3), ("a1", 5), ("f", 6))
        a = Attention(nc, c, "l2", 4, 2, 3, extra, ("k0", "k1", "v0", "v1", "x", "q0", "q1", "a0", "a1", "o"),
                      shared=("k0", "k1"))
        B = attn_buffers(nc, c, "l2")
        ctxT = sb("ctxT", [P, 2, 2, P])
        xn = sb("xn", [P, 2, D])
        xnT = sb("xnT", [P, 2, P])
        qT = sb("qT", [P, 2, NT, P])
        kz = sb("kz", [P, 2, NT, 2, P])
        vx = sb("vx", [P, 2, H, W])
        attn = sb("attn", [P, 2, H * HD])
        attnT = sb("attnT", [P, 2, NT, P])
        xb = sb("xb", [P, 2, D])
        neg_nullk = sb("neg_nullk", [P, 1])
        null_row = sb("null_row", [1, P])
        gscale = sb("gscale", [P, D])
        gbias = sb("gbias", [P, D])
        ost = sb("ost", [P, 2, 6])
        omv = sb("omv", [P, 2, 2])
        ovar = sb("ovar", [P, 2])
        orstd = sb("orstd", [P, 2])
        centred = sb("centred", [P, 2, D])
        ctx_loaded = [sem(f"ctx_loaded{k}") for k in range(2)]
        prepared = sem("prepared")
        null_ready = sem("null_row_ready")
        xb_ready = sem("xb_ready")
        ostat = sem("ostat")
        ostat_seen = sem("ostat_seen")
        orstd_ready = sem("orstd_ready")

        with nc.Block() as block:
            @block.sync
            def _(sp):
                with sp.Fori(0, TURNS2) as it:
                    for k in range(2):
                        sp.wait_ge(a.copied["v1"], done(2 * it + k - 1))
                        sp.dma_start(ctxT[:, k, :, :], A["ctxT"].rearrange("b (c p) t -> p b c t", p=P)[:, 2 * it + k, :, :])\
                            .then_inc(ctx_loaded[k], 16)

            @block.tensor
            def _(pe):
                start_counts(pe, [a.scores_ready, a.turned, a.summed, *a.j_ready.values()])
                pe.wait_ge(K.w_loaded[4], K.w_count[4])
                for t in range(NT):
                    m = nc.tensor.matmul(K.O[0:1, 0, 0:P], K.w["nullv"][:, 0:1], K.w["wout2"][:, t, :], start=(t == 0), stop=(t == NT - 1))
                m.then_inc(null_ready, 1)
                pe.wait_ge(prepared, 6)

                def step_of(it, step):
                    kind, k = step[0], step[1]
                    b = 2 * it + k
                    if kind in a.copied:
                        a.wait_bank(pe, it, kind, k)
                        J = K.J[:, a.j_bank(kind, k), :]
                    if kind in ("k0", "k1"):
                        if kind == "k0":
                            pe.wait_ge(ctx_loaded[k], 16 * it + 16)
                        for t in range(4):
                            f = P * (t + 4 * int(kind[1]))
                            for j in range(2):
                                m = nc.tensor.matmul(J[:, t * P:(t + 1) * P], K.w["wkv2"][:, j, f:f + P], ctxT[:, k, j, :],
                                                     start=(j == 0), stop=(j == 1))
                    elif kind in ("v0", "v1"):
                        f = H * HD + 512 * int(kind[1])
                        for j in range(2):
                            m = nc.tensor.matmul(J, ctxT[:, k, j, :], K.w["wkv2"][:, j, f:f + 512], start=(j == 0), stop=(j == 1))
                    elif kind == "x":
                        pe.wait_ge(a.xn_ready, done(b + 1))
                        m = nc.tensor.transpose(J[:, 0:P], xn[:, k, :], K.w["ident"][:, :])
                    elif kind in ("q0", "q1"):
                        pe.wait_ge(a.copied["x"], done(b + 1))
                        for t in range(4):
                            m = nc.tensor.matmul(J[:, t * P:(t + 1) * P], K.w["wq2"][:, t + 4 * int(kind[1]), :], xnT[:, k, :],
                                                 start=True, stop=True)
                    elif kind in ("a0", "a1"):
                        half = int(kind[1])
                        pe.wait_ge(a.normed, done(a.unit(it, k, 2 * half + 1) + 1))
                        for t in range(4):
                            f = P * (t + 4 * half)
                            m = nc.tensor.transpose(J[:, t * P:(t + 1) * P], attn[:, k, f:f + P], K.w["ident"][:, :])
                    elif kind == "o":
                        nc.tensor.matmul(J[:, 0:P], K.ones_row[0:1, :], null_row[0:1, :], start=True, stop=False)
                        for t in range(NT):
                            if t % 4 == 0:
                                pe.wait_ge(a.copied[f"a{t // 4}"], done(b + 1))
                            m = nc.tensor.matmul(J[:, 0:P], attnT[:, k, t, :], K.w["wout2"][:, t, :], start=False, stop=(t == NT - 1))
                    elif kind == "S":
                        g = step[2]
                        u = a.unit(it, k, g)
                        s = g % 2
                        if g % 2 == 0:
                            for need in (f"q{g // 2}", f"k{g // 2}"):
                                pe.wait_ge(a.copied[need], a.copied_at(need, b + 1))
                        pe.wait_ge(a.shifted, done(u - 1))
                        for i in range(2):
                            m = nc.tensor.matmul(K.S[:, s, 256 * i:256 * i + 256], qT[:, k, 2 * g + i, :],
                                                 kz[:, k, 2 * g + i, :, :], start=True, stop=True)
                        m.then_inc(a.scores_ready, 1)
                    elif kind == "T":
                        pe_turn(nc, K, pe, a, B, it, k, step[2])
                    elif kind == "V":
                        g = step[2]
                        if g % 2 == 0:
                            pe.wait_ge(a.copied[f"v{g // 2}"], done(b + 1))
                        pe_values(nc, K, pe, a, B, it, k, g, lambda h: vx[:, k, 4 * g + h, :], W)
                    if kind in a.copied:
                        m.then_inc(a.j_ready[kind], 1)
                a.run(pe, step_of)

            @block.vector
            def _(v):
                start_counts(v, [a.max_ready, a.shifted, a.recip_ready, a.normed, a.x_done, ostat,
                                 a.copied["v0"], a.copied["v1"], a.copied["o"]])
                ln_statistics(nc, K, v, a.ln_chain)
                v.wait_ge(K.w_loaded[4], K.w_count[4])
                nc.vector.memset(vx[:, :, :, HD:W], 1.0).then_inc(prepared, 1)
                nc.vector.memset(kz[:, :, :, :, :], 0.0).then_inc(prepared, 1)
                nc.vector.tensor_scalar(neg_nullk[:, :], K.w["nullk"][:, :], -1.0, None, ALU.mult).then_inc(prepared, 1)
                nc.vector.tensor_scalar(gscale[:, :], K.w["ln_scale"][:, :], K.tg[:, 2:3], None, ALU.mult).then_inc(prepared, 1)
                nc.vector.tensor_scalar(gbias[:, :], K.w["ln_bias"][:, :], K.tg[:, 2:3], None, ALU.mult).then_inc(prepared, 1)
                v.wait_ge(null_ready, 1)
                nc.vector.tensor_copy(null_row[0:1, :], K.O[0:1, 0, 0:P]).then_inc(prepared, 1)
                v.wait_ge(prepared, 6)

                def step_of(it, step):
                    kind, k = step[0], step[1]
                    b = 2 * it + k
                    if kind in ("k0", "k1"):
                        v.wait_ge(a.j_ready[kind], done(b + 1))
                        if kind == "k0":
                            v.wait_ge(a.scores_ready, done(a.unit(it, k, 3) + 1 - a.units))
                        t = 4 * int(kind[1])
                        J = K.J[64:128, a.j_bank(kind, k), :].rearrange("p (t q) -> p t q", t=4)
                        nc.vector.tensor_scalar(kz[64:128, k, t:t + 4, 1, :], J, K.w["nullk"][64:128, 0:1], None, ALU.subtract)\
                            .then_inc(a.copied[kind], 1)
                    elif kind in ("v0", "v1"):
                        v.wait_ge(a.j_ready[kind], done(b + 1))
                        if kind == "v0":
                            v.wait_ge(a.summed, done(a.unit(it, k, 3) + 1 - a.units))
                        h = 8 * int(kind[1])
                        J = K.J[:, a.j_bank(kind, k), :].rearrange("p (h d) -> p h d", h=8)
                        nc.vector.tensor_tensor(vx[:, k, h:h + 8, 0:HD], J, bc(K.w["nullv_row"][:, :].unsqueeze(1), [P, 8, HD]),
                                                ALU.subtract).then_inc(a.copied[kind], 1)
                    elif kind == "S":
                        dve_shift(nc, K, v, a, B, it, k, step[2], clamp=True)
                    elif kind == "V":
                        g = step[2]
                        if g == 0:
                            v.wait_ge(a.copied["a1"], done(b - 1))
                        dve_norm(nc, K, v, a, B, it, k, g,
                                 attn[:, k, 256 * g:256 * g + 256].rearrange("p (h d) -> p h d", h=4), W, null=True)
                    elif kind == "o":
                        v.wait_ge(a.j_ready[kind], done(b + 1))
                        v.wait_ge(orstd_ready, done(b - 1))
                        nc.vector.bn_stats(ost[:, k, :], K.J[:, a.j_bank(kind, k), 0:P]).then_inc(ostat, 1)
                        v.wait_ge(ostat, done(3 * b + 1))
                        v.sem_inc(ostat_seen, 1)
                        nc.vector.bn_aggr(omv[:, k, :], ost[:, k, :]).then_inc(ostat, 1)
                        v.wait_ge(ostat, done(3 * b + 2))
                        nc.vector.tensor_scalar(ovar[:, k:k + 1], omv[:, k, 1:2], 1e-6, None, ALU.add).then_inc(ostat, 1)
                        nc.vector.scalar_tensor_tensor(out=centred[:, k, :], in0=K.J[:, a.j_bank(kind, k), 0:P],
                                                       scalar=omv[:, k, 0:1], in1=gscale[:, :], op0=ALU.subtract,
                                                       op1=ALU.mult).then_inc(a.copied["o"], 1)
                    elif kind == "f":
                        v.wait_ge(orstd_ready, done(b + 1))
                        v.wait_ge(xb_ready, done(b + 1))
                        v.wait_ge(a.copied["o"], done(b + 1))
                        nc.vector.scalar_tensor_tensor(out=K.x[:, b, :], in0=centred[:, k, :], scalar=orstd[:, k:k + 1],
                                                       in1=xb[:, k, :], op0=ALU.mult, op1=ALU.add).then_inc(a.x_done, 1)
                        v.wait_ge(a.x_done, done(b + 1))
                        nc.vector.bn_stats(K.st6[:, b, :], K.x[:, b, :])
                a.run(v, step_of)

            @block.scalar
            def _(act):
                start_counts(act, [a.exp_ready, a.null_ready, a.turned_copied, a.copied["x"], a.copied["q0"], a.copied["q1"],
                                   a.copied["a0"], a.copied["a1"], a.copied["k0"], a.copied["k1"]])
                act.wait_ge(prepared, 6)

                def step_of(it, step):
                    kind, k = step[0], step[1]
                    b = 2 * it + k
                    if kind in ("x", "k0", "k1", "q0", "q1", "a0", "a1"):
                        act.wait_ge(a.j_ready[kind], done(b + 1))
                        J = K.J[:, a.j_bank(kind, k), :]
                        J4 = J.rearrange("p (t q) -> p t q", t=4)
                    if kind == "x":
                        act.wait_ge(a.copied["q1"], done(b - 1))
                        nc.scalar.copy(xnT[:, k, :], J[:, 0:P]).then_inc(a.copied["x"], 1)
                    elif kind in ("k0", "k1"):
                        if kind == "k0":
                            act.wait_ge(a.scores_ready, done(a.unit(it, k, 3) + 1 - a.units))
                        t = 4 * int(kind[1])
                        nc.scalar.activation(kz[0:64, k, t:t + 4, 0, :], J4[0:64, :, :], ACT.Identity,
                                             bias=neg_nullk[0:64, 0:1]).then_inc(a.copied[kind], 1)
                    elif kind in ("q0", "q1"):
                        if kind == "q0":
                            act.wait_ge(a.scores_ready, done(a.unit(it, k, 3) + 1 - a.units))
                        t = 4 * int(kind[1])
                        nc.scalar.copy(qT[:, k, t:t + 4, :], J4).then_inc(a.copied[kind], 1)
                    elif kind in ("a0", "a1"):
                        if kind == "a0":
                            act.wait_ge(a.copied["o"], done(b - 1))
                        t = 4 * int(kind[1])
                        nc.scalar.copy(attnT[:, k, t:t + 4, :], J4).then_inc(a.copied[kind], 1)
                    elif kind == "S":
                        act_exp(nc, K, act, a, B, it, k, step[2], float(HD) ** -0.5, null=True)
                    elif kind == "T":
                        act_copy_turned(nc, K, act, a, B, it, k, step[2])
                a.run(act, step_of, copies_first=True)

            @block.gpsimd
            def _(pool):
                start_counts(pool, [a.centred_ready, a.xn_ready, xb_ready, orstd_ready])
                pool_rstd(nc, K, pool, a.ln_chain, a.rstd_ready)
                pool.wait_ge(a.rstd_ready, 1)
                pool.wait_ge(prepared, 5)

                def step_of(it, step):
                    kind, k = step[0], step[1]
                    b = 2 * it + k
                    if kind == "n":
                        pool_normalise(nc, K, pool, a, xn, b, k)
                    elif kind == "a0":
                        pool.wait_ge(a.x_done, done(b - 1))
                        pool.sem_inc(a.wait_carried, 1)
                        nc.gpsimd.tensor_tensor(xb[:, k, :], K.x[:, b, :], gbias[:, :], ALU.add).then_inc(xb_ready, 1)
                    elif kind == "o":
                        pool.wait_ge(a.x_done, done(b - 1))
                        pool.wait_ge(ostat, done(3 * b + 3))
                        nc.gpsimd.tensor_tensor(orstd[:, k:k + 1], ovar[:, k:k + 1], K.neg_half[:, 0:1], ALU.pow)\
                            .then_inc(orstd_ready, 1)
                a.run(pool, step_of)


def layer2_ffn(nc, K, A):
    NG, GB = 4, 8
    H, HD = 16, 8
    W = HD + 1
    F = 512
    CH = F // P
    RC = 9
    ROUND = 1.5 * 2.0 ** 23
    TWO_PI = (6.28125, 0.0019350051879882812, 3.0199159795074593e-07)
    with ExitStack() as c:
        def sb(name, shape, dt=F32):
            return c.enter_context(nc.sbuf_tensor(f"f2_{name}", shape, dt))

        def sem(name):
            return c.enter_context(nc.semaphore(f"f2_{name}"))

        xn = sb("xn", [P, NB, D])
        big = sb("big", [P, NB, P])
        big2 = sb("big2", [P, NB, P])
        kz = big2[:, :, :].rearrange("p (s h) t -> p s h t", s=2)
        wr = sb("wr", [P, NB])
        rank = sb("rank", [P, NB])
        ge = sb("ge", [P, NB])
        ties = sb("ties", [P, NB])
        rest = sb("rest", [P, NB])
        above = sb("above", [P, G4, P])
        equal = sb("equal", [P, G4, P])
        sel = sb("sel", [P, NB, SEL])
        pos_i = sb("pos_i", [P, 4], I32)
        pos = sb("pos", [P, 4])
        ang = sb("ang", [P, 4, 4])
        turns = sb("turns", [P, 4, 4])
        cs = sb("cs", [P, 4, 8])
        tab = sb("tab", [P, NB, RC])
        maskr = sb("maskr", [P, 4, P])
        half = sb("half", [P, NB, SEL])
        madd = sb("madd", [P, NG, P])
        xsT = sb("xsT", [P, NG, P])
        tabT = sb("tabT", [RC, NG, P])
        xs = sb("xs", [P, NG, D])
        tabs = sb("tabs", [P, NG, RC])
        sq = sb("sq", [P, NG, D])
        ms = sb("ms", [P, NG])
        rs = sb("rs", [P, NG])
        qkv = sb("qkv", [P, NG, 3 * D])
        rope = sb("rope", [P, NG, 2 * H, HD])
        part = sb("part", [P, NG, 2 * H, 4])
        qT = sb("qT", [P, NG, P])
        kT = sb("kT", [P, NG, P])
        vx = sb("vx", [P, NG, H, W])
        attn = sb("attn", [P, NG, D])
        attnT = sb("attnT", [P, NG, P])
        hT = sb("hT", [P, CH, NG * P])
        wqkv = sb("wqkv", [P, 3 * D])
        w1 = sb("w1", [P, F])
        loaded = sem("loaded")
        ln_chain = sem("ln_chain")
        chain = sem("chain")
        event = {name: sem(name) for name in (
            "diagonal", "stay_weights", "selection", "angles", "table", "folded", "xsT", "mask_rows", "xs_tabs", "ms1",
            "roped", "ms2", "x1n", "result",
            "rstd", "rs1", "rs2", "padded", "x_kept", "xn_scaled",
            "sines", "tabT", "qkv_scaled", "qT", "kT", "attnT", "x1nT",
            "gathered", "half_masked", "turned_back", "masked", "projected", "q_turned", "k_turned",
            "attn_turned", "attn_projected", "x1_turned", "y")}
        spread_ready = sem("spread_ready")
        ranked = sem("ranked")
        kz_ready = sem("kz_ready")
        h_ready = sem("h_ready")
        gelu_ready = sem("gelu_ready")
        sel_turned = sem("sel_turned")
        selT_ready = sem("selT_ready")
        scattered = sem("scattered")
        x_done = sem("x_done")

        units = [(g, h) for g in range(NG) for h in range(4)]
        sched = [("S",) + units[0], ("S",) + units[1]]
        for i in range(len(units)):
            sched.append(("T",) + units[i])
            if i + 2 < len(units):
                sched.append(("S",) + units[i + 2])
            if i >= 1:
                sched.append(("V",) + units[i - 1])
        sched.append(("V",) + units[-1])
        a = Attention(nc, c, "f2a", 4, 4, 0, (), ())
        B = attn_buffers(nc, c, "f2a")
        qkv_banks = (K.S[:, 0, :], K.S[:, 1, :], K.O[:, 0, :], K.O[:, 1, :])
        mask_row = lambda b: min(b, 3)
        by_group = lambda ap: ap.rearrange("p (g t) -> p g t", g=NG)

        with nc.Block() as block:
            @block.sync
            def _(sp):
                sp.dma_start(pos_i[:, :], A["posT"]).then_inc(loaded, 16)
                sp.dma_start(maskr[:, :, :], A["L2_ffn_attention_mask"].rearrange("b o q k -> q (b o) k")[0:P, :, 0:P])\
                    .then_inc(loaded, 16)
                sp.wait_ge(loaded, 32)

            @block.tensor
            def _(pe):
                start_counts(pe, [spread_ready, a.scores_ready, a.turned, a.summed, h_ready, sel_turned, scattered])
                pe.wait_ge(K.w_loaded[5], K.w_count[5])
                pe.wait_ge(loaded, 32)
                pe.wait_ge(event["diagonal"], 1)
                with pe.Fori(0, TURNS4) as it:
                    pe.wait_ge(ranked, done(6 * it - 4))
                    nc.tensor.matmul(K.S[:, 0, :], K.ones_f[:, :], big[:, bass.ds(G4 * it, G4), :], start=True, stop=True)\
                        .then_inc(spread_ready, 1)
                pe.wait_ge(event["table"], 1)
                for b in range(NB):
                    nc.tensor.matmul(K.J[:, 0, b * SEL:(b + 1) * SEL], xn[:, b, :], sel[:, b, :], start=True, stop=True)
                for b in range(NB):
                    m = nc.tensor.matmul(K.O[0:RC, 0, b * SEL:(b + 1) * SEL], tab[:, b, :], sel[:, b, :], start=True, stop=True)
                m.then_inc(event["gathered"], 1)
                for b in range(NB):
                    m = nc.tensor.matmul(K.S[:, 1, b * SEL:(b + 1) * SEL], maskr[:, mask_row(b), :], sel[:, b, :], start=True, stop=True)
                m.then_inc(event["half_masked"], 1)
                pe.wait_ge(event["xsT"], 1)
                pe.wait_ge(event["tabT"], 1)
                for g in range(NG):
                    nc.tensor.transpose(K.T[:, 0, g * P:(g + 1) * P], xsT[:, g, :], K.w["ident"][:, :])
                for g in range(NG):
                    m = nc.tensor.transpose(K.T[:, 1, g * RC:(g + 1) * RC], tabT[0:RC, g, :], K.w["ident"][0:RC, 0:RC])
                m.then_inc(event["turned_back"], 1)
                pe.wait_ge(event["folded"], 1)
                pe.wait_ge(event["mask_rows"], 1)
                for g in range(NG):
                    m = nc.tensor.matmul(qkv_banks[g][:, 0:3 * D], xsT[:, g, :], wqkv[:, :], start=True, stop=True)
                m.then_inc(event["projected"], 1)
                for b in range(NB):
                    g = b // GB
                    m = nc.tensor.matmul(K.J[:, 1, b * SEL:(b + 1) * SEL], half[:, GB * g:GB * g + GB, :], sel[:, b, :],
                                         start=True, stop=True)
                m.then_inc(event["masked"], 1)
                pe.wait_ge(event["roped"], 1)
                for g in range(NG):
                    m = nc.tensor.transpose(K.J[:, 0, g * P:(g + 1) * P], rope[:, g, 0:H, :], K.w["ident"][:, :])
                m.then_inc(event["q_turned"], 1)
                for g in range(NG):
                    m = nc.tensor.transpose(K.T[:, 0, g * P:(g + 1) * P], rope[:, g, H:2 * H, :], K.w["ident"][:, :])
                m.then_inc(event["k_turned"], 1)
                pe.wait_ge(event["qT"], 1)
                pe.wait_ge(event["kT"], 1)
                for kind, g, h in sched:
                    u = 4 * g + h
                    if kind == "S":
                        if h == 0:
                            pe.wait_ge(kz_ready, done(g + 1))
                        pe.wait_ge(a.max_ready, done(2 * (u - 1)))
                        nc.tensor.matmul(K.S[:, u % 2, :], qT[:, g, :], kz[:, g % 2, 4 * h:4 * h + 4, :], start=True, stop=True)\
                            .then_inc(a.scores_ready, 1)
                    elif kind == "T":
                        pe_turn(nc, K, pe, a, B, 0, g, h)
                    elif kind == "V":
                        pe_values(nc, K, pe, a, B, 0, g, h, lambda i: vx[:, g, 4 * h + i, :], W)
                pe.wait_ge(a.normed, done(4 * NG))
                for g in range(NG):
                    m = nc.tensor.transpose(K.J[:, 0, g * P:(g + 1) * P], attn[:, g, :], K.w["ident"][:, :])
                m.then_inc(event["attn_turned"], 1)
                pe.wait_ge(event["attnT"], 1)
                for g in range(NG):
                    m = nc.tensor.matmul(K.J[:, 1, g * P:(g + 1) * P], attnT[:, g, :], K.w["wo2"][:, :], start=True, stop=True)
                m.then_inc(event["attn_projected"], 1)
                pe.wait_ge(event["padded"], NG)
                for t in range(TURNS4):
                    pe.wait_ge(selT_ready, done(t - 1))
                    for j in range(G4):
                        m = nc.tensor.transpose(K.T[:, t % 2, j * P:(j + 1) * P], big[:, G4 * t + j, :], K.w["ident"][:, :])
                    m.then_inc(sel_turned, 1)
                pe.wait_ge(event["x1n"], 1)
                for g in range(NG):
                    m = nc.tensor.transpose(K.J[:, 0, g * P:(g + 1) * P], sq[:, g, :], K.w["ident"][:, :])
                m.then_inc(event["x1_turned"], 1)
                pe.wait_ge(event["x1nT"], 1)
                for ch in range(CH):
                    pe.wait_ge(gelu_ready, done(ch - 1))
                    nc.tensor.matmul(K.S[:, ch % 2, :], w1[:, ch * P:(ch + 1) * P], attnT[:, :, :], start=True, stop=True)\
                        .then_inc(h_ready, 1)
                pe.wait_ge(gelu_ready, done(CH))
                for g in range(NG):
                    for ch in range(CH):
                        m = nc.tensor.matmul(K.O[:, 0, g * P:(g + 1) * P], hT[:, ch, g * P:(g + 1) * P], K.w["w2_2"][:, ch, :],
                                             start=(ch == 0), stop=(ch == CH - 1))
                m.then_inc(event["y"], 1)
                pe.wait_ge(event["result"], 1)
                for t in range(TURNS4):
                    pe.wait_ge(selT_ready, done(t + 1))
                    pe.wait_ge(x_done, done(t - 1))
                    for j in range(G4):
                        b = G4 * t + j
                        m = nc.tensor.matmul(K.S[:, t % 2, j * P:(j + 1) * P], big2[:, b, :], xs[:, b // GB, :], start=True, stop=True)
                    m.then_inc(scattered, 1)

            @block.scalar
            def _(act):
                start_counts(act, [a.exp_ready, a.turned_copied, selT_ready, gelu_ready])
                act.wait_ge(event["angles"], 1)
                nc.scalar.activation(cs[:, :, 4:8], ang[:, :, :], ACT.Sin).then_inc(event["sines"], 1)
                nc.scalar.activation(cs[:, :, 0:4], turns[:, :, :], ACT.Sin).then_inc(event["sines"], 1)
                act.wait_ge(event["gathered"], 1)
                nc.scalar.copy(tabT[:, :, :], by_group(K.O[0:RC, 0, :])).then_inc(event["tabT"], 1)
                act.wait_ge(event["rs1"], 1)
                act.wait_ge(event["projected"], 1)
                for g in range(NG):
                    nc.scalar.mul(qkv[:, g, :], qkv_banks[g][:, 0:3 * D], rs[:, g:g + 1]).then_inc(event["qkv_scaled"], 1)
                act.wait_ge(event["q_turned"], 1)
                nc.scalar.copy(qT[:, :, :], by_group(K.J[:, 0, :])).then_inc(event["qT"], 1)
                act.wait_ge(event["k_turned"], 1)
                nc.scalar.copy(kT[:, :, :], by_group(K.T[:, 0, :])).then_inc(event["kT"], 1)
                for kind, g, h in sched:
                    if kind == "S":
                        act_exp(nc, K, act, a, B, 0, g, h, 1.0)
                    elif kind == "T":
                        act_copy_turned(nc, K, act, a, B, 0, g, h)
                act.wait_ge(event["attn_turned"], 1)
                nc.scalar.copy(attnT[:, :, :], by_group(K.J[:, 0, :])).then_inc(event["attnT"], 1)
                act.wait_ge(a.scores_ready, done(4 * NG))
                for t in range(TURNS4):
                    act.wait_ge(sel_turned, done(t + 1))
                    nc.scalar.copy(big2[:, G4 * t:G4 * t + G4, :], K.T[:, t % 2, :].rearrange("p (j t) -> p j t", j=G4))\
                        .then_inc(selT_ready, 1)
                act.wait_ge(event["x1_turned"], 1)
                nc.scalar.copy(attnT[:, :, :], by_group(K.J[:, 0, :])).then_inc(event["x1nT"], 1)
                for ch in range(CH):
                    act.wait_ge(h_ready, done(ch + 1))
                    nc.scalar.activation(hT[:, ch, :], K.S[:, ch % 2, :], ACT.Gelu_apprx_tanh).then_inc(gelu_ready, 1)

            @block.gpsimd
            def _(pool):
                start_counts(pool, [kz_ready])
                pool.wait_ge(ln_chain, 7)
                nc.gpsimd.tensor_tensor(K.rstd[:, :], K.var[:, :], K.neg_half[:, :], ALU.pow).then_inc(event["rstd"], 1)
                pool.wait_ge(event["ms1"], 1)
                nc.gpsimd.tensor_tensor(rs[:, :], ms[:, :], K.neg_half[:, 0:NG], ALU.pow).then_inc(event["rs1"], 1)
                pool.wait_ge(event["kT"], 1)
                for g in range(NG):
                    pool.wait_ge(a.scores_ready, done(4 * (g - 1)))
                    nc.gpsimd.tensor_tensor(kz[:, g % 2, :, :], bc(kT[:, g, :].unsqueeze(1), [P, H, P]),
                                            bc(K.w["head8"][:, :].unsqueeze(2), [P, H, P]), ALU.mult).then_inc(kz_ready, 1)
                    own = slice(GB * g, GB * g + GB)
                    nc.gpsimd.tensor_tensor(big[:, own, :].rearrange("p b (k s) -> p b k s", s=SEL),
                                            bc(sel[:, own, :].unsqueeze(2), [P, GB, GB, SEL]),
                                            bc(K.w["eye8"][:, :, :].unsqueeze(3), [P, GB, GB, SEL]), ALU.mult).then_inc(event["padded"], 1)
                nc.gpsimd.tensor_tensor(xn[:, :, :], xn[:, :, :], bc(rest[:, :].unsqueeze(2), [P, NB, D]), ALU.mult)\
                    .then_inc(event["xn_scaled"], 1)
                pool.wait_ge(event["xn_scaled"], 1)
                nc.gpsimd.tensor_tensor(K.x[:, :, :], K.x[:, :, :], xn[:, :, :], ALU.add).then_inc(event["x_kept"], 1)
                pool.wait_ge(event["ms2"], 1)
                nc.gpsimd.tensor_tensor(rs[:, :], ms[:, :], K.neg_half[:, 0:NG], ALU.pow).then_inc(event["rs2"], 1)

            @block.vector
            def _(v):
                n = [0]

                def link(ins):
                    n[0] += 1
                    ins.then_inc(chain, 1)
                    v.wait_ge(chain, n[0])

                def tell(name):
                    v.sem_inc(event[name], 1)

                start_counts(v, [ranked, a.max_ready, a.shifted, a.recip_ready, a.normed, x_done])
                ln_statistics(nc, K, v, ln_chain)
                v.wait_ge(K.w_loaded[5], K.w_count[5])
                v.wait_ge(loaded, 32)
                link(nc.vector.tensor_tensor(xn[:, :, :], K.x[:, :, :], bc(K.mean[:, :].unsqueeze(2), [P, NB, D]), ALU.subtract))
                v.wait_ge(event["rstd"], 1)
                link(nc.vector.tensor_tensor(xn[:, :, :], xn[:, :, :], bc(K.rstd[:, :].unsqueeze(2), [P, NB, D]), ALU.mult))
                link(nc.vector.tensor_tensor(big[:, :, :], xn[:, :, :], bc(K.w["router2"][:, :].unsqueeze(1), [P, NB, D]), ALU.mult))
                link(nc.vector.tensor_reduce(wr[:, :], big[:, :, :], AX.X, ALU.add))
                link(nc.vector.tensor_scalar(wr[:, :], wr[:, :], K.w["router2_b"][:, 0:1], None, ALU.add))
                link(nc.vector.tensor_tensor(big[:, :, :], bc(K.w["ident"][:, :].unsqueeze(1), [P, NB, P]),
                                             bc(wr[:, :].unsqueeze(2), [P, NB, P]), ALU.mult))
                tell("diagonal")
                with v.Fori(0, TURNS4) as it:
                    seqs = bass.ds(G4 * it, G4)
                    own = bc(wr[:, seqs].unsqueeze(2), [P, G4, P])
                    other = K.S[:, 0, :].rearrange("p (j t) -> p j t", j=G4)
                    v.wait_ge(ranked, done(6 * it))
                    v.wait_ge(spread_ready, done(it + 1))
                    nc.vector.tensor_tensor(above[:, :, :], other, own, ALU.is_gt).then_inc(ranked, 1)
                    nc.vector.tensor_tensor(equal[:, :, :], other, own, ALU.is_equal).then_inc(ranked, 1)
                    v.wait_ge(ranked, done(6 * it + 2))
                    nc.vector.tensor_reduce(rank[:, seqs], above[:, :, :], AX.X, ALU.add).then_inc(ranked, 1)
                    nc.vector.tensor_reduce(ge[:, seqs], equal[:, :, :], AX.X, ALU.add).then_inc(ranked, 1)
                    v.wait_ge(ranked, done(6 * it + 4))
                    nc.vector.tensor_tensor(equal[:, :, :], equal[:, :, :], bc(K.w["before128"][:, :].unsqueeze(1), [P, G4, P]),
                                            ALU.mult).then_inc(ranked, 1)
                    v.wait_ge(ranked, done(6 * it + 5))
                    nc.vector.tensor_reduce(ties[:, seqs], equal[:, :, :], AX.X, ALU.add).then_inc(ranked, 1)
                v.wait_ge(ranked, done(6 * TURNS4))
                link(nc.vector.tensor_tensor(ge[:, :], ge[:, :], rank[:, :], ALU.add))
                link(nc.vector.tensor_tensor(rank[:, :], rank[:, :], ties[:, :], ALU.add))
                link(nc.vector.tensor_scalar(rest[:, :], ge[:, :], float(SEL), K.tg[:, 6:7], ALU.is_ge, ALU.mult))
                link(nc.vector.tensor_tensor(sel[:, :, :], bc(K.w["slots"][:, :].unsqueeze(1), [P, NB, SEL]),
                                             bc(rank[:, :].unsqueeze(2), [P, NB, SEL]), ALU.is_equal))
                link(nc.vector.tensor_copy(pos[:, :], pos_i[:, :]))
                link(nc.vector.tensor_tensor(ang[:, :, :], bc(pos[:, :].unsqueeze(2), [P, 4, 4]),
                                             bc(K.w["inv_freq"][:, :].unsqueeze(1), [P, 4, 4]), ALU.mult))
                link(nc.vector.tensor_scalar(turns[:, :, :], ang[:, :, :], 0.15915494309189535, ROUND, ALU.mult, ALU.add))
                link(nc.vector.tensor_scalar(turns[:, :, :], turns[:, :, :], -ROUND, None, ALU.add))
                for part_of_2pi in TWO_PI:
                    link(nc.vector.scalar_tensor_tensor(out=ang[:, :, :], in0=turns[:, :, :], scalar=-part_of_2pi,
                                                        in1=ang[:, :, :], op0=ALU.mult, op1=ALU.add))
                link(nc.vector.tensor_scalar(ang[:, :, :], ang[:, :, :], 3.1415925, -3.1415925, ALU.min, ALU.max))
                link(nc.vector.tensor_scalar(turns[:, :, :], ang[:, :, :], -1.0, None, ALU.mult))
                link(nc.vector.tensor_tensor(turns[:, :, :], turns[:, :, :], ang[:, :, :], ALU.max))
                link(nc.vector.tensor_scalar(turns[:, :, :], turns[:, :, :], -1.0, 1.5707963267948966, ALU.mult, ALU.add))
                tell("angles")
                link(nc.vector.tensor_scalar(wqkv[:, :], K.w["wqkv2"][:, :], K.w["ln1"][:, 0:1], None, ALU.mult))
                link(nc.vector.tensor_scalar(w1[:, :], K.w["w1_2"][:, :], K.w["ln2"][:, 0:1], None, ALU.mult))
                link(nc.vector.memset(vx[:, :, :, HD:W], 1.0))
                tell("folded")
                v.wait_ge(event["sines"], 2)
                link(nc.vector.tensor_copy(tab[:, 0:4, 0:8], cs[:, :, :]))
                link(nc.vector.tensor_copy(tab[:, 4:NB, 0:8], bc(cs[:, 3:4, :], [P, NB - 4, 8])))
                link(nc.vector.tensor_copy(tab[:, :, 8:9], wr[:, :].unsqueeze(2)))
                tell("table")
                v.wait_ge(event["gathered"], 1)
                link(nc.vector.tensor_copy(xsT[:, :, :], by_group(K.J[:, 0, :])))
                tell("xsT")
                v.wait_ge(event["half_masked"], 1)
                link(nc.vector.tensor_copy(half[:, :, :], K.S[:, 1, :].rearrange("p (b s) -> p b s", b=NB)))
                tell("mask_rows")
                v.wait_ge(event["turned_back"], 1)
                link(nc.vector.tensor_copy(xs[:, :, :], by_group(K.T[:, 0, :])))
                link(nc.vector.tensor_copy(tabs[:, :, :], K.T[:, 1, 0:NG * RC].rearrange("p (g r) -> p g r", g=NG)))
                link(nc.vector.tensor_tensor(sq[:, :, :], xs[:, :, :], xs[:, :, :], ALU.mult))
                link(nc.vector.tensor_reduce(ms[:, :], sq[:, :, :], AX.X, ALU.add))
                link(nc.vector.tensor_scalar(ms[:, :], ms[:, :], 1.0 / D, 1e-6, ALU.mult, ALU.add))
                tell("ms1")
                v.wait_ge(event["masked"], 1)
                link(nc.vector.tensor_tensor(madd[:, :, :], by_group(K.J[:, 1, :]), bc(K.w["block"][:, :].unsqueeze(1), [P, NG, P]), ALU.mult))
                link(nc.vector.tensor_tensor(madd[:, :, :], madd[:, :, :], bc(K.w["off_block"][:, :].unsqueeze(1), [P, NG, P]), ALU.add))
                v.wait_ge(event["qkv_scaled"], NG)
                for g in range(NG):
                    qk = qkv[:, g, 0:2 * D].rearrange("p (h d) -> p h d", d=HD)
                    lo, hi = qk[:, :, 0:4], qk[:, :, 4:8]
                    cos = bc(tabs[:, g, 0:4].unsqueeze(1), [P, 2 * H, 4])
                    sin = bc(tabs[:, g, 4:8].unsqueeze(1), [P, 2 * H, 4])
                    link(nc.vector.tensor_tensor(part[:, g], hi, sin, ALU.mult))
                    link(nc.vector.tensor_tensor(rope[:, g, :, 0:4], lo, cos, ALU.mult))
                    link(nc.vector.tensor_tensor(rope[:, g, :, 0:4], rope[:, g, :, 0:4], part[:, g], ALU.subtract))
                    link(nc.vector.tensor_tensor(part[:, g], lo, sin, ALU.mult))
                    link(nc.vector.tensor_tensor(rope[:, g, :, 4:8], hi, cos, ALU.mult))
                    link(nc.vector.tensor_tensor(rope[:, g, :, 4:8], rope[:, g, :, 4:8], part[:, g], ALU.add))
                    link(nc.vector.tensor_copy(vx[:, g, :, 0:HD], qkv[:, g, 2 * D:3 * D].rearrange("p (h d) -> p h d", d=HD)))
                tell("roped")
                for kind, g, h in sched:
                    u = 4 * g + h
                    s = u % 2
                    if kind == "S":
                        v.wait_ge(a.scores_ready, done(u + 1))
                        v.wait_ge(a.exp_ready, done(u - 1))
                        nc.vector.scalar_tensor_tensor(out=B.shift[:, s, :, :], in0=K.S[:, s, :].rearrange("p (h k) -> p h k", h=4),
                                                       scalar=float(HD) ** -0.5, in1=bc(madd[:, g, :].unsqueeze(1), [P, 4, P]),
                                                       op0=ALU.mult, op1=ALU.add).then_inc(a.max_ready, 1)
                        v.wait_ge(a.max_ready, done(2 * u + 1))
                        nc.vector.tensor_reduce(B.max[:, s, :], B.shift[:, s, :, :], AX.X, ALU.max).then_inc(a.max_ready, 1)
                        v.wait_ge(a.max_ready, done(2 * u + 2))
                        nc.vector.tensor_tensor(B.shift[:, s, :, :], B.shift[:, s, :, :],
                                                bc(B.max[:, s, :].unsqueeze(2), [P, 4, P]), ALU.subtract).then_inc(a.shifted, 1)
                    elif kind == "V":
                        dve_norm(nc, K, v, a, B, 0, g, h, attn[:, g, 32 * h:32 * h + 32].rearrange("p (h d) -> p h d", h=4), W)
                v.wait_ge(event["attn_projected"], 1)
                link(nc.vector.tensor_tensor(xs[:, :, :], xs[:, :, :], by_group(K.J[:, 1, :]), ALU.add))
                link(nc.vector.tensor_tensor(sq[:, :, :], xs[:, :, :], xs[:, :, :], ALU.mult))
                link(nc.vector.tensor_reduce(ms[:, :], sq[:, :, :], AX.X, ALU.add))
                link(nc.vector.tensor_scalar(ms[:, :], ms[:, :], 1.0 / D, 1e-6, ALU.mult, ALU.add))
                tell("ms2")
                v.wait_ge(event["rs2"], 1)
                link(nc.vector.tensor_tensor(sq[:, :, :], xs[:, :, :], bc(rs[:, :].unsqueeze(2), [P, NG, D]), ALU.mult))
                tell("x1n")
                v.wait_ge(event["y"], 1)
                link(nc.vector.tensor_tensor(xs[:, :, :], xs[:, :, :], by_group(K.O[:, 0, :]), ALU.add))
                link(nc.vector.tensor_tensor(xs[:, :, :], xs[:, :, :], bc(tabs[:, :, 8:9], [P, NG, D]), ALU.mult))
                tell("result")
                v.wait_ge(event["x_kept"], 1)
                for t in range(TURNS4):
                    to = K.x[:, G4 * t:G4 * t + G4, :]
                    v.wait_ge(scattered, done(t + 1))
                    nc.vector.scalar_tensor_tensor(out=to, in0=K.S[:, t % 2, :].rearrange("p (j d) -> p j d", j=G4),
                                                   scalar=K.tg[:, 6:7], in1=to, op0=ALU.mult, op1=ALU.add).then_inc(x_done, 1)
                    v.wait_ge(x_done, done(t + 1))
                    for j in range(G4):
                        nc.vector.bn_stats(K.st6[:, G4 * t + j, :], K.x[:, G4 * t + j, :])


def layer3_attention(nc, K, A):
    H, HD = 16, 8
    W = HD + 1
    with ExitStack() as c:
        def sb(name, shape, dt=F32):
            return c.enter_context(nc.sbuf_tensor(f"l3_{name}", shape, dt))

        def sem(name):
            return c.enter_context(nc.semaphore(f"l3_{name}"))

        a = Attention(nc, c, "l3", 4, 2, 2, (("x", -4), ("f", 5)), ("x",))
        B = attn_buffers(nc, c, "l3")
        kT = sb("kT", [P, 2, P])
        kz = sb("kz", [P, 2, H, P])
        vx = sb("vx", [P, 2, H, W])
        xn = sb("xn", [P, 2, D])
        qT = sb("qT", [P, 2, P])
        upd = sb("upd", [P, 2, D])
        kbias_rows = sb("kbias_rows", [3, NB * P], BF16)
        keys_loaded = [sem(f"keys_loaded{k}") for k in range(2)]
        bias_moved = sem("bias_moved")
        ones_set = sem("ones_set")
        keys_ready = sem("keys_ready")
        values_ready = sem("values_ready")

        with nc.Block() as block:
            @block.sync
            def _(sp):
                for i in range(3):
                    sp.dma_start(kbias_rows[i:i + 1, :].rearrange("o (b k) -> o b k", b=NB), K.part32[:, i, :])\
                        .then_inc(bias_moved, 16)
                with sp.Fori(0, TURNS2) as it:
                    for k in range(2):
                        sp.wait_ge(keys_ready, done(2 * it + k - 1))
                        sp.dma_start(kT[:, k, :], A["ctxT"].rearrange("b (c p) t -> p b c t", p=P)[:, 2 * it + k, 0, :])\
                            .then_inc(keys_loaded[k], 16)
                sp.wait_ge(bias_moved, 48)

            @block.tensor
            def _(pe):
                start_counts(pe, [a.scores_ready, a.turned, a.summed, *a.j_ready.values()])
                pe.wait_ge(bias_moved, 48)

                def step_of(it, step):
                    kind, k = step[0], step[1]
                    b = 2 * it + k
                    if kind == "x":
                        a.wait_bank(pe, it, kind, k)
                        pe.wait_ge(a.xn_ready, done(b + 1))
                        nc.tensor.transpose(K.J[:, a.j_bank(kind, k), 0:P], xn[:, k, :], K.w["ident"][:, :]).then_inc(a.j_ready[kind], 1)
                    elif kind == "S":
                        g = step[2]
                        u = a.unit(it, k, g)
                        s = g % 2
                        if g == 0:
                            pe.wait_ge(a.copied["x"], done(b + 1))
                            pe.wait_ge(keys_ready, done(b + 1))
                        pe.wait_ge(a.shifted, done(u - 1))
                        bias = bc(kbias_rows[0:3, bass.ds(b * P, P)].unsqueeze(1), [3, 4, P])
                        nc.tensor.matmul(K.S[:, s, :], qT[:, k, :], kz[:, k, 4 * g:4 * g + 4, :], start=True, stop=False)
                        nc.tensor.matmul(K.S[:, s, :], K.ones_bf[0:3, :], bias, start=False, stop=True)\
                            .then_inc(a.scores_ready, 1)
                    elif kind == "T":
                        pe_turn(nc, K, pe, a, B, it, k, step[2])
                    elif kind == "V":
                        g = step[2]
                        if g == 0:
                            pe.wait_ge(values_ready, done(b + 1))
                        pe_values(nc, K, pe, a, B, it, k, g, lambda h: vx[:, k, 4 * g + h, :], W)
                a.run(pe, step_of)

            @block.vector
            def _(v):
                start_counts(v, [a.max_ready, a.shifted, a.recip_ready, a.normed, a.x_done])
                nc.vector.memset(vx[:, :, :, HD:W], 1.0).then_inc(ones_set, 1)
                ln_statistics(nc, K, v, a.ln_chain)

                def step_of(it, step):
                    kind, k = step[0], step[1]
                    b = 2 * it + k
                    if kind == "S":
                        dve_shift(nc, K, v, a, B, it, k, step[2])
                    elif kind == "V":
                        g = step[2]
                        dve_norm(nc, K, v, a, B, it, k, g,
                                 upd[:, k, 32 * g:32 * g + 32].rearrange("p (h d) -> p h d", h=4), W)
                    elif kind == "f":
                        v.wait_ge(a.normed, done(a.unit(it, k, 3) + 1))
                        nc.vector.scalar_tensor_tensor(out=K.x[:, b, :], in0=upd[:, k, :], scalar=K.tg[:, 3:4],
                                                       in1=K.x[:, b, :], op0=ALU.mult, op1=ALU.add).then_inc(a.x_done, 1)
                        v.wait_ge(a.x_done, done(b + 1))
                        nc.vector.bn_stats(K.st6[:, b, :], K.x[:, b, :])
                a.run(v, step_of)

            @block.scalar
            def _(act):
                start_counts(act, [a.exp_ready, a.turned_copied, a.copied["x"]])

                def step_of(it, step):
                    kind, k = step[0], step[1]
                    b = 2 * it + k
                    if kind == "x":
                        act.wait_ge(a.j_ready[kind], done(b + 1))
                        act.wait_ge(a.scores_ready, done(a.unit(it, k, 3) + 1 - a.units))
                        nc.scalar.mul(qT[:, k, :], K.J[:, a.j_bank(kind, k), 0:P], float(HD) ** -0.5).then_inc(a.copied["x"], 1)
                    elif kind == "S":
                        act_exp(nc, K, act, a, B, it, k, step[2], 1.0)
                    elif kind == "T":
                        act_copy_turned(nc, K, act, a, B, it, k, step[2])
                a.run(act, step_of, copies_first=True)

            @block.gpsimd
            def _(pool):
                start_counts(pool, [a.centred_ready, a.xn_ready, keys_ready, values_ready])
                pool_rstd(nc, K, pool, a.ln_chain, a.rstd_ready)
                pool.wait_ge(a.rstd_ready, 1)
                pool.wait_ge(ones_set, 1)
                pool_normalise(nc, K, pool, a, xn, 0, 0)

                def keys_values_rows(it, k):
                    b = 2 * it + k
                    pool.wait_ge(keys_loaded[k], 16 * it + 16)
                    pool.wait_ge(a.scores_ready, done(a.unit(it, k, 3) + 1 - a.units))
                    nc.gpsimd.tensor_tensor(kz[:, k, :, :], bc(kT[:, k, :].unsqueeze(1), [P, H, P]),
                                            bc(K.w["head8"][:, :].unsqueeze(2), [P, H, P]), ALU.mult).then_inc(keys_ready, 1)
                    pool.wait_ge(a.summed, done(a.unit(it, k, 3) + 1 - a.units))
                    nc.gpsimd.tensor_copy(vx[:, k, :, 0:HD], K.w["ctx"][:, b, D:DC].rearrange("p (h d) -> p h d", h=H))\
                        .then_inc(values_ready, 1)
                    if not (isinstance(b, int) and b == NB - 1):
                        pool_normalise(nc, K, pool, a, xn, b + 1, k + 1)
                with pool.Fori(0, a.turns - 1) as it:
                    for k in range(2):
                        keys_values_rows(it, k)
                for k in range(2):
                    keys_values_rows(a.turns - 1, k)


def layer3_ffn(nc, K, A, out):
    CH = 4
    with ExitStack() as c:
        def sb(name, shape, dt=F32):
            return c.enter_context(nc.sbuf_tensor(f"f3_{name}", shape, dt))

        def sem(name):
            return c.enter_context(nc.semaphore(f"f3_{name}"))

        xn = sb("xn", [P, G4, D])
        xnT = sb("xnT", [P, G4 * P])
        hidden = sb("hidden", [P, 2, G4 * P])
        w_con = sb("w_con", [P, CH, D])
        h_bias = sb("h_bias", [P, CH])
        y_bias = sb("y_bias", [1, D])
        ln_chain = sem("ln_chain")
        rstd_ready = sem("rstd_ready")
        xn_ready = sem("xn_ready")
        xn_used = sem("xn_used")
        xnT_ready = sem("xnT_ready")
        folded = sem("folded")
        prepared = sem("prepared")
        h_ready = sem("h_ready")
        gelu_ready = sem("gelu_ready")
        y_ready = sem("y_ready")
        x_done = sem("x_done")
        stored = sem("stored")

        with nc.Block() as block:
            @block.sync
            def _(sp):
                with sp.Fori(0, TURNS4) as it:
                    sp.wait_ge(x_done, done(it + 1))
                    sp.dma_start(out.rearrange("b t f -> t b f")[:, bass.ds(G4 * it, G4), :], K.x[:, bass.ds(G4 * it, G4), :])\
                        .then_inc(stored, 16)
                sp.wait_ge(stored, 16 * TURNS4)

            @block.gpsimd
            def _(pool):
                start_counts(pool, [rstd_ready])
                pool.wait_ge(ln_chain, 7)
                with pool.Fori(0, TURNS4) as it:
                    pool_rstd4(nc, K, it, rstd_ready)

            @block.tensor
            def _(pe):
                start_counts(pe, [xn_used, h_ready, y_ready])
                for ch in range(CH):
                    nc.tensor.transpose(K.O[:, 0, ch * P:(ch + 1) * P], K.w["down_rows"][:, 0, ch * P:(ch + 1) * P], K.w["ident"][:, :])
                for ch in range(CH):
                    m = nc.tensor.matmul(K.O[:, 1, ch:ch + 1], K.w["up_rows"][0:1, 1, ch * P:(ch + 1) * P], K.ones_row[0:1, 0:1],
                                         start=True, stop=True)
                m.then_inc(folded, 1)
                pe.wait_ge(prepared, 3)
                with pe.Fori(0, TURNS4) as it:
                    pe.wait_ge(xn_ready, done(it + 1))
                    pe.wait_ge(xnT_ready, done(it))
                    for j in range(G4):
                        m = nc.tensor.transpose(K.T[:, 0, j * P:(j + 1) * P], xn[:, j, :], K.w["ident"][:, :])
                    m.then_inc(xn_used, 1)

                    def first(ch):
                        pe.wait_ge(gelu_ready, done(CH * it + ch - 1))
                        nc.tensor.matmul(K.S[:, ch % 2, :], K.w["up_rows"][:, 0, ch * P:(ch + 1) * P], xnT[:, :],
                                         start=True, stop=True).then_inc(h_ready, 1)
                    pe.wait_ge(xnT_ready, done(it + 1))
                    first(0)
                    first(1)
                    pe.wait_ge(x_done, done(it))
                    for ch in range(CH):
                        pe.wait_ge(gelu_ready, done(CH * it + ch + 1))
                        for j in range(G4):
                            m = nc.tensor.matmul(K.J[:, 0, j * P:(j + 1) * P], hidden[:, ch % 2, j * P:(j + 1) * P],
                                                 w_con[:, ch, :], start=(ch == 0 and j == 0), stop=False, skip_group_check=True)
                        if ch == CH - 1:
                            for j in range(G4):
                                m = nc.tensor.matmul(K.J[:, 0, j * P:(j + 1) * P], K.ones_row[0:1, :], y_bias[0:1, :],
                                                     start=False, stop=True, skip_group_check=True)
                        m.then_inc(y_ready, 1)
                        if ch + 2 < CH:
                            first(ch + 2)

            @block.scalar
            def _(act):
                start_counts(act, [xnT_ready, gelu_ready])
                act.wait_ge(prepared, 3)
                with act.Fori(0, TURNS4) as it:
                    act.wait_ge(xn_used, done(it + 1))
                    act.wait_ge(h_ready, done(CH * it))
                    nc.scalar.copy(xnT[:, :], K.T[:, 0, :]).then_inc(xnT_ready, 1)
                    for ch in range(CH):
                        act.wait_ge(h_ready, done(CH * it + ch + 1))
                        act.wait_ge(y_ready, done(CH * it + ch - 1))
                        nc.scalar.activation(hidden[:, ch % 2, :], K.S[:, ch % 2, :], ACT.Gelu, bias=h_bias[:, ch:ch + 1])\
                            .then_inc(gelu_ready, 1)

            @block.vector
            def _(v):
                ln_statistics(nc, K, v, ln_chain)
                start_counts(v, [xn_ready, x_done])
                v.wait_ge(folded, 1)
                nc.vector.tensor_copy(w_con[:, :, :], K.O[:, 0, :].rearrange("p (c d) -> p c d", c=CH)).then_inc(prepared, 1)
                nc.vector.tensor_tensor(h_bias[:, :], K.O[:, 1, 0:CH], K.w["up_bias"][:, :], ALU.add).then_inc(prepared, 1)
                nc.vector.tensor_tensor(y_bias[0:1, :], K.w["b_con"][0:1, :], K.w["down_bias"][0:1, :], ALU.add).then_inc(prepared, 1)
                with v.Fori(0, TURNS4) as it:
                    normalise4(nc, K, v, it, xn, rstd_ready, xn_ready, xn_used)
                    v.wait_ge(y_ready, done(CH * (it + 1)))
                    xs = K.x[:, bass.ds(G4 * it, G4), :]
                    nc.vector.scalar_tensor_tensor(out=xs, in0=K.J[:, 0, :].rearrange("p (j d) -> p j d", j=G4),
                                                   scalar=K.tg[:, 7:8], in1=xs, op0=ALU.mult, op1=ALU.add).then_inc(x_done, 1)




WEIGHTS = [
    [("ident", [P, P], "c_ident", None, False),
     ("head16", [P, 8], "c_head16", None, False),
     ("w_src", [P, 2, DC], "w_srcT", "(c p) o -> p c o", False),
     ("w_tgt", [P, P], "w_tgtT", None, False),
     ("w_out0", [P, 2, P], "w_out0T", "(c p) o -> p c o", False),
     ("b_srck", [P, 1], "b_srck", None, False),
     ("b_srcv", [1, P], "b_srcv", None, False),
     ("b_tgt", [P, 1], "b_tgt", None, False),
     ("b_out0", [1, P], "b_out0", None, False)],
    [("w_gate", [P, 8], "L0_ffn_W_gate", None, False),
     ("b_gate", [1, 8], "b_gate", None, False),
     ("w1_0", [P, 8, P], "W1T", None, False),
     ("w2_0", [P, 8, P], "W2T", None, False),
     ("b1_0", [P, 8], "b1T", None, False),
     ("b2_0", [8, P], "L0_ffn_b2", None, False),
     ("before8", [P, 8, 8], "c_before8", None, True)],
    [("w_in", [P, P], "w_inT", None, False),
     ("g_res", [P, 1], "g_res", None, False),
     ("b_in", [1, P], "b_in", None, False),
     ("g_init", [P, P], "g_init", None, True),
     ("upto", [P, P], "c_upto", None, False),
     ("iota_row", [P, P], "c_iota", None, True),
     ("iota_col", [P, 1], "c_iota_col", None, False),
     ("ctx", [P, NB, DC], "ctx_2048", "b p f -> p b f", False)],
    [("router1", [P, 16], "L1_ffn_router_w", None, False),
     ("wg1", [P, 5, P], "wg1", None, False),
     ("wu1", [P, 5, P], "wu1", None, False),
     ("wd1", [P, 5, P], "wd1", None, False),
     ("spread", [16, 4, P], "c_spread", None, False),
     ("before16", [P, 16, 16], "c_before16", None, True)],
    [("wq2", [P, 8, P], "wq2", None, False),
     ("wkv2", [P, 2, 2048], "L2_xattn_Wkv", "(c p) o -> p c o", False),
     ("wout2", [P, 8, P], "L2_xattn_Wout", "(c p) o -> p c o", False),
     ("nullk", [P, 1], "nullk", None, False),
     ("nullv", [P, 1], "nullv", None, False),
     ("nullv_row", [P, 64], "nullv_row", None, True),
     ("ln_scale", [P, P], "ln_scale", None, True),
     ("ln_bias", [P, P], "ln_bias", None, True)],
    [("router2", [P, P], "router2", None, True),
     ("router2_b", [P, 1], "router2_b", None, True),
     ("before128", [P, P], "c_before128", None, False),
     ("slots", [P, SEL], "c_slots", None, True),
     ("inv_freq", [P, 4], "c_inv_freq", None, True),
     ("block", [P, P], "c_block", None, False),
     ("off_block", [P, P], "c_off_block", None, False),
     ("eye8", [P, 8, 8], "c_eye8", None, True),
     ("head8", [P, 16], "c_head8", None, False),
     ("wqkv2", [P, 3 * P], "wqkv2", None, False),
     ("ln1", [P, 1], "ln1", None, False),
     ("ln2", [P, 1], "ln2", None, False),
     ("wo2", [P, P], "L2_ffn_wo", None, False),
     ("w1_2", [P, 512], "L2_ffn_w1", None, False),
     ("w2_2", [P, 4, P], "L2_ffn_w2", "(c p) o -> p c o", False)],
    [],
    [("up_rows", [P, 2, 512], "up_rows", None, False),
     ("up_bias", [P, 4], "up_bias", None, False),
     ("b_con", [1, P], "b_con", None, False),
     ("down_bias", [1, P], "down_bias", None, False),
     ("down_rows", [P, 1, 512], "down_rows", None, False)],
]


def clear_semaphores(nc):
    free = sorted(int(s) for s in nc.released_uncleared_semaphores)
    with nc.Block() as block:
        @block.gpsimd
        def _(pool):
            first = free[0]
            for i, s in enumerate(free):
                if i + 1 == len(free) or free[i + 1] != s + 1:
                    pool.sem_clear(range(first, s + 1))
                    if i + 1 < len(free):
                        first = free[i + 1]


def program(nc, A, out):
    with ExitStack() as c:
        def sb(name, shape, dt=F32):
            return c.enter_context(nc.sbuf_tensor(name, shape, dt))

        def ps(name):
            return c.enter_context(nc.psum_tensor(name, [P, 2, 512], F32))

        def sem(name):
            return c.enter_context(nc.semaphore(name))

        early = ExitStack()
        short_lived = {name for group in WEIGHTS[:5] for name, *_ in group} - {"ident", "ctx"}
        shapes = {name: shape for group in WEIGHTS for name, shape, *_ in group}
        weights = {name: sb("w_" + name, shape) for name, shape in shapes.items() if name not in short_lived}
        K = Buffers()
        K.x, K.st6 = sb("x", [P, NB, D]), sb("st6", [P, NB, 6])
        K.mean, K.var, K.rstd = sb("mean", [P, NB]), sb("var", [P, NB]), sb("rstd", [P, NB])
        K.lna, K.lnb = sb("lna", [P, NB]), sb("lnb", [P, NB])
        K.tg, K.neg_half = sb("tg", [P, 8]), sb("neg_half", [P, NB])
        K.ones_row, K.ones_bf, K.ones_f = sb("ones_row", [1, P]), sb("ones_bf", [P, P], BF16), sb("ones_f", [P, P])
        K.neg32, K.part32 = sb("neg32", [NB, P], BF16), sb("part32", [NB, 3, P], BF16)
        K.S, K.T, K.O, K.J = ps("S"), ps("T"), ps("O"), ps("J")
        K.gates_ready = sem("gates_ready")
        K.w_loaded = [sem(f"weights{i}_loaded") for i in range(len(WEIGHTS))]
        K.w_count = [16 * len(w) for w in WEIGHTS]
        weights.update({name: early.enter_context(nc.sbuf_tensor("w_" + name, shapes[name], F32)) for name in shapes
                        if name in short_lived})
        K.w = weights

        def load_weights(engine):
            for i, group in enumerate(WEIGHTS):
                for name, shape, source, order, spread in group:
                    src = A[source] if not order else A[source].rearrange(order, p=P)
                    if spread:
                        src = bc(src, shape)
                    dst = weights[name]
                    engine.dma_start(dst[tuple(slice(None) for _ in shape)], src).then_inc(K.w_loaded[i], 16)
        K.load_weights = load_weights
        setup_block(nc, K, A)
        layer0_attention(nc, K, A)
        layer0_ffn(nc, K, A)
        layer1_attention(nc, K, A)
        layer1_ffn(nc, K, A)
        clear_semaphores(nc)
        layer2_attention(nc, K, A)
        early.close()
        clear_semaphores(nc)
        layer2_ffn(nc, K, A)
        layer3_attention(nc, K, A)
        layer3_ffn(nc, K, A, out)




def laid_out(inputs):
    import numpy as np
    f = {n: np.asarray(v) for n, v in inputs.items()}
    d = {}
    for n in ("x", "g_xattn", "g_ffn", "mask_BxS2_fk1", "itok_Bx1_68_817", "L3_xattn_b"):
        d[n] = f[n]
    ctx = f["ctx_2048"]
    d["ctxT"] = ctx.transpose(0, 2, 1)
    d["maskT"] = f["mask_BxS2_fk1"].T
    d["w_srcT"] = f["L0_xattn_W_src"].T
    d["w_tgtT"] = f["L0_xattn_W_tgt"].T
    d["w_out0T"] = f["L0_xattn_W_out"].T
    d["b_srck"] = f["L0_xattn_b_src"][:D, None]
    d["b_srcv"] = f["L0_xattn_b_src"][None, D:]
    d["b_tgt"] = f["L0_xattn_b_tgt"][:, None]
    d["b_out0"] = f["L0_xattn_b_out"][None, :]
    d["L0_ffn_W_gate"] = f["L0_ffn_W_gate"]
    d["b_gate"] = f["L0_ffn_b_gate"][None, :]
    d["W1T"] = f["L0_ffn_W1"].transpose(1, 0, 2)
    d["W2T"] = f["L0_ffn_W2"].transpose(1, 0, 2)
    d["b1T"] = f["L0_ffn_b1"].T
    d["L0_ffn_b2"] = f["L0_ffn_b2"]
    before = lambda n: (np.arange(n)[None, :] < np.arange(n)[:, None]).astype(np.float32)[None]
    d["c_before8"] = before(8)
    d["up_w"] = f["L3_ffn_up_weights"].transpose(0, 2, 3, 1)[None]
    d["up_rows"] = np.concatenate([f["L3_ffn_W_exp"][:, None, :], np.broadcast_to(f["L3_ffn_b_exp"], (P, 1, 512))], axis=1)
    d["w_inT"] = f["L1_xattn_W_in"].T
    d["g_res"] = f["L1_xattn_g_res"][:, None]
    d["b_in"] = f["L1_xattn_b_in"][None, :]
    d["g_init"] = f["L1_xattn_g_init"][None, :D]
    d["ctx_2048"] = ctx
    d["lensT"] = f["mask_BxS2_if0"].T
    d["c_upto"] = (np.arange(P)[:, None] <= np.arange(P)[None, :]).astype(np.float32)
    d["c_iota_col"] = np.arange(P, dtype=np.float32)[:, None]
    d["L1_ffn_router_w"] = f["L1_ffn_router_w"]
    for g in "gu":
        shared, routed = f[f"L1_ffn_w{g}_s"], f[f"L1_ffn_w{g}_r"]
        d[f"w{g}1"] = np.concatenate([shared.transpose(1, 0, 2).reshape(P, 1, P),
                                      routed.transpose(1, 0, 2).reshape(P, 4, P)], axis=1)
    d["wd1"] = np.concatenate([f["L1_ffn_wd_s"].reshape(1, P, P), f["L1_ffn_wd_r"].reshape(4, P, P)]).transpose(1, 0, 2)
    d["c_spread"] = (np.arange(16)[:, None, None] == 4 * np.arange(4)[None, :, None] + np.arange(P)[None, None, :] // 32)\
        .astype(np.float32)
    d["c_before16"] = before(16)
    d["down_w"] = f["L3_ffn_down_weights"].transpose(0, 2, 3, 1)[None]
    d["down_rows"] = f["L3_ffn_W_con"].T[:, None, :]
    d["wq2"] = f["L2_xattn_Wq"].reshape(P, 8, P)
    d["L2_xattn_Wkv"] = f["L2_xattn_Wkv"]
    d["L2_xattn_Wout"] = f["L2_xattn_Wout"]
    null = f["L2_xattn_null_kv"]
    d["nullk"] = np.concatenate([null[0], null[0]])[:, None]
    d["nullv"] = np.concatenate([null[1], null[1]])[:, None]
    d["nullv_row"] = null[1:2]
    d["ln_scale"] = f["L2_xattn_ln_scale"][None]
    d["ln_bias"] = f["L2_xattn_ln_bias"][None]
    d["c_head8"] = (np.arange(P)[:, None] // 8 == np.arange(16)[None, :]).astype(np.float32)
    d["up_bias"] = f["L3_ffn_up_bias"].reshape(4, P).T
    d["b_con"] = f["L3_ffn_b_con"][None]
    d["down_bias"] = f["L3_ffn_down_bias"][None]
    d["router2"] = f["L2_ffn_router_w"].T
    d["router2_b"] = f["L2_ffn_router_b"][None]
    d["wqkv2"] = np.concatenate([f["L2_ffn_wq"], f["L2_ffn_wk"], f["L2_ffn_wv"]], axis=1)
    d["ln1"], d["ln2"] = f["L2_ffn_ln1"][:, None], f["L2_ffn_ln2"][:, None]
    for n in ("L2_ffn_wo", "L2_ffn_w1", "L2_ffn_w2", "L2_ffn_attention_mask"):
        d[n] = f[n]
    d["posT"] = f["L2_ffn_position_ids"][:, :P].T
    d["c_before128"] = before(P)[0]
    d["c_slots"] = np.array([list(range(KEEP)) + [-1]], np.float32)
    d["c_inv_freq"] = (np.float32(1.0) / np.float32(10000.0) ** (np.arange(0, 8, 2, dtype=np.float32) / np.float32(8)))\
        .astype(np.float32)[None]
    row = np.arange(P)
    own = (row[:, None] // SEL == row[None, :] // SEL) & (row[None, :] % SEL != SEL - 1)
    d["c_block"] = own.astype(np.float32)
    d["c_off_block"] = np.where(own, 0.0, -BIG).astype(np.float32)
    d["c_eye8"] = np.eye(8, dtype=np.float32)[None]
    d["c_iota"] = np.arange(P, dtype=np.float32)[None, :]
    d["c_ident"] = np.eye(P, dtype=np.float32)
    d["c_head16"] = (np.arange(P)[:, None] // 16 == np.arange(8)[None, :]).astype(np.float32)
    return {n: np.ascontiguousarray(v) for n, v in d.items()}


def kernel(**inputs):
    import concourse.bacc as _bacc
    from concourse import mybir as _mybir
    from concourse.bass_utils import run_bass_kernel_spmd as _run

    nc = _bacc.Bacc("TRN2", target_bir_lowering=False, num_devices=1)
    arrays, A = {}, {}
    for name, a in laid_out(inputs).items():
        arrays[f"in_{name}"] = a
        A[name] = nc.dram_tensor(f"in_{name}", a.shape, _mybir.dt.from_np(a.dtype), kind="ExternalInput").ap()
    out = nc.dram_tensor("out_0", (NB, P, D), _mybir.dt.float32, kind="ExternalOutput").ap()
    program(nc, A, out)
    r = _run(nc, [arrays], core_ids=[0])
    return r.results[0]["out_0"]
```

```python
from contextlib import ExitStack

import concourse.bass as bass
from concourse import mybir

F32 = mybir.dt.float32
BF16 = mybir.dt.bfloat16
I32 = mybir.dt.int32
U32 = mybir.dt.uint32
ALU = mybir.AluOpType
ACT = mybir.ActivationFunctionType
AX = mybir.AxisListType

P = 128
NB = 32
D = 128
DC = 256
G4 = 4
TURNS4 = NB // G4
TURNS2 = NB // 2
EPS_LN = 1e-5
BIG = 1e30
BASE = 9
EXPERTS0 = 8
EXPERTS1 = 16
SEL = 16
KEEP = 15


def done(n):
    return n + BASE


def bc(ap, shape):
    return ap.broadcast_to(shape)


def setup_block(nc, K, A):
    with ExitStack() as c:
        def sb(name, shape, dt=F32):
            return c.enter_context(nc.sbuf_tensor(name, shape, dt))

        def sem(name):
            return c.enter_context(nc.semaphore(name))

        gates = sb("gates", [P, 8])
        mask32 = sb("mask32", [NB, P])
        len32i = sb("len32i", [NB, 1], I32)
        len32 = sb("len32", [NB, 1])
        iota32 = sb("iota32", [NB, P])
        kb32 = sb("kb32", [NB, P])
        sum32 = sb("sum32", [NB, P])
        rest32 = sb("rest32", [NB, P])
        lens_i = sb("lens_i", [P, NB], I32)
        lens = sb("lens", [P, NB])
        upto = sb("upto", [P, P])
        iota_row = sb("iota_row", [P, P])
        ends = sb("ends", [P, NB])
        wrap = sb("wrap", [P, NB])
        ends_hot = sb("ends_hot", [P, NB, P], BF16)
        x_loaded = [sem(f"x_loaded{i}") for i in range(4)]
        small_loaded = sem("small_loaded")
        chain = sem("setup_chain")
        lens_loaded = sem("lens_loaded")
        lens_ready = sem("lens_ready")
        ends_hot_ready = sem("ends_hot_ready")
        marks_ready = sem("marks_ready")
        counted = sem("counted")

        with nc.Block() as block:
            @block.sync
            def _(sp):
                sp.dma_start(gates[:, 0:4], bc(A["g_xattn"].rearrange("(o g) -> o g", o=1), [P, 4])).then_inc(small_loaded, 16)
                sp.dma_start(gates[:, 4:8], bc(A["g_ffn"].rearrange("(o g) -> o g", o=1), [P, 4])).then_inc(small_loaded, 16)
                sp.dma_start(mask32[:, :], A["mask_BxS2_fk1"]).then_inc(small_loaded, 16)
                sp.dma_start(len32i[:, :], A["itok_Bx1_68_817"]).then_inc(small_loaded, 16)
                sp.dma_start(iota32[:, :], bc(A["c_iota"], [NB, P])).then_inc(small_loaded, 16)
                sp.dma_start(kb32[:, :], bc(A["L3_xattn_b"].rearrange("(o k) -> o k", o=1), [NB, P])).then_inc(small_loaded, 16)
                sp.dma_start(lens_i[:, :], A["lensT"]).then_inc(lens_loaded, 16)
                sp.dma_start(upto[:, :], A["c_upto"]).then_inc(lens_loaded, 16)
                sp.dma_start(iota_row[:, :], bc(A["c_iota"], [P, P])).then_inc(lens_loaded, 16)
                xv = A["x"].rearrange("b t f -> t b f")
                for i in range(4):
                    sp.dma_start(K.x[:, 8 * i:8 * i + 8, :], xv[:, 8 * i:8 * i + 8, :]).then_inc(x_loaded[i], 16)

            @block.scalar
            def _(act):
                K.load_weights(act, 0)
                act.wait_ge(small_loaded, 96)
                nc.scalar.activation(K.tg[:, :], gates[:, :], ACT.Tanh).then_inc(K.gates_ready, 1)

            @block.vector
            def _(v):
                n = [0]

                def link(ins):
                    n[0] += 1
                    ins.then_inc(chain, 1)
                    v.wait_ge(chain, n[0])
                nc.vector.memset(K.ones_row[:, :], 1.0)
                nc.vector.memset(K.ones_bf[:, :], 1.0)
                nc.vector.memset(K.ones_f[:, :], 1.0)
                nc.vector.memset(K.neg_half[:, :], -0.5)
                v.wait_ge(small_loaded, 96)
                nc.vector.tensor_scalar(K.neg32[:, :], mask32[:, :], 0.0, -BIG, ALU.is_equal, ALU.mult)
                link(nc.vector.tensor_copy(len32[:, :], len32i[:, :]))
                link(nc.vector.tensor_scalar(rest32[:, :], iota32[:, :], len32[:, 0:1], -1e12, ALU.is_ge, ALU.mult))
                link(nc.vector.tensor_tensor(sum32[:, :], kb32[:, :], rest32[:, :], ALU.add))
                link(nc.vector.tensor_copy(K.part32[:, 0, :], sum32[:, :]))
                link(nc.vector.tensor_tensor(rest32[:, :], sum32[:, :], K.part32[:, 0, :], ALU.subtract))
                link(nc.vector.tensor_copy(K.part32[:, 1, :], rest32[:, :]))
                link(nc.vector.tensor_tensor(sum32[:, :], rest32[:, :], K.part32[:, 1, :], ALU.subtract))
                link(nc.vector.tensor_copy(K.part32[:, 2, :], sum32[:, :]))
                v.wait_ge(lens_loaded, 48)
                nc.vector.tensor_copy(lens[:, :], lens_i[:, :]).then_inc(lens_ready, 1)
                v.wait_ge(counted, 1)
                link(nc.vector.tensor_scalar(ends[:, :], K.J[:, 0, 0:NB], -1.0, None, ALU.add))
                link(nc.vector.tensor_scalar(wrap[:, :], ends[:, :], 0.0, float(P), ALU.is_lt, ALU.mult))
                link(nc.vector.tensor_tensor(ends[:, :], ends[:, :], wrap[:, :], ALU.add))
                nc.vector.tensor_tensor(ends_hot[:, :, :], bc(iota_row[:, :].unsqueeze(1), [P, NB, P]),
                                        bc(ends[:, :].unsqueeze(2), [P, NB, P]), ALU.is_equal).then_inc(ends_hot_ready, 1)
                for i in range(4):
                    v.wait_ge(x_loaded[i], 16)
                    for b in range(8 * i, 8 * i + 8):
                        nc.vector.bn_stats(K.st6[:, b, :], K.x[:, b, :])
                v.wait_ge(counted, 2)
                nc.vector.tensor_scalar(ends[:, :], K.J[:, 1, 0:NB], 1.0, None, ALU.min).then_inc(marks_ready, 1)
                v.wait_ge(counted, 3)
                link(nc.vector.tensor_scalar(K.plug[:, :], K.J[:, 0, 0:NB], -1.0, 0.0, ALU.add, ALU.max))
                link(nc.vector.tensor_scalar(K.plug[:, :], K.plug[:, :], float(P - 1), None, ALU.min))

            @block.tensor
            def _(pe):
                pe.wait_ge(lens_ready, 1)
                nc.tensor.matmul(K.J[:, 0, 0:NB], upto[:, :], lens[:, :], start=True, stop=True).then_inc(counted, 1)
                pe.wait_ge(ends_hot_ready, 1)
                for b in range(NB):
                    m = nc.tensor.matmul(K.J[:, 1, b:b + 1], ends_hot[:, b, :], K.ones_bf[:, 0:1], start=True, stop=True)
                m.then_inc(counted, 1)
                pe.wait_ge(marks_ready, 1)
                nc.tensor.matmul(K.J[:, 0, 0:NB], upto[:, :], ends[:, :], start=True, stop=True).then_inc(counted, 1)


def ln_statistics(nc, K, v, chain):
    even_mean, odd_mean = K.st6[:, :, 1], K.st6[:, :, 4]
    even_m2, odd_m2 = K.st6[:, :, 2], K.st6[:, :, 5]
    a, b2 = K.lna, K.lnb
    nc.vector.tensor_tensor(K.mean[:, :], even_mean, odd_mean, ALU.add).then_inc(chain, 1)
    nc.vector.tensor_tensor(a[:, :], even_mean, odd_mean, ALU.subtract).then_inc(chain, 1)
    nc.vector.tensor_tensor(b2[:, :], even_m2, odd_m2, ALU.add).then_inc(chain, 1)
    v.wait_ge(chain, 3)
    nc.vector.tensor_scalar(K.mean[:, :], K.mean[:, :], 0.5, None, ALU.mult).then_inc(chain, 1)
    nc.vector.tensor_tensor(a[:, :], a[:, :], a[:, :], ALU.mult).then_inc(chain, 1)
    nc.vector.tensor_scalar(b2[:, :], b2[:, :], 1.0 / D, EPS_LN, ALU.mult, ALU.add).then_inc(chain, 1)
    v.wait_ge(chain, 6)
    nc.vector.scalar_tensor_tensor(out=K.var[:, :], in0=a[:, :], scalar=0.25, in1=b2[:, :],
                                   op0=ALU.mult, op1=ALU.add).then_inc(chain, 1)
    v.wait_ge(chain, 7)


class Attention:

    def __init__(self, nc, c, tag, groups, seqs, first, extra, psum_steps, shared=()):
        self.groups, self.seqs, self.tag = groups, seqs, tag
        self.units = seqs * groups
        self.turns = NB // seqs
        self.sched, self.copies_first = [], []
        for i in range(first, first + self.units):
            steps, others = [], []
            for kind, j in (("T", i), ("S", i + 2), ("V", i - 1)):
                unit = j % self.units
                steps.append((j // self.units, (kind, unit // groups, unit % groups)))
            for kind, at in extra:
                for k in range(seqs):
                    slot = groups * k + at
                    assert first - self.units <= slot < first + self.units
                    if slot in (i, i - self.units):
                        others.append((int(slot != i), (kind, k)))
            self.sched += steps + others
            self.copies_first += [steps[0], steps[2]] + others + [steps[1]]

        def sem(name):
            return c.enter_context(nc.semaphore(f"{tag}_{name}"))
        self.scores_ready = sem("scores_ready")
        self.max_ready = sem("max_ready")
        self.shifted = sem("shifted")
        self.exp_ready = sem("exp_ready")
        self.turned = sem("turned")
        self.turned_copied = sem("turned_copied")
        self.summed = sem("summed")
        self.recip_ready = sem("recip_ready")
        self.null_ready = sem("null_ready")
        self.weighed = sem("weighed")
        self.normed = sem("normed")
        self.ln_chain = sem("ln_chain")
        self.rstd_ready = sem("rstd_ready")
        self.centred_ready = sem("centred_ready")
        self.xn_ready = sem("xn_ready")
        self.wait_carried = sem("wait_carried")
        self.x_done = sem("x_done")
        self.j_steps = [(ahead, s) for ahead, s in self.sched if s[0] in psum_steps]
        assert len(self.j_steps) % 2 == 0
        self.j_ready = {s: sem(f"ready_{s}") for s in psum_steps}
        self.copied = {s: sem(f"copied_{s}") for s in psum_steps}
        self.shared = shared

    def run(self, engine, step_of, copies_first=False):
        sched = self.copies_first if copies_first else self.sched
        for ahead, step in sched:
            if ahead:
                step_of(0, step)
        with engine.Fori(0, self.turns - 1) as it:
            for ahead, step in sched:
                step_of(it + ahead, step)
        for ahead, step in sched:
            if not ahead:
                step_of(self.turns - 1, step)

    def unit(self, it, k, g):
        return self.units * it + self.groups * k + g

    def j_index(self, kind, k):
        return [s for _, s in self.j_steps].index((kind, k))

    def j_bank(self, kind, k):
        return self.j_index(kind, k) % 2

    def wait_bank(self, pe, it, kind, k):
        n = len(self.j_steps)
        i = self.j_index(kind, k)
        own_ahead = self.j_steps[i][0]
        peeled = isinstance(it, int)
        for back in range(i - 2, i - n - 2, -2):
            ahead0, (kind0, k0) = self.j_steps[back % n]
            turn = it + (ahead0 - own_ahead - (1 if back < 0 else 0))
            if peeled and not 0 <= turn < self.turns:
                continue
            pe.wait_ge(self.copied[kind0], self.copied_at(kind0, self.seqs * turn + k0 + 1))
            if peeled or back >= 0 or ahead0:
                break

    def copied_at(self, kind, n):
        return done((2 if kind in self.shared else 1) * n)


def start_counts(engine, sems):
    for s in sems:
        engine.sem_inc(s, BASE)


class Buffers:
    pass


def attn_buffers(nc, c, tag):
    def sb(name, shape, dt=F32):
        return c.enter_context(nc.sbuf_tensor(f"{tag}_{name}", shape, dt))
    B = Buffers()
    B.shift = sb("shift", [P, 2, 4])
    B.exp = sb("exp", [P, 2, 4, P])
    B.expT = sb("expT", [P, 2, 4, P])
    B.max = sb("max", [P, 2, 4])
    B.rec = sb("rec", [P, 2, 4])
    B.null = sb("null", [P, 4, 4])
    B.sum = sb("sum", [P, 2, 4])
    return B


def pe_turn(nc, K, pe, a, B, it, k, g, ready):
    u = a.unit(it, k, g)
    s = (a.groups * k + g) % 2
    pe.wait_ge(ready, done(u + 1))
    pe.wait_ge(a.turned_copied, done(u - 1))
    for h in range(4):
        m = nc.tensor.transpose(K.T[:, s, h * P:(h + 1) * P], B.exp[:, s, h, :], K.w["ident"][:, :])
    m.then_inc(a.turned, 1)


def pe_values(nc, K, pe, a, B, it, k, g, values, width):
    u = a.unit(it, k, g)
    s = (a.groups * k + g) % 2
    pe.wait_ge(a.turned_copied, done(u + 1))
    pe.wait_ge(a.normed, done(u - 1))
    for h in range(4):
        m = nc.tensor.matmul(K.O[:, s, h * width:(h + 1) * width], B.expT[:, s, h, :], values(h),
                             start=True, stop=True)
    m.then_inc(a.summed, 1)


def dve_shift(nc, K, v, a, B, it, k, g, scale, clamp=False):
    u = a.unit(it, k, g)
    s = (a.groups * k + g) % 2
    scores = K.S[:, s, :].rearrange("p (h k) -> p h k", h=4)
    v.wait_ge(a.scores_ready, done(u + 1))
    v.wait_ge(a.exp_ready, done(u - 1))
    nc.vector.tensor_reduce(B.max[:, s, :], scores, AX.X, ALU.max).then_inc(a.max_ready, 1)
    v.wait_ge(a.max_ready, done(u + 1))
    if clamp:
        nc.vector.tensor_scalar(B.shift[:, s, :], B.max[:, s, :], 0.0, -scale, ALU.max, ALU.mult).then_inc(a.shifted, 1)
    else:
        nc.vector.tensor_scalar(B.shift[:, s, :], B.max[:, s, :], -scale, None, ALU.mult).then_inc(a.shifted, 1)


def act_exp(nc, K, act, a, B, it, k, g, scale, null=False):
    u = a.unit(it, k, g)
    s = (a.groups * k + g) % 2
    act.wait_ge(a.shifted, done(u + 1))
    if null:
        act.wait_ge(a.weighed, done(u - 3))
        nc.scalar.activation(B.null[:, g, :], B.shift[:, s, :], ACT.Exp).then_inc(a.null_ready, 1)
    act.wait_ge(a.turned, done(u - 1))
    for h in range(4):
        sums = {"accum_out": B.sum[:, s, h:h + 1]} if null else {}
        m = nc.scalar.activation(B.exp[:, s, h, :], K.S[:, s, h * P:(h + 1) * P], ACT.Exp, bias=B.shift[:, s, h:h + 1],
                                 scale=scale, **sums)
    m.then_inc(a.exp_ready, 1)


def act_copy_turned(nc, K, act, a, B, it, k, g):
    u = a.unit(it, k, g)
    s = (a.groups * k + g) % 2
    act.wait_ge(a.turned, done(u + 1))
    act.wait_ge(a.summed, done(u - 1))
    nc.scalar.copy(B.expT[:, s, :, :], K.T[:, s, :].rearrange("p (h k) -> p h k", h=4)).then_inc(a.turned_copied, 1)


def dve_norm(nc, K, v, a, B, it, k, g, out, width):
    u = a.unit(it, k, g)
    s = (a.groups * k + g) % 2
    o = K.O[:, s, 0:4 * width].rearrange("p (h w) -> p h w", h=4)
    v.wait_ge(a.summed, done(u + 1))
    nc.vector.reciprocal(B.rec[:, s, :].unsqueeze(2), o[:, :, width - 1:width]).then_inc(a.recip_ready, 1)
    v.wait_ge(a.recip_ready, done(u + 1))
    nc.vector.tensor_tensor(out, o[:, :, 0:width - 1], bc(B.rec[:, s, :].unsqueeze(2), [P, 4, width - 1]),
                            ALU.mult).then_inc(a.normed, 1)


def pool_rstd(nc, K, pool, ln_chain, rstd_ready):
    pool.wait_ge(ln_chain, 7)
    for own in (slice(0, G4), slice(G4, NB)):
        nc.gpsimd.tensor_tensor(K.rstd[:, own], K.var[:, own], K.neg_half[:, own], ALU.pow).then_inc(rstd_ready, 1)


def pool_normalise(nc, K, pool, a, xn, turn, k):
    b = a.seqs * turn + k
    own = bass.ds(b, 1)
    if k == 0:
        seqs = bass.ds(b, a.seqs)
        nc.gpsimd.tensor_tensor(K.rstd[:, seqs], K.var[:, seqs], K.neg_half[:, 0:a.seqs], ALU.pow).then_inc(a.rstd_ready, 1)
    pool.wait_ge(a.copied["x"], done(b - 1))
    pool.sem_inc(a.wait_carried, 1)
    nc.gpsimd.tensor_tensor(xn[:, k % 2, :], K.x[:, b, :], bc(K.mean[:, own], [P, D]), ALU.subtract).then_inc(a.centred_ready, 1)
    if k == 0:
        pool.wait_ge(a.rstd_ready, done(turn + 1))
    pool.wait_ge(a.centred_ready, done(b + 1))
    pool.sem_inc(a.wait_carried, 1)
    nc.gpsimd.tensor_tensor(xn[:, k % 2, :], xn[:, k % 2, :], bc(K.rstd[:, own], [P, D]), ALU.mult).then_inc(a.xn_ready, 1)




def layer0_attention(nc, K, A):
    H, HD = 8, 16
    W = HD + 1
    with ExitStack() as c:
        def sb(name, shape, dt=F32):
            return c.enter_context(nc.sbuf_tensor(f"l0_{name}", shape, dt))

        def sem(name):
            return c.enter_context(nc.semaphore(f"l0_{name}"))

        extra = (("u", 3), ("v", -1), ("k", -5), ("q", -3), ("o", 4), ("x", -4))
        a = Attention(nc, c, "l0", 2, 4, 3, extra, ("k", "v", "x", "q", "u", "o"))
        B = attn_buffers(nc, c, "l0")
        ctxT = sb("ctxT", [P, 4, 2, P])
        mask_bc = sb("mask_bc", [P, NB, P])
        mask_col = sb("mask_col", [P, NB])
        xn = sb("xn", [P, 2, D])
        xnT = sb("xnT", [P, 4, P])
        qT = sb("qT", [P, 2, P])
        kT = sb("kT", [P, 2, P])
        kz = sb("kz", [P, 2, H, P])
        vx = sb("vx", [P, 2, H, W])
        upd = sb("upd", [P, 2, D])
        updT = sb("updT", [P, 2, D])
        ctx_loaded = [sem(f"ctx_loaded{k}") for k in range(4)]
        neg_row = sb("neg_row", [1, NB * P], BF16)
        mask_loaded = sem("mask_loaded")
        neg_moved = sem("neg_moved")
        keys_ready = sem("keys_ready")
        ones_set = sem("ones_set")

        with nc.Block() as block:
            @block.sync
            def _(sp):
                mv = A["mask_BxS2_fk1"].rearrange("(o b) k -> o b k", o=1)
                sp.dma_start(mask_bc[:, :, :], bc(mv, [P, NB, P])).then_inc(mask_loaded, 16)
                sp.dma_start(mask_col[:, :], A["maskT"]).then_inc(mask_loaded, 16)
                sp.dma_start(neg_row[0:1, :].rearrange("o (b k) -> o b k", b=NB), K.neg32[:, :]).then_inc(neg_moved, 16)
                context = A["ctxT"].rearrange("b (c p) t -> p b c t", p=P)
                for turn in range(TURNS4):
                    for b in range(4 * turn, 4 * turn + 4):
                        sp.wait_ge(a.copied["v"], done(b - 3))
                        sp.dma_start(ctxT[:, b % 4, :, :], context[:, b, :, :]).then_inc(ctx_loaded[b % 4], 16)
                    if turn + 1 < len(WEIGHTS):
                        K.load_weights(sp, turn + 1)
                    own = slice(G4 * turn, G4 * turn + G4)
                    sp.dma_start(K.ctx[:, own, :], A["ctx_2048"].rearrange("b p f -> p b f")[:, own, :]).then_inc(K.ctx_loaded, 16)

            @block.tensor
            def _(pe):
                start_counts(pe, [a.scores_ready, a.turned, a.summed, *a.j_ready.values()])
                pe.wait_ge(K.w_loaded[0], K.w_count[0])
                pe.wait_ge(neg_moved, 16)

                def step_of(it, step):
                    kind, k = step[0], step[1]
                    b = 4 * it + k
                    if kind in a.copied:
                        a.wait_bank(pe, it, kind, k)
                        J = K.J[:, a.j_bank(kind, k), 0:P]
                    if kind == "k":
                        pe.wait_ge(ctx_loaded[k], 16 * it + 16)
                        for j in range(2):
                            m = nc.tensor.matmul(J, K.w["w_src"][:, j, 0:D], ctxT[:, k, j, :], start=(j == 0), stop=(j == 1))
                    elif kind == "v":
                        for j in range(2):
                            nc.tensor.matmul(J, ctxT[:, k, j, :], K.w["w_src"][:, j, D:2 * D], start=(j == 0), stop=False)
                        m = nc.tensor.matmul(J, K.ones_row[0:1, :], K.w["b_srcv"][0:1, :], start=False, stop=True)
                    elif kind == "x":
                        pe.wait_ge(a.xn_ready, done(b + 1))
                        m = nc.tensor.transpose(J, xn[:, k % 2, :], K.w["ident"][:, :])
                    elif kind == "q":
                        pe.wait_ge(a.copied["x"], done(4 * it + k + 1))
                        m = nc.tensor.matmul(J, K.w["w_tgt"][:, :], xnT[:, k, :], start=True, stop=True)
                    elif kind == "u":
                        pe.wait_ge(a.normed, done(a.unit(it, k, 1) + 1))
                        m = nc.tensor.transpose(J, upd[:, k % 2, :], K.w["ident"][:, :])
                    elif kind == "o":
                        pe.wait_ge(a.copied["u"], done(4 * it + k + 1))
                        nc.tensor.matmul(J, xnT[:, k, :], K.w["w_out0"][:, 0, :], start=True, stop=False)
                        nc.tensor.matmul(J, K.ones_row[0:1, :], K.w["b_out0"][0:1, :], start=False, stop=False)
                        m = nc.tensor.matmul(J, updT[:, k % 2, :], K.w["w_out0"][:, 1, :], start=False, stop=True)
                    elif kind == "S":
                        g = step[2]
                        u = a.unit(it, k, g)
                        s = (2 * k + g) % 2
                        if g == 0:
                            pe.wait_ge(a.copied["q"], done(4 * it + k + 1))
                            pe.wait_ge(keys_ready, done(4 * it + k + 1))
                        pe.wait_ge(a.exp_ready, done(u - 1))
                        neg = bc(neg_row[0:1, bass.ds((4 * it + k) * P, P)].unsqueeze(1), [1, 4, P])
                        nc.tensor.matmul(K.S[:, s, :], qT[:, k % 2, :], kz[:, k % 2, 4 * g:4 * g + 4, :],
                                         start=True, stop=False)
                        nc.tensor.matmul(K.S[:, s, :], K.ones_bf[0:1, :], neg, start=False, stop=True)\
                            .then_inc(a.scores_ready, 1)
                    elif kind == "T":
                        pe_turn(nc, K, pe, a, B, it, k, step[2], a.exp_ready)
                    elif kind == "V":
                        g = step[2]
                        if g == 0:
                            pe.wait_ge(a.copied["v"], done(4 * it + k + 1))
                        pe_values(nc, K, pe, a, B, it, k, g, lambda h: vx[:, k % 2, 4 * g + h, :], W)
                    if kind in a.copied:
                        m.then_inc(a.j_ready[kind], 1)
                a.run(pe, step_of)

            @block.vector
            def _(v):
                start_counts(v, [a.max_ready, a.shifted, a.recip_ready, a.normed, a.x_done,
                                 a.copied["k"], a.copied["q"], a.copied["o"]])
                nc.vector.memset(vx[:, :, :, HD:W], 1.0).then_inc(ones_set, 1)
                ln_statistics(nc, K, v, a.ln_chain)
                v.wait_ge(K.w_loaded[0], K.w_count[0])
                v.wait_ge(mask_loaded, 32)
                v.wait_ge(K.gates_ready, 1)

                def step_of(it, step):
                    kind, k = step[0], step[1]
                    b = 4 * it + k
                    if kind in ("k", "q"):
                        v.wait_ge(a.j_ready[kind], done(b + 1))
                        if kind == "k":
                            v.wait_ge(keys_ready, done(b - 1))
                        else:
                            v.wait_ge(a.scores_ready, done(a.unit(it, k, 1) + 1 - 4))
                        dst, bias = (kT, K.w["b_srck"]) if kind == "k" else (qT, K.w["b_tgt"])
                        nc.vector.scalar_tensor_tensor(
                            out=dst[:, k % 2, :], in0=K.J[:, a.j_bank(kind, k), 0:P], scalar=bias[:, 0:1],
                            in1=mask_bc[:, b, :], op0=ALU.add, op1=ALU.mult).then_inc(a.copied[kind], 1)
                    elif kind == "S":
                        dve_shift(nc, K, v, a, B, it, k, step[2], float(HD) ** -0.5)
                    elif kind == "V":
                        g = step[2]
                        if g == 0:
                            v.wait_ge(a.copied["u"], done(b - 1))
                        dve_norm(nc, K, v, a, B, it, k, g,
                                 upd[:, k % 2, 64 * g:64 * g + 64].rearrange("p (h d) -> p h d", h=4), W)
                    elif kind == "o":
                        v.wait_ge(a.j_ready[kind], done(b + 1))
                        nc.vector.scalar_tensor_tensor(
                            out=K.x[:, b, :], in0=K.J[:, a.j_bank(kind, k), 0:P], scalar=K.tg[:, 0:1],
                            in1=K.x[:, b, :], op0=ALU.mult, op1=ALU.add).then_inc(a.copied["o"], 1)
                        v.wait_ge(a.copied["o"], done(b + 1))
                        nc.vector.bn_stats(K.st6[:, b, :], K.x[:, b, :])
                a.run(v, step_of)

            @block.scalar
            def _(act):
                start_counts(act, [a.exp_ready, a.turned_copied, a.copied["x"], a.copied["v"], a.copied["u"]])
                act.wait_ge(mask_loaded, 32)
                act.wait_ge(ones_set, 1)

                def step_of(it, step):
                    kind, k = step[0], step[1]
                    b = 4 * it + k
                    if kind in ("x", "u"):
                        act.wait_ge(a.j_ready[kind], done(b + 1))
                        act.wait_ge(a.copied["o"], done(b - 3 if kind == "x" else b - 1))
                        nc.scalar.copy(xnT[:, k, :] if kind == "x" else updT[:, k % 2, :], K.J[:, a.j_bank(kind, k), 0:P])\
                            .then_inc(a.copied[kind], 1)
                    elif kind == "v":
                        act.wait_ge(a.j_ready[kind], done(b + 1))
                        act.wait_ge(a.summed, done(a.unit(it, k, 1) + 1 - 4))
                        nc.scalar.mul(vx[:, k % 2, :, 0:HD], K.J[:, a.j_bank(kind, k), 0:P].rearrange("p (h d) -> p h d", h=H),
                                      mask_col[:, bass.ds(b, 1)]).then_inc(a.copied["v"], 1)
                    elif kind == "S":
                        act_exp(nc, K, act, a, B, it, k, step[2], float(HD) ** -0.5)
                    elif kind == "T":
                        act_copy_turned(nc, K, act, a, B, it, k, step[2])
                a.run(act, step_of, copies_first=True)

            @block.gpsimd
            def _(pool):
                start_counts(pool, [keys_ready, a.rstd_ready, a.centred_ready, a.xn_ready])
                pool.wait_ge(a.ln_chain, 7)
                pool.wait_ge(K.w_loaded[0], K.w_count[0])
                pool_normalise(nc, K, pool, a, xn, 0, 0)

                def keys_and_rows(it, k):
                    b = 4 * it + k
                    pool.wait_ge(a.copied["k"], done(b + 1))
                    pool.wait_ge(a.scores_ready, done(2 * b - 2))
                    nc.gpsimd.tensor_tensor(kz[:, k % 2, :, :], bc(kT[:, k % 2, :].unsqueeze(1), [P, H, P]),
                                            bc(K.w["head16"][:, :].unsqueeze(2), [P, H, P]), ALU.mult).then_inc(keys_ready, 1)
                    if k < 3:
                        pool_normalise(nc, K, pool, a, xn, it, k + 1)
                    elif not isinstance(it, int):
                        pool_normalise(nc, K, pool, a, xn, it + 1, 0)
                with pool.Fori(0, a.turns - 1) as it:
                    for k in range(4):
                        keys_and_rows(it, k)
                for k in range(4):
                    keys_and_rows(a.turns - 1, k)


def run_turns(engine, turn):
    with engine.Fori(0, TURNS4 // 2 - 1) as pair:
        turn(2 * pair, 0, False)
        turn(2 * pair + 1, 1, False)
    turn(TURNS4 - 2, 0, False)
    turn(TURNS4 - 1, 1, True)


def normalise4(nc, K, v, it, xn, xn_ready, used):
    v.wait_ge(used, done(it))
    for j in range(G4):
        b = 4 * it + j
        n = nc.vector.tensor_scalar(xn[:, j, :], K.x[:, b, :], K.mean[:, bass.ds(b, 1)], K.rstd[:, bass.ds(b, 1)],
                                    ALU.subtract, ALU.mult)
    n.then_inc(xn_ready, 1)


TOP2_STEPS = 5


def top2_buffers(sb, experts):
    return {"value": sb("top_value", [P, G4, 8]), "index": sb("top_index", [P, G4, 8], U32), "place": sb("top_place", [P, G4, 2]),
            "equal": sb("top_equal", [P, G4, 2, experts]), "chosen": sb("top_chosen", [P, G4, experts])}


def top2(nc, K, v, top, score, experts, at, step, carried):
    v.sem_inc(carried, 1)
    for j in range(G4):
        m = nc.vector.max(top["value"][:, j, :], score[:, j, :])
    m.then_inc(step, 1)
    v.wait_ge(step, at(1))
    v.sem_inc(carried, 1)
    for j in range(G4):
        m = nc.vector.max_index(top["index"][:, j, :], top["value"][:, j, :], score[:, j, :])
    m.then_inc(step, 1)
    v.wait_ge(step, at(2))
    nc.vector.tensor_copy(top["place"][:, :, :], top["index"][:, :, 0:2]).then_inc(step, 1)
    v.wait_ge(step, at(3))
    shape = [P, 2, experts]
    for j in range(G4):
        m = nc.vector.tensor_tensor(top["equal"][:, j, :, :], bc(K.w["iota_row"][:, 0:experts].unsqueeze(1), shape),
                                    bc(top["place"][:, j, :].unsqueeze(2), shape), ALU.is_equal)
    m.then_inc(step, 1)
    v.wait_ge(step, at(4))
    nc.vector.tensor_tensor(top["chosen"][:, :, :], top["equal"][:, :, 0, :], top["equal"][:, :, 1, :], ALU.add).then_inc(step, 1)
    v.wait_ge(step, at(5))


def layer0_ffn(nc, K, A):
    E = EXPERTS0
    with ExitStack() as c:
        def sb(name, shape, dt=F32):
            return c.enter_context(nc.sbuf_tensor(f"f0_{name}", shape, dt))

        def sem(name):
            return c.enter_context(nc.semaphore(f"f0_{name}"))

        xn = sb("xn", [P, G4, D])
        xnT = sb("xnT", [P, 2, G4 * P])
        score = sb("score", [P, G4, E])
        top = top2_buffers(sb, E)
        weight = sb("weight", [P, 2, G4, E])
        weightT = sb("weightT", [E, G4, P])
        hidden = sb("hidden", [P, 2, G4 * P])
        acc = sb("acc", [P, G4, D])
        fold_rows = sb("fold_rows", [P, 3, 512])
        up_w = sb("up_w", [P, 9, 2, 2, 256])
        ln_chain = sem("ln_chain")
        rstd_ready = sem("rstd_ready")
        xn_ready = sem("xn_ready")
        xn_used = sem("xn_used")
        xnT_ready = sem("xnT_ready")
        gate_ready = sem("gate_ready")
        dve_step = sem("dve_step")
        carried = sem("carried")
        weight_ready = sem("weight_ready")
        weight_turned = sem("weight_turned")
        weightT_ready = sem("weightT_ready")
        bias_ready = sem("bias_ready")
        acc_started = sem("acc_started")
        h_ready = sem("h_ready")
        relu_ready = sem("relu_ready")
        y_ready = sem("y_ready")
        y_added = sem("y_added")
        up_loaded = sem("up_loaded")
        fold = sem("fold")

        with nc.Block() as block:
            @block.sync
            def _(sp):
                sp.dma_start(up_w[:, :, :, :, :], bc(A["up_w"], [P, 9, 2, 2, 256])).then_inc(up_loaded, 16)
                sp.wait_ge(up_loaded, 16)

            @block.gpsimd
            def _(pool):
                pool_rstd(nc, K, pool, ln_chain, rstd_ready)
                pool.wait_ge(up_loaded, 16)
                pool.wait_ge(K.w_loaded[7], K.w_count[7])
                butterfly(nc, pool, K.w["up_rows"], fold_rows, up_w, fold, False)

            @block.tensor
            def _(pe):
                start_counts(pe, [xn_used, gate_ready, weight_turned, bias_ready, h_ready, y_ready])
                pe.wait_ge(K.w_loaded[1], K.w_count[1])

                def rows(it):
                    pe.wait_ge(xn_ready, done(it + 1))
                    pe.wait_ge(xnT_ready, done(it))
                    for j in range(G4):
                        m = nc.tensor.transpose(K.T[:, 0, j * P:(j + 1) * P], xn[:, j, :], K.w["ident"][:, :])
                    m.then_inc(xn_used, 1)

                def gate(it, s):
                    pe.wait_ge(xnT_ready, done(it + 1))
                    pe.wait_ge(weight_ready, done(it))
                    nc.tensor.matmul(K.J[:, 0, 0:G4 * E], K.ones_row[0:1, :], bc(K.w["b_gate"][0:1, :].unsqueeze(1), [1, G4, E]),
                                     start=True, stop=False, skip_group_check=True)
                    for j in range(G4):
                        m = nc.tensor.matmul(K.J[:, 0, j * E:(j + 1) * E], xnT[:, s, j * P:(j + 1) * P], K.w["w_gate"][:, :],
                                             start=False, stop=(j == G4 - 1), skip_group_check=True)
                    m.then_inc(gate_ready, 1)

                def turn_weights(it, s):
                    pe.wait_ge(weight_ready, done(it + 1))
                    pe.wait_ge(weightT_ready, done(it))
                    for j in range(G4):
                        m = nc.tensor.transpose(K.J[0:E, 1, j * P:(j + 1) * P], weight[:, s, j, :], K.w["ident"][:, :])
                    m.then_inc(weight_turned, 1)

                def biases(it):
                    pe.wait_ge(weightT_ready, done(it + 1))
                    pe.wait_ge(acc_started, done(it))
                    for j in range(G4):
                        m = nc.tensor.matmul(K.T[:, 1, j * P:(j + 1) * P], weightT[0:E, j, :], K.w["b2_0"][0:E, :],
                                             start=True, stop=True)
                    m.then_inc(bias_ready, 1)

                def first(it, s, e):
                    pe.wait_ge(relu_ready, done(E * it + e - 1))
                    nc.tensor.matmul(K.S[:, e % 2, :], K.w["w1_0"][:, e, :], xnT[:, s, :], start=True, stop=True)\
                        .then_inc(h_ready, 1)

                def turn(it, s, last):
                    for e in range(E):
                        pe.wait_ge(relu_ready, done(E * it + e + 1))
                        pe.wait_ge(y_added, done(G4 * (E * it + e - 1)))
                        for j in range(G4):
                            m = nc.tensor.matmul(K.O[:, e % 2, j * P:(j + 1) * P], hidden[:, e % 2, j * P:(j + 1) * P],
                                                 K.w["w2_0"][:, e, :], start=True, stop=True)
                        m.then_inc(y_ready, 1)
                        if e + 2 < E:
                            first(it, s, e + 2)
                        elif not last:
                            first(it + 1, 1 - s, e + 2 - E)
                        if not last:
                            if e == 1:
                                rows(it + 1)
                            elif e == 2:
                                gate(it + 1, 1 - s)
                            elif e == 5:
                                turn_weights(it + 1, 1 - s)
                            elif e == 6:
                                biases(it + 1)
                rows(0)
                gate(0, 0)
                first(0, 0, 0)
                first(0, 0, 1)
                turn_weights(0, 0)
                biases(0)
                run_turns(pe, turn)

            @block.scalar
            def _(act):
                start_counts(act, [xnT_ready, weightT_ready, relu_ready])

                def copy_rows(it, s):
                    act.wait_ge(xn_used, done(it + 1))
                    act.wait_ge(h_ready, done(E * (it - 1)))
                    nc.scalar.copy(xnT[:, s, :], K.T[:, 0, :]).then_inc(xnT_ready, 1)

                def copy_weights(it):
                    act.wait_ge(weight_turned, done(it + 1))
                    act.wait_ge(bias_ready, done(it))
                    nc.scalar.copy(weightT[:, :, :], K.J[0:E, 1, :].rearrange("p (j t) -> p j t", j=G4))\
                        .then_inc(weightT_ready, 1)

                def relu(it, e):
                    act.wait_ge(h_ready, done(E * it + e + 1))
                    act.wait_ge(y_ready, done(E * it + e - 1))
                    nc.scalar.activation(hidden[:, e % 2, :], K.S[:, e % 2, :], ACT.Relu, bias=K.w["b1_0"][:, e:e + 1])\
                        .then_inc(relu_ready, 1)

                def turn(it, s, last):
                    for e in range(E):
                        if e + 2 < E:
                            relu(it, e + 2)
                        elif not last:
                            relu(it + 1, e + 2 - E)
                        if e == 1 and not last:
                            copy_rows(it + 1, 1 - s)
                        elif e == 5 and not last:
                            copy_weights(it + 1)
                copy_rows(0, 0)
                relu(0, 0)
                relu(0, 1)
                copy_weights(0)
                run_turns(act, turn)

            @block.vector
            def _(v):
                ln_statistics(nc, K, v, ln_chain)
                start_counts(v, [xn_ready, dve_step, weight_ready, acc_started, y_added])
                v.wait_ge(K.w_loaded[2], K.w_count[2])
                v.wait_ge(K.ctx_loaded, 16 * TURNS4)
                v.wait_ge(rstd_ready, 1)

                def weights(it, s):
                    STEPS = 1 + TOP2_STEPS
                    v.wait_ge(gate_ready, done(it + 1))
                    nc.vector.tensor_copy(score[:, :, :], K.J[:, 0, 0:G4 * E].rearrange("p (j e) -> p j e", j=G4))\
                        .then_inc(dve_step, 1)
                    v.wait_ge(dve_step, done(STEPS * it + 1))
                    top2(nc, K, v, top, score, E, lambda n: done(STEPS * it + 1 + n), dve_step, carried)
                    nc.vector.scalar_tensor_tensor(out=weight[:, s, :, :], in0=top["chosen"][:, :, :], scalar=K.tg[:, 4:5],
                                                   in1=score[:, :, :], op0=ALU.mult, op1=ALU.mult).then_inc(weight_ready, 1)

                def turn(it, s, last):
                    v.wait_ge(bias_ready, done(it + 1))
                    nc.vector.tensor_tensor(acc[:, :, :], K.T[:, 1, :].rearrange("p (j d) -> p j d", j=G4),
                                            K.x[:, bass.ds(G4 * it, G4), :], ALU.add).then_inc(acc_started, 1)
                    v.wait_ge(acc_started, done(it + 1))
                    v.wait_ge(weight_ready, done(it + 1))
                    if not last:
                        normalise4(nc, K, v, it + 1, xn, xn_ready, xn_used)
                    for e in range(E):
                        v.wait_ge(y_ready, done(E * it + e + 1))
                        for j in range(G4):
                            if e > 0:
                                v.wait_ge(y_added, done(G4 * (E * it + e - 1) + j + 1))
                            to = K.x[:, G4 * it + j, :] if e == E - 1 else acc[:, j, :]
                            nc.vector.scalar_tensor_tensor(out=to, in0=K.O[:, e % 2, j * P:(j + 1) * P],
                                                           scalar=weight[:, s, j, e:e + 1], in1=acc[:, j, :],
                                                           op0=ALU.mult, op1=ALU.add).then_inc(y_added, 1)
                        if e == 3 and not last:
                            weights(it + 1, 1 - s)
                        if e == 2 and last:
                            nc.vector.tensor_tensor(K.hot[:, :, :], bc(K.w["ident"][:, :].unsqueeze(1), [P, NB, P]),
                                                    bc(K.plug[:, :].unsqueeze(2), [P, NB, P]), ALU.mult)
                        if e == 5:
                            for j in range(G4):
                                nc.vector.bn_stats(K.st6c[:, G4 * it + j, :], K.ctx[:, G4 * it + j, :])
                    for j in range(G4):
                        v.wait_ge(y_added, done(G4 * (E * it + E - 1) + j + 1))
                        nc.vector.bn_stats(K.st6[:, G4 * it + j, :], K.x[:, G4 * it + j, :])
                normalise4(nc, K, v, 0, xn, xn_ready, xn_used)
                v.wait_ge(rstd_ready, 2)
                weights(0, 0)
                run_turns(v, turn)


def butterfly(nc, pool, rows, spare, w, fold, transposed):
    R = rows.shape[1]
    n = 0
    for r in range(R):
        src, dst = rows[:, r, :], spare[:, r, :]
        for stage in (reversed(range(9)) if transposed else range(9)):
            s = 2 ** stage
            x = src.rearrange("p (n two s) -> p two n s", two=2, s=s)
            y = dst.rearrange("p (n two s) -> p two n s", two=2, s=s)
            part = spare[:, R, 0:256].rearrange("p (n s) -> p n s", s=s)
            for o in range(2):
                pick = lambda i: (w[:, stage, i, o, :] if transposed else w[:, stage, o, i, :]).rearrange("p (n s) -> p n s", s=s)
                if n:
                    pool.wait_ge(fold, n)
                nc.gpsimd.tensor_tensor(part, x[:, 1, :, :], pick(1), ALU.mult).then_inc(fold, 1)
                nc.gpsimd.tensor_tensor(y[:, o, :, :], x[:, 0, :, :], pick(0), ALU.mult).then_inc(fold, 1)
                n += 2
                pool.wait_ge(fold, n)
                nc.gpsimd.tensor_tensor(y[:, o, :, :], y[:, o, :, :], part, ALU.add).then_inc(fold, 1)
                n += 1
            src, dst = dst, src
        pool.wait_ge(fold, n)
        nc.gpsimd.tensor_copy(rows[:, r, :], spare[:, r, :]).then_inc(fold, 1)
        n += 1
    pool.wait_ge(fold, n)


def layer1_attention(nc, K, A):
    import math
    import numpy as np
    dt = float(-np.log(-np.expm1(np.float32(-1e-3))))
    keep = math.exp(-1e-3)
    with ExitStack() as c:
        def sb(name, shape, dt=F32):
            return c.enter_context(nc.sbuf_tensor(f"l1_{name}", shape, dt))

        def sem(name):
            return c.enter_context(nc.semaphore(f"l1_{name}"))

        m1 = sb("m1", [P, NB])
        m2 = sb("m2", [P, NB])
        rctx = sb("rctx", [P, NB])
        row_square = sb("row_square", [P, NB])
        row_scale = sb("row_scale", [P, NB])
        w_in = sb("w_in", [P, P])
        g_init = sb("g_init", [P, P])
        hn = sb("hn", [P, G4, D])
        hT = sb("hT", [P, 2, G4 * P])
        lag = sb("lag", [P, G4 * P])
        decay = sb("decay", [P, G4 * P])
        pick = sb("pick", [P, 2, G4, P])
        u = sb("u", [P, 2, G4, D])
        ln_chain = sem("ln_chain")
        pre = sem("pre")
        scales_ready = sem("scales_ready")
        plug_ready = sem("plug_ready")
        lag_ready = sem("lag_ready")
        decay_ready = sem("decay_ready")
        pick_ready = sem("pick_ready")
        hn_ready = sem("hn_ready")
        turned = sem("turned")
        hT_ready = sem("hT_ready")
        sum_ready = sem("sum_ready")
        x_done = sem("x_done")

        with nc.Block() as block:
            @block.vector
            def _(v):
                n = [0]

                def link(ins):
                    n[0] += 1
                    ins.then_inc(pre, 1)
                    v.wait_ge(pre, n[0])
                ln_statistics(nc, K, v, ln_chain)
                v.wait_ge(K.w_loaded[2], K.w_count[2])
                link(nc.vector.reciprocal(K.lna[:, :], K.var[:, :]))
                link(nc.vector.scalar_tensor_tensor(out=K.lnb[:, :], in0=K.var[:, :], scalar=-EPS_LN, in1=K.lna[:, :],
                                                    op0=ALU.add, op1=ALU.mult))
                link(nc.vector.scalar_tensor_tensor(out=row_square[:, :], in0=K.lnb[:, :], scalar=1e-5, in1=K.var[:, :],
                                                    op0=ALU.add, op1=ALU.mult))
                link(nc.vector.tensor_tensor(m1[:, :], K.st6c[:, :, 1], K.st6c[:, :, 1], ALU.mult))
                link(nc.vector.tensor_tensor(m2[:, :], K.st6c[:, :, 4], K.st6c[:, :, 4], ALU.mult))
                link(nc.vector.tensor_tensor(m1[:, :], m1[:, :], m2[:, :], ALU.add))
                link(nc.vector.tensor_tensor(m2[:, :], K.st6c[:, :, 2], K.st6c[:, :, 5], ALU.add))
                link(nc.vector.tensor_scalar(m2[:, :], m2[:, :], 1.0 / DC, 1e-5, ALU.mult, ALU.add))
                link(nc.vector.scalar_tensor_tensor(out=m1[:, :], in0=m1[:, :], scalar=0.5, in1=m2[:, :],
                                                    op0=ALU.mult, op1=ALU.add))
                link(nc.vector.tensor_scalar(w_in[:, :], K.w["w_in"][:, :], K.w["g_res"][:, 0:1], None, ALU.mult))
                link(nc.vector.tensor_scalar(g_init[:, :], K.w["g_init"][:, :], keep, None, ALU.mult))
                start_counts(v, [lag_ready, pick_ready, hn_ready, x_done])

                def prepare(it, s):
                    v.wait_ge(scales_ready, done(2 * it + 2))
                    v.wait_ge(turned, done(it))
                    for j in range(G4):
                        b = G4 * it + j
                        m = nc.vector.tensor_scalar(hn[:, j, :], K.x[:, b, :], K.mean[:, bass.ds(b, 1)],
                                                    row_scale[:, bass.ds(b, 1)], ALU.subtract, ALU.mult)
                    m.then_inc(hn_ready, 1)
                    v.wait_ge(plug_ready, done(it + 1))
                    v.wait_ge(decay_ready, done(it))
                    nc.vector.tensor_scalar(lag[:, :], K.S[:, s, :], K.w["iota_col"][:, 0:1], 0.0, ALU.subtract, ALU.max)\
                        .then_inc(lag_ready, 1)
                    v.wait_ge(sum_ready, done(it - 1))
                    for j in range(G4):
                        b = G4 * it + j
                        nc.vector.scalar_tensor_tensor(out=u[:, s, j, :], in0=K.ctx[:, b, 0:D], scalar=rctx[:, bass.ds(b, 1)],
                                                       in1=g_init[:, :], op0=ALU.mult, op1=ALU.mult)
                    v.wait_ge(decay_ready, done(it + 1))
                    nc.vector.scalar_tensor_tensor(out=pick[:, s, :, :].rearrange("p j t -> p (j t)"), in0=K.S[:, s, :],
                                                   scalar=K.w["iota_col"][:, 0:1], in1=decay[:, :],
                                                   op0=ALU.is_ge, op1=ALU.mult).then_inc(pick_ready, 1)

                def turn(it, s, last):
                    if not last:
                        prepare(it + 1, 1 - s)
                    v.wait_ge(sum_ready, done(it + 1))
                    xs = K.x[:, bass.ds(G4 * it, G4), :]
                    nc.vector.scalar_tensor_tensor(out=xs, in0=K.O[:, s, :].rearrange("p (j d) -> p j d", j=G4),
                                                   scalar=K.tg[:, 1:2], in1=xs, op0=ALU.mult, op1=ALU.add).then_inc(x_done, 1)
                    v.wait_ge(x_done, done(it + 1))
                    for j in range(G4):
                        nc.vector.bn_stats(K.st6[:, G4 * it + j, :], K.x[:, G4 * it + j, :])
                prepare(0, 0)
                run_turns(v, turn)

            @block.gpsimd
            def _(pool):
                start_counts(pool, [scales_ready])
                pool.wait_ge(pre, 9)
                with pool.Fori(0, TURNS4) as it:
                    own = bass.ds(G4 * it, G4)
                    nc.gpsimd.tensor_tensor(row_scale[:, own], row_square[:, own], K.neg_half[:, 0:G4], ALU.pow)\
                        .then_inc(scales_ready, 1)
                    nc.gpsimd.tensor_tensor(rctx[:, own], m1[:, own], K.neg_half[:, 0:G4], ALU.pow).then_inc(scales_ready, 1)

            @block.scalar
            def _(act):
                start_counts(act, [decay_ready, hT_ready])

                def prepare(it, s):
                    act.wait_ge(lag_ready, done(it + 1))
                    act.wait_ge(pick_ready, done(it))
                    nc.scalar.activation(decay[:, :], lag[:, :], ACT.Exp, scale=-dt).then_inc(decay_ready, 1)
                    act.wait_ge(turned, done(it + 1))
                    act.wait_ge(sum_ready, done(it - 1))
                    nc.scalar.copy(hT[:, s, :], K.T[:, s, :]).then_inc(hT_ready, 1)

                def turn(it, s, last):
                    if not last:
                        prepare(it + 1, 1 - s)
                prepare(0, 0)
                run_turns(act, turn)

            @block.tensor
            def _(pe):
                start_counts(pe, [plug_ready, turned, sum_ready])
                pe.wait_ge(K.w_loaded[2], K.w_count[2])
                pe.wait_ge(pre, 11)

                def spread_picks(it, s):
                    pe.wait_ge(pick_ready, done(it - 1))
                    nc.tensor.matmul(K.S[:, s, :], K.ones_bf[:, :], K.hot[:, bass.ds(G4 * it, G4), :],
                                     start=True, stop=True).then_inc(plug_ready, 1)

                def rows(it, s):
                    pe.wait_ge(hn_ready, done(it + 1))
                    pe.wait_ge(hT_ready, done(it - 1))
                    for j in range(G4):
                        m = nc.tensor.transpose(K.T[:, s, j * P:(j + 1) * P], hn[:, j, :], K.w["ident"][:, :])
                    m.then_inc(turned, 1)

                def turn(it, s, last):
                    if not last:
                        spread_picks(it + 1, 1 - s)
                    pe.wait_ge(hT_ready, done(it + 1))
                    pe.wait_ge(x_done, done(it - 1))
                    pe.wait_ge(pick_ready, done(it + 1))
                    for j in range(G4):
                        o = K.O[:, s, j * P:(j + 1) * P]
                        nc.tensor.matmul(o, hT[:, s, j * P:(j + 1) * P], w_in[:, :], start=True, stop=False)
                        nc.tensor.matmul(o, K.ones_row[0:1, :], K.w["b_in"][0:1, :], start=False, stop=False)
                        m = nc.tensor.matmul(o, pick[:, s, j, :], u[:, s, j, :], start=False, stop=True)
                    m.then_inc(sum_ready, 1)
                    if not last:
                        rows(it + 1, 1 - s)
                spread_picks(0, 0)
                rows(0, 0)
                run_turns(pe, turn)


def layer1_ffn(nc, K, A):
    E = EXPERTS1
    CH = 5
    with ExitStack() as c:
        def sb(name, shape, dt=F32):
            return c.enter_context(nc.sbuf_tensor(f"f1_{name}", shape, dt))

        def sem(name):
            return c.enter_context(nc.semaphore(f"f1_{name}"))

        xn = sb("xn", [P, G4, D])
        xnT = sb("xnT", [P, 2, G4 * P])
        prob = sb("prob", [P, G4, E])
        best = sb("best", [P, G4])
        total = sb("total", [P, G4])
        top = top2_buffers(sb, E)
        comb = sb("comb", [P, G4, E])
        combT = sb("combT", [E, 2, G4 * P])
        tanh = sb("tanh", [P, 2, G4 * P])
        gated = sb("gated", [P, 2, G4 * P])
        hidden = sb("hidden", [P, 2, G4 * P])
        half_gate = sb("half_gate", [P, 1])
        fold_rows = sb("fold_rows", [P, 2, 512])
        down_w = sb("down_w", [P, 9, 2, 2, 256])
        ln_chain = sem("ln_chain")
        rstd_ready = sem("rstd_ready")
        xn_ready = sem("xn_ready")
        xn_used = sem("xn_used")
        xnT_ready = sem("xnT_ready")
        logits_ready = sem("logits_ready")
        dve_step = sem("dve_step")
        carried = sem("carried")
        exp_ready = sem("exp_ready")
        comb_ready = sem("comb_ready")
        comb_turned = sem("comb_turned")
        combT_ready = sem("combT_ready")
        g_ready = sem("g_ready")
        gu_ready = sem("gu_ready")
        tanh_ready = sem("tanh_ready")
        mul_step = sem("mul_step")
        hidden_ready = sem("hidden_ready")
        y_ready = sem("y_ready")
        x_done = sem("x_done")
        down_loaded = sem("down_loaded")
        fold = sem("fold")
        step2_done = sem("step2_done")
        MUL = 1 + 2 * (CH - 1)

        with nc.Block() as block:
            @block.sync
            def _(sp):
                sp.dma_start(down_w[:, :, :, :, :], bc(A["down_w"], [P, 9, 2, 2, 256])).then_inc(down_loaded, 16)
                sp.wait_ge(down_loaded, 16)

            @block.gpsimd
            def _(pool):
                pool_rstd(nc, K, pool, ln_chain, rstd_ready)
                pool.wait_ge(down_loaded, 16)
                pool.wait_ge(K.w_loaded[7], K.w_count[7])
                butterfly(nc, pool, K.w["down_rows"], fold_rows, down_w, fold, True)

            @block.tensor
            def _(pe):
                start_counts(pe, [xn_used, logits_ready, comb_turned, g_ready, gu_ready, y_ready])
                pe.wait_ge(K.w_loaded[3], K.w_count[3])

                def rows(it):
                    pe.wait_ge(xn_ready, done(it + 1))
                    pe.wait_ge(combT_ready, done(it))
                    for j in range(G4):
                        m = nc.tensor.transpose(K.J[:, 0, j * P:(j + 1) * P], xn[:, j, :], K.w["ident"][:, :])
                    m.then_inc(xn_used, 1)

                def router(it, s):
                    pe.wait_ge(xnT_ready, done(it + 1))
                    for j in range(G4):
                        m = nc.tensor.matmul(K.J[:, 0, j * E:(j + 1) * E], xnT[:, s, j * P:(j + 1) * P], K.w["router1"][:, :],
                                             start=True, stop=True)
                    m.then_inc(logits_ready, 1)

                def turn_comb(it):
                    pe.wait_ge(comb_ready, done(it + 1))
                    for j in range(G4):
                        m = nc.tensor.transpose(K.J[0:E, 0, j * P:(j + 1) * P], comb[:, j, :], K.w["ident"][:, :])
                    m.then_inc(comb_turned, 1)

                def up(it, s, ch):
                    bank = (CH * s + ch) % 2
                    pe.wait_ge(hidden_ready, done(CH * it + ch - 1))
                    nc.tensor.matmul(K.S[:, bank, :], K.w["wg1"][:, ch, :], xnT[:, s, :], start=True, stop=True).then_inc(g_ready, 1)
                    m = nc.tensor.matmul(K.O[:, bank, :], K.w["wu1"][:, ch, :], xnT[:, s, :], start=True, stop=True)
                    if ch > 0:
                        if ch == 1:
                            pe.wait_ge(combT_ready, done(it + 1))
                        m = nc.tensor.matmul(K.T[:, bank, :], K.w["spread"][0:E, ch - 1, :], combT[0:E, s, :], start=True, stop=True)
                    m.then_inc(gu_ready, 1)

                def down(it, s, ch):
                    bank = (CH * s + ch) % 2
                    pe.wait_ge(hidden_ready, done(CH * it + ch + 1))
                    if ch == 0:
                        pe.wait_ge(x_done, done(it))
                    for j in range(G4):
                        m = nc.tensor.matmul(K.J[:, 1, j * P:(j + 1) * P], hidden[:, bank, j * P:(j + 1) * P],
                                             K.w["wd1"][:, ch, :], start=(ch == 0 and j == 0), stop=(ch == CH - 1),
                                             skip_group_check=True)
                    m.then_inc(y_ready, 1)

                def turn(it, s, last):
                    for ch in range(CH):
                        if ch + 1 < CH:
                            up(it, s, ch + 1)
                        elif not last:
                            up(it + 1, 1 - s, 0)
                            turn_comb(it + 1)
                        down(it, s, ch)
                        if ch == 0 and not last:
                            rows(it + 1)
                        elif ch == 1 and not last:
                            router(it + 1, 1 - s)
                rows(0)
                router(0, 0)
                up(0, 0, 0)
                turn_comb(0)
                run_turns(pe, turn)

            @block.scalar
            def _(act):
                start_counts(act, [xnT_ready, exp_ready, combT_ready, tanh_ready])

                def tanh_of(it, s, ch):
                    bank = (CH * s + ch) % 2
                    act.wait_ge(g_ready, done(CH * it + ch + 1))
                    act.wait_ge(mul_step, done(MUL * it + (-3, -1, 1, 2, 4)[ch]))
                    nc.scalar.activation(tanh[:, bank, :], K.S[:, bank, :], ACT.Tanh, scale=0.5).then_inc(tanh_ready, 1)

                def copy_rows(it, s):
                    act.wait_ge(xn_used, done(it + 1))
                    act.wait_ge(gu_ready, done(CH * (it - 1)))
                    nc.scalar.copy(xnT[:, s, :], K.J[:, 0, :]).then_inc(xnT_ready, 1)

                def exp(it):
                    act.wait_ge(dve_step, done(10 * it + 2))
                    nc.scalar.activation(prob[:, :, :], prob[:, :, :], ACT.Exp).then_inc(exp_ready, 1)

                def copy_comb(it, s):
                    act.wait_ge(comb_turned, done(it + 1))
                    act.wait_ge(gu_ready, done(CH * (it - 1)))
                    nc.scalar.copy(combT[:, s, :], K.J[0:E, 0, :]).then_inc(combT_ready, 1)

                def turn(it, s, last):
                    for ch in range(CH):
                        if ch + 1 < CH:
                            tanh_of(it, s, ch + 1)
                        elif not last:
                            tanh_of(it + 1, 1 - s, 0)
                            copy_comb(it + 1, 1 - s)
                        if ch == 0 and not last:
                            copy_rows(it + 1, 1 - s)
                        elif ch == 2 and not last:
                            exp(it + 1)
                copy_rows(0, 0)
                exp(0)
                tanh_of(0, 0, 0)
                copy_comb(0, 0)
                run_turns(act, turn)

            @block.vector
            def _(v):
                ln_statistics(nc, K, v, ln_chain)
                nc.vector.tensor_scalar(half_gate[:, :], K.tg[:, 5:6], 0.5, None, ALU.mult).then_inc(ln_chain, 1)
                v.wait_ge(ln_chain, 8)
                v.wait_ge(rstd_ready, 1)
                start_counts(v, [xn_ready, dve_step, step2_done, comb_ready, mul_step, hidden_ready, x_done])

                def gate(it, turn_s, ch):
                    s = (CH * turn_s + ch) % 2
                    first = MUL * it + (0 if ch == 0 else 2 * ch - 1)
                    v.wait_ge(tanh_ready, done(CH * it + ch + 1))
                    nc.vector.scalar_tensor_tensor(out=gated[:, s, :], in0=tanh[:, s, :], scalar=1.0, in1=K.S[:, s, :],
                                                   op0=ALU.add, op1=ALU.mult).then_inc(mul_step, 1)
                    v.wait_ge(mul_step, done(first + 1))
                    v.wait_ge(gu_ready, done(CH * it + ch + 1))
                    v.wait_ge(y_ready, done(CH * it + ch - 1))
                    if ch == 0:
                        nc.vector.tensor_tensor(hidden[:, s, :], gated[:, s, :], K.O[:, s, :], ALU.mult).then_inc(hidden_ready, 1)
                    else:
                        nc.vector.tensor_tensor(gated[:, s, :], gated[:, s, :], K.O[:, s, :], ALU.mult).then_inc(mul_step, 1)
                        v.wait_ge(mul_step, done(first + 2))
                        nc.vector.tensor_tensor(hidden[:, s, :], gated[:, s, :], K.T[:, s, :], ALU.mult).then_inc(hidden_ready, 1)

                def step(it, n, ins):
                    ins.then_inc(dve_step, 1)
                    v.wait_ge(dve_step, done(10 * it + n))

                def step2(it, n, ins):
                    ins.then_inc(step2_done, 1)
                    v.wait_ge(step2_done, done(4 * it + n))

                def shift_logits(it):
                    v.wait_ge(logits_ready, done(it + 1))
                    logits = K.J[:, 0, 0:G4 * E].rearrange("p (j e) -> p j e", j=G4)
                    step(it, 1, nc.vector.tensor_reduce(best[:, :], logits, AX.X, ALU.max))
                    step(it, 2, nc.vector.tensor_tensor(prob[:, :, :], logits, bc(best[:, :].unsqueeze(2), [P, G4, E]), ALU.subtract))

                def probabilities(it):
                    v.wait_ge(exp_ready, done(it + 1))
                    step(it, 3, nc.vector.tensor_reduce(total[:, :], prob[:, :, :], AX.X, ALU.add))
                    step(it, 4, nc.vector.reciprocal(total[:, :], total[:, :]))
                    step(it, 5, nc.vector.tensor_tensor(prob[:, :, :], prob[:, :, :], bc(total[:, :].unsqueeze(2), [P, G4, E]), ALU.mult))

                def weights(it):
                    top2(nc, K, v, top, prob, E, lambda n: done(10 * it + 5 + n), dve_step, carried)
                    step2(it, 1, nc.vector.tensor_tensor(comb[:, :, :], top["chosen"][:, :, :], prob[:, :, :], ALU.mult))
                    step2(it, 2, nc.vector.tensor_reduce(total[:, :], comb[:, :, :], AX.X, ALU.add))
                    step2(it, 3, nc.vector.tensor_scalar(total[:, :], total[:, :], 1e-9, None, ALU.add))
                    step2(it, 4, nc.vector.reciprocal(total[:, :], total[:, :]))
                    nc.vector.tensor_tensor(comb[:, :, :], comb[:, :, :], bc(total[:, :].unsqueeze(2), [P, G4, E]), ALU.mult)\
                        .then_inc(comb_ready, 1)

                def turn(it, s, last):
                    if not last:
                        normalise4(nc, K, v, it + 1, xn, xn_ready, xn_used)
                    for ch in range(1, CH):
                        gate(it, s, ch)
                        if not last:
                            if ch == 1:
                                shift_logits(it + 1)
                            elif ch == 2:
                                probabilities(it + 1)
                            elif ch == 3:
                                weights(it + 1)
                    if not last:
                        gate(it + 1, 1 - s, 0)
                    v.wait_ge(y_ready, done(CH * (it + 1)))
                    xs = K.x[:, bass.ds(G4 * it, G4), :]
                    nc.vector.scalar_tensor_tensor(out=xs, in0=K.J[:, 1, :].rearrange("p (j d) -> p j d", j=G4),
                                                   scalar=half_gate[:, 0:1], in1=xs, op0=ALU.mult, op1=ALU.add).then_inc(x_done, 1)
                    v.wait_ge(x_done, done(it + 1))
                    for j in range(G4):
                        nc.vector.bn_stats(K.st6[:, G4 * it + j, :], K.x[:, G4 * it + j, :])
                normalise4(nc, K, v, 0, xn, xn_ready, xn_used)
                v.wait_ge(rstd_ready, 2)
                shift_logits(0)
                probabilities(0)
                weights(0)
                gate(0, 0, 0)
                run_turns(v, turn)


def layer2_attention(nc, K, A):
    H, HD, NT = 16, 64, 8
    with ExitStack() as c:
        def sb(name, shape, dt=F32):
            return c.enter_context(nc.sbuf_tensor(f"l2_{name}", shape, dt))

        def sem(name):
            return c.enter_context(nc.semaphore(f"l2_{name}"))

        extra = (("k0", -5), ("n", -5), ("x", -4), ("q0", -3), ("o", 5), ("k1", -2), ("q1", -2), ("v0", -1), ("v1", 0),
                 ("f", 6))
        a = Attention(nc, c, "l2", 4, 2, 3, extra, ("k0", "k1", "v0", "v1", "x", "q0", "q1", "o"),
                      shared=("k0", "k1"))
        B = attn_buffers(nc, c, "l2")
        ctxT = sb("ctxT", [P, 2, 2, P])
        xn = sb("xn", [P, 2, D])
        xnT = sb("xnT", [P, 2, P])
        qT = sb("qT", [P, 2, NT, P])
        kz = sb("kz", [P, 2, NT, 2, P])
        vz = sb("vz", [P, 2, NT, 2, P])
        attnT = sb("attnT", [P, 2, NT, P])
        xb = sb("xb", [P, 2, D])
        neg_nullk = sb("neg_nullk", [P, 1])
        null_row = sb("null_row", [1, P])
        gscale = sb("gscale", [P, D])
        gbias = sb("gbias", [P, D])
        ost = sb("ost", [P, 2, 6])
        omv = sb("omv", [P, 2, 2])
        ovar = sb("ovar", [P, 2])
        orstd = sb("orstd", [P, 2])
        centred = sb("centred", [P, 2, D])
        ctx_loaded = [sem(f"ctx_loaded{k}") for k in range(2)]
        prepared = sem("prepared")
        null_ready = sem("null_row_ready")
        xb_ready = sem("xb_ready")
        ostat = sem("ostat")
        ostat_seen = sem("ostat_seen")
        orstd_ready = sem("orstd_ready")

        with nc.Block() as block:
            @block.sync
            def _(sp):
                with sp.Fori(0, TURNS2) as it:
                    for k in range(2):
                        sp.wait_ge(a.copied["v1"], done(2 * it + k - 1))
                        sp.dma_start(ctxT[:, k, :, :], A["ctxT"].rearrange("b (c p) t -> p b c t", p=P)[:, 2 * it + k, :, :])\
                            .then_inc(ctx_loaded[k], 16)

            @block.tensor
            def _(pe):
                start_counts(pe, [a.scores_ready, a.turned, a.summed, *a.j_ready.values()])
                pe.wait_ge(K.w_loaded[4], K.w_count[4])
                for t in range(NT):
                    m = nc.tensor.matmul(K.O[0:1, 0, 0:P], K.w["nullv"][:, 0:1], K.w["wout2"][:, t, :], start=(t == 0), stop=(t == NT - 1))
                m.then_inc(null_ready, 1)
                pe.wait_ge(prepared, 6)

                def step_of(it, step):
                    kind, k = step[0], step[1]
                    b = 2 * it + k
                    if kind in a.copied:
                        a.wait_bank(pe, it, kind, k)
                        J = K.J[:, a.j_bank(kind, k), :]
                    if kind in ("k0", "k1"):
                        if kind == "k0":
                            pe.wait_ge(ctx_loaded[k], 16 * it + 16)
                        for t in range(4):
                            f = P * (t + 4 * int(kind[1]))
                            for j in range(2):
                                m = nc.tensor.matmul(J[:, t * P:(t + 1) * P], K.w["wkv2"][:, j, f:f + P], ctxT[:, k, j, :],
                                                     start=(j == 0), stop=(j == 1))
                    elif kind in ("v0", "v1"):
                        f = H * HD + 512 * int(kind[1])
                        for j in range(2):
                            m = nc.tensor.matmul(J, ctxT[:, k, j, :], K.w["wkv2"][:, j, f:f + 512], start=(j == 0), stop=(j == 1))
                    elif kind == "x":
                        pe.wait_ge(a.xn_ready, done(b + 1))
                        m = nc.tensor.transpose(J[:, 0:P], xn[:, k, :], K.w["ident"][:, :])
                    elif kind in ("q0", "q1"):
                        pe.wait_ge(a.copied["x"], done(b + 1))
                        for t in range(4):
                            m = nc.tensor.matmul(J[:, t * P:(t + 1) * P], K.w["wq2"][:, t + 4 * int(kind[1]), :], xnT[:, k, :],
                                                 start=True, stop=True)
                    elif kind == "o":
                        nc.tensor.matmul(J[:, 0:P], K.ones_row[0:1, :], null_row[0:1, :], start=True, stop=False)
                        pe.wait_ge(a.normed, done(a.unit(it, k, 3) + 1))
                        for t in range(NT):
                            m = nc.tensor.matmul(J[:, 0:P], attnT[:, k, t, :], K.w["wout2"][:, t, :], start=False, stop=(t == NT - 1))
                    elif kind == "S":
                        g = step[2]
                        u = a.unit(it, k, g)
                        s = g % 2
                        if g % 2 == 0:
                            for need in (f"q{g // 2}", f"k{g // 2}"):
                                pe.wait_ge(a.copied[need], a.copied_at(need, b + 1))
                        pe.wait_ge(a.exp_ready, done(u - 1))
                        for i in range(2):
                            m = nc.tensor.matmul(K.S[:, s, 256 * i:256 * i + 256], qT[:, k, 2 * g + i, :],
                                                 kz[:, k, 2 * g + i, :, :], start=True, stop=True)
                        m.then_inc(a.scores_ready, 1)
                    elif kind == "T":
                        pe_turn(nc, K, pe, a, B, it, k, step[2], a.weighed)
                    elif kind == "V":
                        g = step[2]
                        if g % 2 == 0:
                            pe.wait_ge(a.copied[f"v{g // 2}"], done(b + 1))
                        u = a.unit(it, k, g)
                        pe.wait_ge(a.turned_copied, done(u + 1))
                        pe.wait_ge(a.normed, done(u - 1))
                        for i in range(2):
                            for e in range(2):
                                n = nc.tensor.matmul(K.O[:, g % 2, i * P:(i + 1) * P], vz[:, k, 2 * g + i, e, :],
                                                     B.expT[:, g % 2, 2 * i + e, :], start=(e == 0), stop=(e == 1))
                        n.then_inc(a.summed, 1)
                    if kind in a.copied:
                        m.then_inc(a.j_ready[kind], 1)
                a.run(pe, step_of)

            @block.vector
            def _(v):
                start_counts(v, [a.max_ready, a.shifted, a.recip_ready, a.weighed, a.x_done, ostat,
                                 a.copied["v0"], a.copied["v1"], a.copied["o"]])
                ln_statistics(nc, K, v, a.ln_chain)
                v.wait_ge(K.w_loaded[4], K.w_count[4])
                nc.vector.memset(vz[:, :, :, :, :], 0.0).then_inc(prepared, 1)
                nc.vector.memset(kz[:, :, :, :, :], 0.0).then_inc(prepared, 1)
                nc.vector.tensor_scalar(neg_nullk[:, :], K.w["nullk"][:, :], -1.0, None, ALU.mult).then_inc(prepared, 1)
                nc.vector.tensor_scalar(gscale[:, :], K.w["ln_scale"][:, :], K.tg[:, 2:3], None, ALU.mult).then_inc(prepared, 1)
                nc.vector.tensor_scalar(gbias[:, :], K.w["ln_bias"][:, :], K.tg[:, 2:3], None, ALU.mult).then_inc(prepared, 1)
                v.wait_ge(null_ready, 1)
                nc.vector.tensor_copy(null_row[0:1, :], K.O[0:1, 0, 0:P]).then_inc(prepared, 1)
                v.wait_ge(prepared, 6)

                def weigh(it, k, g):
                    u = a.unit(it, k, g)
                    s = g % 2
                    v.wait_ge(a.exp_ready, done(u + 1))
                    v.wait_ge(a.null_ready, done(u + 1))
                    nc.vector.tensor_tensor(B.rec[:, s, :], B.sum[:, s, :], B.null[:, g, :], ALU.add).then_inc(a.recip_ready, 1)
                    v.wait_ge(a.recip_ready, done(2 * u + 1))
                    nc.vector.reciprocal(B.rec[:, s, :], B.rec[:, s, :]).then_inc(a.recip_ready, 1)
                    v.wait_ge(a.recip_ready, done(2 * u + 2))
                    nc.vector.tensor_tensor(B.exp[:, s, :, :], B.exp[:, s, :, :], bc(B.rec[:, s, :].unsqueeze(2), [P, 4, P]),
                                            ALU.mult).then_inc(a.weighed, 1)

                def step_of(it, step):
                    kind, k = step[0], step[1]
                    b = 2 * it + k
                    if kind in ("k0", "k1"):
                        v.wait_ge(a.j_ready[kind], done(b + 1))
                        if kind == "k0":
                            v.wait_ge(a.scores_ready, done(a.unit(it, k, 3) + 1 - a.units))
                        t = 4 * int(kind[1])
                        J = K.J[64:128, a.j_bank(kind, k), :].rearrange("p (t q) -> p t q", t=4)
                        nc.vector.tensor_scalar(kz[64:128, k, t:t + 4, 1, :], J, K.w["nullk"][64:128, 0:1], None, ALU.subtract)\
                            .then_inc(a.copied[kind], 1)
                    elif kind in ("v0", "v1"):
                        v.wait_ge(a.j_ready[kind], done(b + 1))
                        if kind == "v0":
                            v.wait_ge(a.summed, done(a.unit(it, k, 3) + 1 - a.units))
                        t = 4 * int(kind[1])
                        J = K.J[:, a.j_bank(kind, k), :].rearrange("p (t e d) -> p t e d", t=4, e=2)
                        for e in range(2):
                            m = nc.vector.tensor_tensor(vz[:, k, t:t + 4, e, HD * e:HD * (e + 1)], J[:, :, e, :],
                                                        bc(K.w["nullv_row"][:, :].unsqueeze(1), [P, 4, HD]), ALU.subtract)
                        m.then_inc(a.copied[kind], 1)
                    elif kind == "S":
                        g = step[2]
                        dve_shift(nc, K, v, a, B, it, k, g, float(HD) ** -0.5, clamp=True)
                        before = (k, g - 1) if g > 0 else (1 - k, 3)
                        turn = it if (k, g) != (0, 0) else it - 1
                        if not isinstance(turn, int) or turn >= 0:
                            weigh(turn, *before)
                        if isinstance(it, int) and it == a.turns - 1 and (k, g) == (1, 3):
                            weigh(it, k, g)
                    elif kind == "o":
                        v.wait_ge(a.j_ready[kind], done(b + 1))
                        v.wait_ge(orstd_ready, done(b - 1))
                        nc.vector.bn_stats(ost[:, k, :], K.J[:, a.j_bank(kind, k), 0:P]).then_inc(ostat, 1)
                        v.wait_ge(ostat, done(3 * b + 1))
                        v.sem_inc(ostat_seen, 1)
                        nc.vector.bn_aggr(omv[:, k, :], ost[:, k, :]).then_inc(ostat, 1)
                        v.wait_ge(ostat, done(3 * b + 2))
                        nc.vector.tensor_scalar(ovar[:, k:k + 1], omv[:, k, 1:2], 1e-6, None, ALU.add).then_inc(ostat, 1)
                        nc.vector.scalar_tensor_tensor(out=centred[:, k, :], in0=K.J[:, a.j_bank(kind, k), 0:P],
                                                       scalar=omv[:, k, 0:1], in1=gscale[:, :], op0=ALU.subtract,
                                                       op1=ALU.mult).then_inc(a.copied["o"], 1)
                    elif kind == "f":
                        v.wait_ge(orstd_ready, done(b + 1))
                        v.wait_ge(xb_ready, done(b + 1))
                        v.wait_ge(a.copied["o"], done(b + 1))
                        nc.vector.scalar_tensor_tensor(out=K.x[:, b, :], in0=centred[:, k, :], scalar=orstd[:, k:k + 1],
                                                       in1=xb[:, k, :], op0=ALU.mult, op1=ALU.add).then_inc(a.x_done, 1)
                        v.wait_ge(a.x_done, done(b + 1))
                        nc.vector.bn_stats(K.st6[:, b, :], K.x[:, b, :])
                a.run(v, step_of)

            @block.scalar
            def _(act):
                start_counts(act, [a.exp_ready, a.null_ready, a.turned_copied, a.normed, a.copied["x"], a.copied["q0"], a.copied["q1"],
                                   a.copied["k0"], a.copied["k1"]])
                act.wait_ge(prepared, 6)

                def step_of(it, step):
                    kind, k = step[0], step[1]
                    b = 2 * it + k
                    if kind in ("x", "k0", "k1", "q0", "q1"):
                        act.wait_ge(a.j_ready[kind], done(b + 1))
                        J = K.J[:, a.j_bank(kind, k), :]
                        J4 = J.rearrange("p (t q) -> p t q", t=4)
                    if kind == "x":
                        act.wait_ge(a.copied["q1"], done(b - 1))
                        nc.scalar.copy(xnT[:, k, :], J[:, 0:P]).then_inc(a.copied["x"], 1)
                    elif kind in ("k0", "k1"):
                        if kind == "k0":
                            act.wait_ge(a.scores_ready, done(a.unit(it, k, 3) + 1 - a.units))
                        t = 4 * int(kind[1])
                        nc.scalar.activation(kz[0:64, k, t:t + 4, 0, :], J4[0:64, :, :], ACT.Identity,
                                             bias=neg_nullk[0:64, 0:1]).then_inc(a.copied[kind], 1)
                    elif kind in ("q0", "q1"):
                        if kind == "q0":
                            act.wait_ge(a.scores_ready, done(a.unit(it, k, 3) + 1 - a.units))
                        t = 4 * int(kind[1])
                        nc.scalar.copy(qT[:, k, t:t + 4, :], J4).then_inc(a.copied[kind], 1)
                    elif kind == "V":
                        g = step[2]
                        act.wait_ge(a.summed, done(a.unit(it, k, g) + 1))
                        if g == 0:
                            act.wait_ge(a.copied["o"], done(b - 1))
                        nc.scalar.copy(attnT[:, k, 2 * g:2 * g + 2, :], K.O[:, g % 2, 0:2 * P].rearrange("p (t q) -> p t q", t=2))\
                            .then_inc(a.normed, 1)
                    elif kind == "S":
                        act_exp(nc, K, act, a, B, it, k, step[2], float(HD) ** -0.5, null=True)
                    elif kind == "T":
                        act_copy_turned(nc, K, act, a, B, it, k, step[2])
                a.run(act, step_of, copies_first=True)

            @block.gpsimd
            def _(pool):
                start_counts(pool, [a.rstd_ready, a.centred_ready, a.xn_ready, xb_ready, orstd_ready])
                pool.wait_ge(a.ln_chain, 7)
                pool.wait_ge(prepared, 5)

                def step_of(it, step):
                    kind, k = step[0], step[1]
                    b = 2 * it + k
                    if kind == "n":
                        pool_normalise(nc, K, pool, a, xn, it, k)
                    elif kind == "v1":
                        pool.wait_ge(a.x_done, done(b - 1))
                        pool.sem_inc(a.wait_carried, 1)
                        nc.gpsimd.tensor_tensor(xb[:, k, :], K.x[:, b, :], gbias[:, :], ALU.add).then_inc(xb_ready, 1)
                    elif kind == "o":
                        pool.wait_ge(a.x_done, done(b - 1))
                        pool.wait_ge(ostat, done(3 * b + 3))
                        nc.gpsimd.tensor_tensor(orstd[:, k:k + 1], ovar[:, k:k + 1], K.neg_half[:, 0:1], ALU.pow)\
                            .then_inc(orstd_ready, 1)
                a.run(pool, step_of)


def layer2_ffn(nc, K, A):
    NG, GB = 4, 8
    H, HD = 16, 8
    W = HD + 1
    F = 512
    CH = F // P
    RC = 9
    LOWEST = -3.4028234663852886e38
    ROUND = 1.5 * 2.0 ** 23
    TWO_PI = (6.28125, 0.0019350051879882812, 3.0199159795074593e-07)
    with ExitStack() as c:
        def sb(name, shape, dt=F32):
            return c.enter_context(nc.sbuf_tensor(f"f2_{name}", shape, dt))

        def sem(name):
            return c.enter_context(nc.semaphore(f"f2_{name}"))

        xn = sb("xn", [P, NB, D])
        big = sb("big", [P, NB, P])
        big2 = sb("big2", [P, NB, P])
        kz = big2[:, :, :].rearrange("p (s h) t -> p s h t", s=2)
        wr = sb("wr", [P, NB])
        rest = sb("rest", [P, NB])
        wrT = sb("wrT", [NB, P])
        wrT_rest = sb("wrT_rest", [NB, P])
        top = sb("top", [NB, SEL])
        top_at = sb("top_at", [NB, SEL], U32)
        place = sb("place", [NB, SEL])
        place_diag = sb("place_diag", [NB, NB, SEL])
        limit_diag = sb("limit_diag", [NB, NB])
        sel = sb("sel", [P, NB, SEL])
        pos_i = sb("pos_i", [P, 4], I32)
        pos = sb("pos", [P, 4])
        ang = sb("ang", [P, 4, 4])
        turns = sb("turns", [P, 4, 4])
        cs = sb("cs", [P, 4, 8])
        tab = sb("tab", [P, NB, RC])
        maskr = sb("maskr", [P, 4, P])
        half = sb("half", [P, NB, SEL])
        madd = sb("madd", [P, NG, P])
        xsT = sb("xsT", [P, NG, P])
        tabT = sb("tabT", [RC, NG, P])
        xs = sb("xs", [P, NG, D])
        tabs = sb("tabs", [P, NG, RC])
        sq = sb("sq", [P, NG, D])
        ms = sb("ms", [P, NG])
        rs = sb("rs", [P, NG])
        qkv = sb("qkv", [P, NG, 3 * D])
        rope = sb("rope", [P, NG, 2 * H, HD])
        part = sb("part", [P, NG, 2 * H, 4])
        qT = sb("qT", [P, NG, P])
        kT = sb("kT", [P, NG, P])
        vx = sb("vx", [P, NG, H, W])
        attn = sb("attn", [P, NG, D])
        attnT = sb("attnT", [P, NG, P])
        hT = sb("hT", [P, CH, NG * P])
        wqkv = sb("wqkv", [P, 3 * D])
        w1 = sb("w1", [P, F])
        loaded = sem("loaded")
        ln_chain = sem("ln_chain")
        chain = sem("chain")
        event = {name: sem(name) for name in (
            "router", "places", "angles", "table", "folded", "xsT", "mask_rows", "ms1",
            "roped", "values", "ms2", "x1n", "result",
            "rstd", "rs1", "rs2", "padded", "x_kept", "xn_scaled",
            "sines", "tabT", "qkv_scaled", "qT", "kT", "attnT", "x1nT",
            "router_turned", "places_spread", "gathered", "half_masked", "turned_back",
            "masked", "projected", "q_turned", "k_turned",
            "attn_turned", "attn_projected", "x1_turned", "y")}
        kz_ready = sem("kz_ready")
        h_ready = sem("h_ready")
        gelu_ready = sem("gelu_ready")
        sel_turned = sem("sel_turned")
        selT_ready = sem("selT_ready")
        scattered = sem("scattered")
        x_done = sem("x_done")

        units = [(g, h) for g in range(NG) for h in range(4)]
        sched = [("S",) + units[0], ("S",) + units[1]]
        for i in range(len(units)):
            sched.append(("T",) + units[i])
            if i + 2 < len(units):
                sched.append(("S",) + units[i + 2])
            if i >= 1:
                sched.append(("V",) + units[i - 1])
        sched.append(("V",) + units[-1])
        a = Attention(nc, c, "f2a", 4, 4, 0, (), ())
        B = attn_buffers(nc, c, "f2a")
        masked = sb("masked", [P, 2, 4, P])
        qkv_banks = (K.S[:, 0, :], K.S[:, 1, :], K.O[:, 0, :], K.O[:, 1, :])
        by_group = lambda ap: ap.rearrange("p (g t) -> p g t", g=NG)

        with nc.Block() as block:
            @block.sync
            def _(sp):
                sp.dma_start(pos_i[:, :], A["posT"]).then_inc(loaded, 16)
                sp.dma_start(maskr[:, :, :], A["L2_ffn_attention_mask"].rearrange("b o q k -> q (b o) k")[0:P, :, 0:P])\
                    .then_inc(loaded, 16)
                for i in range(3):
                    sp.dma_start(K.kbias_rows[i:i + 1, :].rearrange("o (b k) -> o b k", b=NB), K.part32[:, i, :])\
                        .then_inc(K.kbias_moved, 16)
                sp.wait_ge(loaded, 32)

            @block.tensor
            def _(pe):
                start_counts(pe, [a.scores_ready, a.turned, a.summed, h_ready, sel_turned, scattered])
                pe.wait_ge(K.w_loaded[5], K.w_count[5])
                pe.wait_ge(loaded, 32)
                pe.wait_ge(event["router"], 1)
                nc.tensor.transpose(K.S[0:NB, 0, 0:P], wr[:, :], K.w["ident"][:, :]).then_inc(event["router_turned"], 1)
                pe.wait_ge(event["places"], 1)
                nc.tensor.matmul(K.S[:, 0, :], K.ones_f[0:NB, :], place_diag[:, :, :], start=True, stop=True)
                nc.tensor.matmul(K.S[:, 1, 0:NB], K.ones_f[0:NB, :], limit_diag[:, :], start=True, stop=True)\
                    .then_inc(event["places_spread"], 1)
                pe.wait_ge(event["table"], 1)
                for b in range(NB):
                    nc.tensor.matmul(K.J[:, 0, b * SEL:(b + 1) * SEL], xn[:, b, :], sel[:, b, :], start=True, stop=True)
                for b in range(NB):
                    m = nc.tensor.matmul(K.O[0:RC, 0, b * SEL:(b + 1) * SEL], tab[:, b, :], sel[:, b, :], start=True, stop=True)
                m.then_inc(event["gathered"], 1)
                for i in range(4):
                    b1 = i + 1 if i < 3 else NB
                    m = nc.tensor.matmul(K.S[:, 1, i * SEL:b1 * SEL], maskr[:, i, :], sel[:, i:b1, :], start=True, stop=True)
                m.then_inc(event["half_masked"], 1)
                pe.wait_ge(event["xsT"], 1)
                pe.wait_ge(event["tabT"], 1)
                for g in range(NG):
                    nc.tensor.transpose(K.T[:, 0, g * P:(g + 1) * P], xsT[:, g, :], K.w["ident"][:, :])
                for g in range(NG):
                    m = nc.tensor.transpose(K.T[:, 1, g * RC:(g + 1) * RC], tabT[0:RC, g, :], K.w["ident"][0:RC, 0:RC])
                m.then_inc(event["turned_back"], 1)
                pe.wait_ge(event["folded"], 1)
                pe.wait_ge(event["mask_rows"], 1)
                for g in range(NG):
                    m = nc.tensor.matmul(qkv_banks[g][:, 0:3 * D], xsT[:, g, :], wqkv[:, :], start=True, stop=True)
                m.then_inc(event["projected"], 1)
                for b in range(NB):
                    g = b // GB
                    m = nc.tensor.matmul(K.J[:, 1, b * SEL:(b + 1) * SEL], half[:, GB * g:GB * g + GB, :], sel[:, b, :],
                                         start=True, stop=True)
                m.then_inc(event["masked"], 1)
                pe.wait_ge(event["roped"], 1)
                for g in range(NG):
                    m = nc.tensor.transpose(K.J[:, 0, g * P:(g + 1) * P], rope[:, g, 0:H, :], K.w["ident"][:, :])
                m.then_inc(event["q_turned"], 1)
                for g in range(NG):
                    m = nc.tensor.transpose(K.T[:, 0, g * P:(g + 1) * P], rope[:, g, H:2 * H, :], K.w["ident"][:, :])
                m.then_inc(event["k_turned"], 1)
                pe.wait_ge(event["qT"], 1)
                pe.wait_ge(event["kT"], 1)
                pe.wait_ge(event["values"], 1)
                for kind, g, h in sched:
                    u = 4 * g + h
                    if kind == "S":
                        pe.wait_ge(kz_ready, done(u + 1))
                        pe.wait_ge(a.max_ready, done(2 * (u - 1)))
                        nc.tensor.matmul(K.S[:, u % 2, :], qT[:, g, :], kz[:, g % 2, 4 * h:4 * h + 4, :], start=True, stop=True)\
                            .then_inc(a.scores_ready, 1)
                    elif kind == "T":
                        pe_turn(nc, K, pe, a, B, 0, g, h, a.exp_ready)
                    elif kind == "V":
                        pe_values(nc, K, pe, a, B, 0, g, h, lambda i: vx[:, g, 4 * h + i, :], W)
                pe.wait_ge(a.normed, done(4 * NG))
                for g in range(NG):
                    m = nc.tensor.transpose(K.J[:, 0, g * P:(g + 1) * P], attn[:, g, :], K.w["ident"][:, :])
                m.then_inc(event["attn_turned"], 1)
                pe.wait_ge(event["attnT"], 1)
                for g in range(NG):
                    m = nc.tensor.matmul(K.J[:, 1, g * P:(g + 1) * P], attnT[:, g, :], K.w["wo2"][:, :], start=True, stop=True)
                m.then_inc(event["attn_projected"], 1)
                pe.wait_ge(event["padded"], NG)
                for t in range(TURNS4):
                    pe.wait_ge(selT_ready, done(t - 1))
                    for j in range(G4):
                        m = nc.tensor.transpose(K.T[:, t % 2, j * P:(j + 1) * P], big[:, G4 * t + j, :], K.w["ident"][:, :])
                    m.then_inc(sel_turned, 1)
                pe.wait_ge(event["x1n"], 1)
                for g in range(NG):
                    m = nc.tensor.transpose(K.J[:, 0, g * P:(g + 1) * P], sq[:, g, :], K.w["ident"][:, :])
                m.then_inc(event["x1_turned"], 1)
                pe.wait_ge(event["x1nT"], 1)
                for ch in range(CH):
                    pe.wait_ge(gelu_ready, done(ch - 1))
                    nc.tensor.matmul(K.S[:, ch % 2, :], w1[:, ch * P:(ch + 1) * P], attnT[:, :, :], start=True, stop=True)\
                        .then_inc(h_ready, 1)
                pe.wait_ge(gelu_ready, done(CH))
                for g in range(NG):
                    for ch in range(CH):
                        m = nc.tensor.matmul(K.O[:, 0, g * P:(g + 1) * P], hT[:, ch, g * P:(g + 1) * P], K.w["w2_2"][:, ch, :],
                                             start=(ch == 0), stop=(ch == CH - 1))
                m.then_inc(event["y"], 1)
                pe.wait_ge(event["result"], 1)
                for t in range(TURNS4):
                    pe.wait_ge(selT_ready, done(t + 1))
                    pe.wait_ge(x_done, done(t - 1))
                    for j in range(G4):
                        b = G4 * t + j
                        m = nc.tensor.matmul(K.S[:, t % 2, j * P:(j + 1) * P], big2[:, b, :], xs[:, b // GB, :], start=True, stop=True)
                    m.then_inc(scattered, 1)

            @block.scalar
            def _(act):
                start_counts(act, [a.exp_ready, a.turned_copied, selT_ready, gelu_ready])
                act.wait_ge(event["angles"], 1)
                nc.scalar.activation(cs[:, :, 4:8], ang[:, :, :], ACT.Sin).then_inc(event["sines"], 1)
                nc.scalar.activation(cs[:, :, 0:4], turns[:, :, :], ACT.Sin).then_inc(event["sines"], 1)
                act.wait_ge(event["gathered"], 1)
                nc.scalar.copy(tabT[:, :, :], by_group(K.O[0:RC, 0, :])).then_inc(event["tabT"], 1)
                act.wait_ge(event["rs1"], 1)
                act.wait_ge(event["projected"], 1)
                for g in range(NG):
                    nc.scalar.mul(qkv[:, g, :], qkv_banks[g][:, 0:3 * D], rs[:, g:g + 1]).then_inc(event["qkv_scaled"], 1)
                act.wait_ge(event["q_turned"], 1)
                nc.scalar.copy(qT[:, :, :], by_group(K.J[:, 0, :])).then_inc(event["qT"], 1)
                act.wait_ge(event["k_turned"], 1)
                nc.scalar.copy(kT[:, :, :], by_group(K.T[:, 0, :])).then_inc(event["kT"], 1)
                for kind, g, h in sched:
                    u = 4 * g + h
                    if kind == "S":
                        act.wait_ge(a.shifted, done(u + 1))
                        act.wait_ge(a.turned, done(u - 1))
                        nc.scalar.activation(B.exp[:, u % 2, :, :], masked[:, u % 2, :, :], ACT.Exp).then_inc(a.exp_ready, 1)
                    elif kind == "T":
                        act_copy_turned(nc, K, act, a, B, 0, g, h)
                act.wait_ge(event["attn_turned"], 1)
                nc.scalar.copy(attnT[:, :, :], by_group(K.J[:, 0, :])).then_inc(event["attnT"], 1)
                act.wait_ge(a.scores_ready, done(4 * NG))
                for t in range(TURNS4):
                    act.wait_ge(sel_turned, done(t + 1))
                    nc.scalar.copy(big2[:, G4 * t:G4 * t + G4, :], K.T[:, t % 2, :].rearrange("p (j t) -> p j t", j=G4))\
                        .then_inc(selT_ready, 1)
                act.wait_ge(event["x1_turned"], 1)
                nc.scalar.copy(attnT[:, :, :], by_group(K.J[:, 0, :])).then_inc(event["x1nT"], 1)
                for ch in range(CH):
                    act.wait_ge(h_ready, done(ch + 1))
                    nc.scalar.activation(hT[:, ch, :], K.S[:, ch % 2, :], ACT.Gelu_apprx_tanh).then_inc(gelu_ready, 1)

            @block.gpsimd
            def _(pool):
                start_counts(pool, [kz_ready])
                pool.wait_ge(ln_chain, 7)
                nc.gpsimd.tensor_tensor(K.rstd[:, :], K.var[:, :], K.neg_half[:, :], ALU.pow).then_inc(event["rstd"], 1)
                pool.wait_ge(event["ms1"], 1)
                nc.gpsimd.tensor_tensor(rs[:, :], ms[:, :], K.neg_half[:, 0:NG], ALU.pow).then_inc(event["rs1"], 1)
                pool.wait_ge(event["kT"], 1)
                for g in range(NG):
                    pool.wait_ge(a.scores_ready, done(4 * (g - 1)))
                    for h in range(0, H, 4):
                        nc.gpsimd.tensor_tensor(kz[:, g % 2, h:h + 4, :], bc(kT[:, g, :].unsqueeze(1), [P, 4, P]),
                                                bc(K.w["head8"][:, h:h + 4].unsqueeze(2), [P, 4, P]), ALU.mult).then_inc(kz_ready, 1)
                    own = slice(GB * g, GB * g + GB)
                    nc.gpsimd.tensor_tensor(big[:, own, :].rearrange("p b (k s) -> p b k s", s=SEL),
                                            bc(sel[:, own, :].unsqueeze(2), [P, GB, GB, SEL]),
                                            bc(K.w["eye8"][:, :, :].unsqueeze(3), [P, GB, GB, SEL]), ALU.mult).then_inc(event["padded"], 1)
                nc.gpsimd.tensor_tensor(xn[:, :, :], xn[:, :, :], bc(rest[:, :].unsqueeze(2), [P, NB, D]), ALU.mult)\
                    .then_inc(event["xn_scaled"], 1)
                pool.wait_ge(event["xn_scaled"], 1)
                nc.gpsimd.tensor_tensor(K.x[:, :, :], K.x[:, :, :], xn[:, :, :], ALU.add).then_inc(event["x_kept"], 1)
                pool.wait_ge(event["ms2"], 1)
                nc.gpsimd.tensor_tensor(rs[:, :], ms[:, :], K.neg_half[:, 0:NG], ALU.pow).then_inc(event["rs2"], 1)

            @block.vector
            def _(v):
                n = [0]

                def link(ins):
                    n[0] += 1
                    ins.then_inc(chain, 1)
                    v.wait_ge(chain, n[0])

                def tell(name):
                    v.sem_inc(event[name], 1)

                start_counts(v, [a.max_ready, a.shifted, a.recip_ready, a.normed, x_done])
                ln_statistics(nc, K, v, ln_chain)
                v.wait_ge(K.w_loaded[5], K.w_count[5])
                v.wait_ge(loaded, 32)
                link(nc.vector.tensor_tensor(xn[:, :, :], K.x[:, :, :], bc(K.mean[:, :].unsqueeze(2), [P, NB, D]), ALU.subtract))
                v.wait_ge(event["rstd"], 1)
                link(nc.vector.tensor_tensor(xn[:, :, :], xn[:, :, :], bc(K.rstd[:, :].unsqueeze(2), [P, NB, D]), ALU.mult))
                link(nc.vector.tensor_tensor(big[:, :, :], xn[:, :, :], bc(K.w["router2"][:, :].unsqueeze(1), [P, NB, D]), ALU.mult))
                link(nc.vector.tensor_reduce(wr[:, :], big[:, :, :], AX.X, ALU.add))
                link(nc.vector.tensor_scalar(wr[:, :], wr[:, :], K.w["router2_b"][:, 0:1], None, ALU.add))
                tell("router")
                link(nc.vector.tensor_copy(pos[:, :], pos_i[:, :]))
                link(nc.vector.tensor_tensor(ang[:, :, :], bc(pos[:, :].unsqueeze(2), [P, 4, 4]),
                                             bc(K.w["inv_freq"][:, :].unsqueeze(1), [P, 4, 4]), ALU.mult))
                link(nc.vector.tensor_scalar(turns[:, :, :], ang[:, :, :], 0.15915494309189535, ROUND, ALU.mult, ALU.add))
                link(nc.vector.tensor_scalar(turns[:, :, :], turns[:, :, :], -ROUND, None, ALU.add))
                for part_of_2pi in TWO_PI:
                    link(nc.vector.scalar_tensor_tensor(out=ang[:, :, :], in0=turns[:, :, :], scalar=-part_of_2pi,
                                                        in1=ang[:, :, :], op0=ALU.mult, op1=ALU.add))
                link(nc.vector.tensor_scalar(ang[:, :, :], ang[:, :, :], 3.1415925, -3.1415925, ALU.min, ALU.max))
                link(nc.vector.tensor_scalar(turns[:, :, :], ang[:, :, :], -1.0, None, ALU.mult))
                link(nc.vector.tensor_tensor(turns[:, :, :], turns[:, :, :], ang[:, :, :], ALU.max))
                link(nc.vector.tensor_scalar(turns[:, :, :], turns[:, :, :], -1.0, 1.5707963267948966, ALU.mult, ALU.add))
                tell("angles")
                link(nc.vector.tensor_scalar(wqkv[:, :], K.w["wqkv2"][:, :], K.w["ln1"][:, 0:1], None, ALU.mult))
                link(nc.vector.tensor_scalar(w1[:, :], K.w["w1_2"][:, :], K.w["ln2"][:, 0:1], None, ALU.mult))
                link(nc.vector.memset(vx[:, :, :, HD:W], 1.0))
                tell("folded")
                v.wait_ge(event["router_turned"], 1)
                link(nc.vector.tensor_copy(wrT[:, :], K.S[0:NB, 0, 0:P]))
                link(nc.vector.max(top[:, 0:8], wrT[:, :]))
                link(nc.vector.max_index(top_at[:, 0:8], top[:, 0:8], wrT[:, :]))
                link(nc.vector.match_replace(wrT_rest[:, :], top[:, 0:8], wrT[:, :], LOWEST))
                link(nc.vector.max(top[:, 8:16], wrT_rest[:, :]))
                link(nc.vector.max_index(top_at[:, 8:16], top[:, 8:16], wrT_rest[:, :]))
                link(nc.vector.tensor_copy(place[:, :], top_at[:, :]))
                link(nc.vector.memset(place[:, KEEP:SEL], -1.0))
                own = K.w["ident"][0:NB, 0:NB]
                link(nc.vector.tensor_tensor(place_diag[:, :, :], bc(place[:, :].unsqueeze(1), [NB, NB, SEL]),
                                             bc(own.unsqueeze(2), [NB, NB, SEL]), ALU.mult))
                link(nc.vector.tensor_tensor(limit_diag[:, :], bc(top[:, KEEP:SEL], [NB, NB]), own, ALU.mult))
                tell("places")
                v.wait_ge(event["places_spread"], 1)
                link(nc.vector.tensor_scalar(sel[:, :, :], K.S[:, 0, :].rearrange("p (b s) -> p b s", b=NB),
                                             K.w["token"][:, 0:1], None, ALU.is_equal))
                link(nc.vector.tensor_tensor(rest[:, :], wr[:, :], K.S[:, 1, 0:NB], ALU.is_le))
                link(nc.vector.tensor_scalar(rest[:, :], rest[:, :], K.tg[:, 6:7], None, ALU.mult))
                v.wait_ge(event["sines"], 2)
                link(nc.vector.tensor_copy(tab[:, 0:4, 0:8], cs[:, :, :]))
                link(nc.vector.tensor_copy(tab[:, 4:NB, 0:8], bc(cs[:, 3:4, :], [P, NB - 4, 8])))
                link(nc.vector.tensor_copy(tab[:, :, 8:9], wr[:, :].unsqueeze(2)))
                tell("table")
                v.wait_ge(event["gathered"], 1)
                link(nc.vector.tensor_copy(xsT[:, :, :], by_group(K.J[:, 0, :])))
                tell("xsT")
                v.wait_ge(event["half_masked"], 1)
                link(nc.vector.tensor_copy(half[:, :, :], K.S[:, 1, :].rearrange("p (b s) -> p b s", b=NB)))
                tell("mask_rows")
                v.wait_ge(event["turned_back"], 1)
                link(nc.vector.tensor_copy(xs[:, :, :], by_group(K.T[:, 0, :])))
                link(nc.vector.tensor_copy(tabs[:, :, :], K.T[:, 1, 0:NG * RC].rearrange("p (g r) -> p g r", g=NG)))
                link(nc.vector.tensor_tensor(sq[:, :, :], xs[:, :, :], xs[:, :, :], ALU.mult))
                link(nc.vector.tensor_reduce(ms[:, :], sq[:, :, :], AX.X, ALU.add))
                link(nc.vector.tensor_scalar(ms[:, :], ms[:, :], 1.0 / D, 1e-6, ALU.mult, ALU.add))
                tell("ms1")
                v.wait_ge(event["qkv_scaled"], NG)
                qk = qkv[:, :, 0:2 * D].rearrange("p g (h d) -> p g h d", d=HD)
                lo, hi = qk[:, :, :, 0:4], qk[:, :, :, 4:8]
                cos = bc(tabs[:, :, 0:4].unsqueeze(2), [P, NG, 2 * H, 4])
                sin = bc(tabs[:, :, 4:8].unsqueeze(2), [P, NG, 2 * H, 4])
                link(nc.vector.tensor_tensor(part[:, :, :, :], hi, sin, ALU.mult))
                link(nc.vector.tensor_tensor(rope[:, :, :, 0:4], lo, cos, ALU.mult))
                link(nc.vector.tensor_tensor(rope[:, :, :, 0:4], rope[:, :, :, 0:4], part[:, :, :, :], ALU.subtract))
                link(nc.vector.tensor_tensor(part[:, :, :, :], lo, sin, ALU.mult))
                link(nc.vector.tensor_tensor(rope[:, :, :, 4:8], hi, cos, ALU.mult))
                link(nc.vector.tensor_tensor(rope[:, :, :, 4:8], rope[:, :, :, 4:8], part[:, :, :, :], ALU.add))
                tell("roped")
                link(nc.vector.tensor_copy(vx[:, :, :, 0:HD], qkv[:, :, 2 * D:3 * D].rearrange("p g (h d) -> p g h d", d=HD)))
                tell("values")
                v.wait_ge(event["masked"], 1)
                link(nc.vector.tensor_tensor(madd[:, :, :], by_group(K.J[:, 1, :]), bc(K.w["block"][:, :].unsqueeze(1), [P, NG, P]), ALU.mult))
                link(nc.vector.tensor_tensor(madd[:, :, :], madd[:, :, :], bc(K.w["off_block"][:, :].unsqueeze(1), [P, NG, P]), ALU.add))
                for kind, g, h in sched:
                    u = 4 * g + h
                    s = u % 2
                    if kind == "S":
                        v.wait_ge(a.scores_ready, done(u + 1))
                        v.wait_ge(a.exp_ready, done(u - 1))
                        nc.vector.scalar_tensor_tensor(out=masked[:, s, :, :], in0=K.S[:, s, :].rearrange("p (h k) -> p h k", h=4),
                                                       scalar=float(HD) ** -0.5, in1=bc(madd[:, g, :].unsqueeze(1), [P, 4, P]),
                                                       op0=ALU.mult, op1=ALU.add).then_inc(a.max_ready, 1)
                        v.wait_ge(a.max_ready, done(2 * u + 1))
                        nc.vector.tensor_reduce(B.max[:, s, :], masked[:, s, :, :], AX.X, ALU.max).then_inc(a.max_ready, 1)
                        v.wait_ge(a.max_ready, done(2 * u + 2))
                        nc.vector.tensor_tensor(masked[:, s, :, :], masked[:, s, :, :],
                                                bc(B.max[:, s, :].unsqueeze(2), [P, 4, P]), ALU.subtract).then_inc(a.shifted, 1)
                    elif kind == "V":
                        dve_norm(nc, K, v, a, B, 0, g, h, attn[:, g, 32 * h:32 * h + 32].rearrange("p (h d) -> p h d", h=4), W)
                v.wait_ge(event["attn_projected"], 1)
                link(nc.vector.tensor_tensor(xs[:, :, :], xs[:, :, :], by_group(K.J[:, 1, :]), ALU.add))
                link(nc.vector.tensor_tensor(sq[:, :, :], xs[:, :, :], xs[:, :, :], ALU.mult))
                link(nc.vector.tensor_reduce(ms[:, :], sq[:, :, :], AX.X, ALU.add))
                link(nc.vector.tensor_scalar(ms[:, :], ms[:, :], 1.0 / D, 1e-6, ALU.mult, ALU.add))
                tell("ms2")
                v.wait_ge(event["rs2"], 1)
                link(nc.vector.tensor_tensor(sq[:, :, :], xs[:, :, :], bc(rs[:, :].unsqueeze(2), [P, NG, D]), ALU.mult))
                tell("x1n")
                v.wait_ge(event["y"], 1)
                link(nc.vector.tensor_tensor(xs[:, :, :], xs[:, :, :], by_group(K.O[:, 0, :]), ALU.add))
                link(nc.vector.tensor_tensor(xs[:, :, :], xs[:, :, :], bc(tabs[:, :, 8:9], [P, NG, D]), ALU.mult))
                tell("result")
                v.wait_ge(event["x_kept"], 1)
                for t in range(TURNS4):
                    to = K.x[:, G4 * t:G4 * t + G4, :]
                    v.wait_ge(scattered, done(t + 1))
                    nc.vector.scalar_tensor_tensor(out=to, in0=K.S[:, t % 2, :].rearrange("p (j d) -> p j d", j=G4),
                                                   scalar=K.tg[:, 6:7], in1=to, op0=ALU.mult, op1=ALU.add).then_inc(x_done, 1)
                    v.wait_ge(x_done, done(t + 1))
                    for j in range(G4):
                        nc.vector.bn_stats(K.st6[:, G4 * t + j, :], K.x[:, G4 * t + j, :])


def layer3_attention(nc, K, A):
    H, HD = 16, 8
    W = HD + 1
    with ExitStack() as c:
        def sb(name, shape, dt=F32):
            return c.enter_context(nc.sbuf_tensor(f"l3_{name}", shape, dt))

        def sem(name):
            return c.enter_context(nc.semaphore(f"l3_{name}"))

        a = Attention(nc, c, "l3", 4, 2, 2, (("x", -4), ("f", 5)), ("x",))
        B = attn_buffers(nc, c, "l3")
        kT = sb("kT", [P, 2, P])
        kz = sb("kz", [P, 2, H, P])
        vx = sb("vx", [P, 2, H, W])
        xn = sb("xn", [P, 2, D])
        qT = sb("qT", [P, 2, P])
        upd = sb("upd", [P, 2, D])
        keys_loaded = [sem(f"keys_loaded{k}") for k in range(2)]
        ones_set = sem("ones_set")
        keys_ready = sem("keys_ready")
        values_ready = sem("values_ready")

        with nc.Block() as block:
            @block.sync
            def _(sp):
                with sp.Fori(0, TURNS2) as it:
                    for k in range(2):
                        sp.wait_ge(keys_ready, done(2 * it + k - 1))
                        sp.dma_start(kT[:, k, :], A["ctxT"].rearrange("b (c p) t -> p b c t", p=P)[:, 2 * it + k, 0, :])\
                            .then_inc(keys_loaded[k], 16)

            @block.tensor
            def _(pe):
                start_counts(pe, [a.scores_ready, a.turned, a.summed, *a.j_ready.values()])
                pe.wait_ge(K.kbias_moved, 48)

                def step_of(it, step):
                    kind, k = step[0], step[1]
                    b = 2 * it + k
                    if kind == "x":
                        a.wait_bank(pe, it, kind, k)
                        pe.wait_ge(a.xn_ready, done(b + 1))
                        nc.tensor.transpose(K.J[:, a.j_bank(kind, k), 0:P], xn[:, k, :], K.w["ident"][:, :]).then_inc(a.j_ready[kind], 1)
                    elif kind == "S":
                        g = step[2]
                        u = a.unit(it, k, g)
                        s = g % 2
                        if g == 0:
                            pe.wait_ge(a.copied["x"], done(b + 1))
                            pe.wait_ge(keys_ready, done(b + 1))
                        pe.wait_ge(a.exp_ready, done(u - 1))
                        bias = bc(K.kbias_rows[0:3, bass.ds(b * P, P)].unsqueeze(1), [3, 4, P])
                        nc.tensor.matmul(K.S[:, s, :], qT[:, k, :], kz[:, k, 4 * g:4 * g + 4, :], start=True, stop=False)
                        nc.tensor.matmul(K.S[:, s, :], K.ones_bf[0:3, :], bias, start=False, stop=True)\
                            .then_inc(a.scores_ready, 1)
                    elif kind == "T":
                        pe_turn(nc, K, pe, a, B, it, k, step[2], a.exp_ready)
                    elif kind == "V":
                        g = step[2]
                        if g == 0:
                            pe.wait_ge(values_ready, done(b + 1))
                        pe_values(nc, K, pe, a, B, it, k, g, lambda h: vx[:, k, 4 * g + h, :], W)
                a.run(pe, step_of)

            @block.vector
            def _(v):
                start_counts(v, [a.max_ready, a.shifted, a.recip_ready, a.normed, a.x_done])
                nc.vector.memset(vx[:, :, :, HD:W], 1.0).then_inc(ones_set, 1)
                ln_statistics(nc, K, v, a.ln_chain)

                def step_of(it, step):
                    kind, k = step[0], step[1]
                    b = 2 * it + k
                    if kind == "S":
                        dve_shift(nc, K, v, a, B, it, k, step[2], 1.0)
                    elif kind == "V":
                        g = step[2]
                        dve_norm(nc, K, v, a, B, it, k, g,
                                 upd[:, k, 32 * g:32 * g + 32].rearrange("p (h d) -> p h d", h=4), W)
                    elif kind == "f":
                        v.wait_ge(a.normed, done(a.unit(it, k, 3) + 1))
                        nc.vector.scalar_tensor_tensor(out=K.x[:, b, :], in0=upd[:, k, :], scalar=K.tg[:, 3:4],
                                                       in1=K.x[:, b, :], op0=ALU.mult, op1=ALU.add).then_inc(a.x_done, 1)
                        v.wait_ge(a.x_done, done(b + 1))
                        nc.vector.bn_stats(K.st6[:, b, :], K.x[:, b, :])
                a.run(v, step_of)

            @block.scalar
            def _(act):
                start_counts(act, [a.exp_ready, a.turned_copied, a.copied["x"]])

                def step_of(it, step):
                    kind, k = step[0], step[1]
                    b = 2 * it + k
                    if kind == "x":
                        act.wait_ge(a.j_ready[kind], done(b + 1))
                        act.wait_ge(a.scores_ready, done(a.unit(it, k, 3) + 1 - a.units))
                        nc.scalar.mul(qT[:, k, :], K.J[:, a.j_bank(kind, k), 0:P], float(HD) ** -0.5).then_inc(a.copied["x"], 1)
                    elif kind == "S":
                        act_exp(nc, K, act, a, B, it, k, step[2], 1.0)
                    elif kind == "T":
                        act_copy_turned(nc, K, act, a, B, it, k, step[2])
                a.run(act, step_of, copies_first=True)

            @block.gpsimd
            def _(pool):
                start_counts(pool, [a.rstd_ready, a.centred_ready, a.xn_ready, keys_ready, values_ready])
                pool.wait_ge(a.ln_chain, 7)
                pool.wait_ge(ones_set, 1)
                pool_normalise(nc, K, pool, a, xn, 0, 0)

                def keys_values_rows(it, k):
                    b = 2 * it + k
                    pool.wait_ge(keys_loaded[k], 16 * it + 16)
                    pool.wait_ge(a.scores_ready, done(a.unit(it, k, 3) + 1 - a.units))
                    nc.gpsimd.tensor_tensor(kz[:, k, :, :], bc(kT[:, k, :].unsqueeze(1), [P, H, P]),
                                            bc(K.w["head8"][:, :].unsqueeze(2), [P, H, P]), ALU.mult).then_inc(keys_ready, 1)
                    pool.wait_ge(a.summed, done(a.unit(it, k, 3) + 1 - a.units))
                    nc.gpsimd.tensor_copy(vx[:, k, :, 0:HD], K.ctx[:, b, D:DC].rearrange("p (h d) -> p h d", h=H))\
                        .then_inc(values_ready, 1)
                    if k == 0:
                        pool_normalise(nc, K, pool, a, xn, it, 1)
                    elif not isinstance(it, int):
                        pool_normalise(nc, K, pool, a, xn, it + 1, 0)
                with pool.Fori(0, a.turns - 1) as it:
                    for k in range(2):
                        keys_values_rows(it, k)
                for k in range(2):
                    keys_values_rows(a.turns - 1, k)


def layer3_ffn(nc, K, A, out):
    CH = 4
    with ExitStack() as c:
        def sb(name, shape, dt=F32):
            return c.enter_context(nc.sbuf_tensor(f"f3_{name}", shape, dt))

        def sem(name):
            return c.enter_context(nc.semaphore(f"f3_{name}"))

        xn = sb("xn", [P, G4, D])
        xnT = sb("xnT", [P, 2, G4 * P])
        hidden = sb("hidden", [P, 2, G4 * P])
        w_con = sb("w_con", [P, CH, D])
        h_bias = sb("h_bias", [P, CH])
        y_bias = sb("y_bias", [1, D])
        ln_chain = sem("ln_chain")
        rstd_ready = sem("rstd_ready")
        xn_ready = sem("xn_ready")
        xn_used = sem("xn_used")
        xnT_ready = sem("xnT_ready")
        folded = sem("folded")
        prepared = sem("prepared")
        h_ready = sem("h_ready")
        gelu_ready = sem("gelu_ready")
        y_ready = sem("y_ready")
        x_done = sem("x_done")
        stored = sem("stored")

        with nc.Block() as block:
            @block.sync
            def _(sp):
                with sp.Fori(0, TURNS4) as it:
                    sp.wait_ge(x_done, done(it + 1))
                    sp.dma_start(out.rearrange("b t f -> t b f")[:, bass.ds(G4 * it, G4), :], K.x[:, bass.ds(G4 * it, G4), :])\
                        .then_inc(stored, 16)
                sp.wait_ge(stored, 16 * TURNS4)

            @block.gpsimd
            def _(pool):
                pool_rstd(nc, K, pool, ln_chain, rstd_ready)

            @block.tensor
            def _(pe):
                start_counts(pe, [xn_used, h_ready, y_ready])
                for ch in range(CH):
                    nc.tensor.transpose(K.O[:, 0, ch * P:(ch + 1) * P], K.w["down_rows"][:, 0, ch * P:(ch + 1) * P], K.w["ident"][:, :])
                for ch in range(CH):
                    m = nc.tensor.matmul(K.O[:, 1, ch:ch + 1], K.w["up_rows"][0:1, 1, ch * P:(ch + 1) * P], K.ones_row[0:1, 0:1],
                                         start=True, stop=True)
                m.then_inc(folded, 1)
                pe.wait_ge(prepared, 3)

                def rows(it):
                    pe.wait_ge(xn_ready, done(it + 1))
                    pe.wait_ge(xnT_ready, done(it))
                    for j in range(G4):
                        m = nc.tensor.transpose(K.T[:, 0, j * P:(j + 1) * P], xn[:, j, :], K.w["ident"][:, :])
                    m.then_inc(xn_used, 1)

                def first(it, s, ch):
                    if ch == 0:
                        pe.wait_ge(xnT_ready, done(it + 1))
                    pe.wait_ge(gelu_ready, done(CH * it + ch - 1))
                    nc.tensor.matmul(K.S[:, ch % 2, :], K.w["up_rows"][:, 0, ch * P:(ch + 1) * P], xnT[:, s, :],
                                     start=True, stop=True).then_inc(h_ready, 1)

                def turn(it, s, last):
                    pe.wait_ge(x_done, done(it - 1))
                    for ch in range(CH):
                        pe.wait_ge(gelu_ready, done(CH * it + ch + 1))
                        for j in range(G4):
                            m = nc.tensor.matmul(K.J[:, s, j * P:(j + 1) * P], hidden[:, ch % 2, j * P:(j + 1) * P],
                                                 w_con[:, ch, :], start=(ch == 0 and j == 0), stop=False, skip_group_check=True)
                        if ch == CH - 1:
                            for j in range(G4):
                                m = nc.tensor.matmul(K.J[:, s, j * P:(j + 1) * P], K.ones_row[0:1, :], y_bias[0:1, :],
                                                     start=False, stop=True, skip_group_check=True)
                        m.then_inc(y_ready, 1)
                        if ch + 2 < CH:
                            first(it, s, ch + 2)
                        elif not last:
                            first(it + 1, 1 - s, ch + 2 - CH)
                        if ch == 0 and not last:
                            rows(it + 1)
                rows(0)
                first(0, 0, 0)
                first(0, 0, 1)
                run_turns(pe, turn)

            @block.scalar
            def _(act):
                start_counts(act, [gelu_ready])
                act.wait_ge(prepared, 3)
                with act.Fori(0, TURNS4) as it:
                    for ch in range(CH):
                        act.wait_ge(h_ready, done(CH * it + ch + 1))
                        act.wait_ge(y_ready, done(CH * it + ch - 1))
                        nc.scalar.activation(hidden[:, ch % 2, :], K.S[:, ch % 2, :], ACT.Gelu, bias=h_bias[:, ch:ch + 1])\
                            .then_inc(gelu_ready, 1)

            @block.vector
            def _(v):
                ln_statistics(nc, K, v, ln_chain)
                start_counts(v, [xn_ready, xnT_ready, x_done])
                v.wait_ge(folded, 1)
                nc.vector.tensor_copy(w_con[:, :, :], K.O[:, 0, :].rearrange("p (c d) -> p c d", c=CH)).then_inc(prepared, 1)
                nc.vector.tensor_tensor(h_bias[:, :], K.O[:, 1, 0:CH], K.w["up_bias"][:, :], ALU.add).then_inc(prepared, 1)
                nc.vector.tensor_tensor(y_bias[0:1, :], K.w["b_con"][0:1, :], K.w["down_bias"][0:1, :], ALU.add).then_inc(prepared, 1)
                v.wait_ge(rstd_ready, 1)

                def copy_rows(it, s):
                    v.wait_ge(xn_used, done(it + 1))
                    v.wait_ge(h_ready, done(CH * (it - 1)))
                    nc.vector.tensor_copy(xnT[:, s, :], K.T[:, 0, :]).then_inc(xnT_ready, 1)

                def turn(it, s, last):
                    if not last:
                        normalise4(nc, K, v, it + 1, xn, xn_ready, xn_used)
                        copy_rows(it + 1, 1 - s)
                    v.wait_ge(y_ready, done(CH * (it + 1)))
                    xs = K.x[:, bass.ds(G4 * it, G4), :]
                    nc.vector.scalar_tensor_tensor(out=xs, in0=K.J[:, s, :].rearrange("p (j d) -> p j d", j=G4),
                                                   scalar=K.tg[:, 7:8], in1=xs, op0=ALU.mult, op1=ALU.add).then_inc(x_done, 1)
                normalise4(nc, K, v, 0, xn, xn_ready, xn_used)
                v.wait_ge(rstd_ready, 2)
                copy_rows(0, 0)
                run_turns(v, turn)




WEIGHTS = [
    [("ident", [P, P], "c_ident", None, False),
     ("head16", [P, 8], "c_head16", None, False),
     ("w_src", [P, 2, DC], "w_srcT", "(c p) o -> p c o", False),
     ("w_tgt", [P, P], "w_tgtT", None, False),
     ("w_out0", [P, 2, P], "w_out0T", "(c p) o -> p c o", False),
     ("b_srck", [P, 1], "b_srck", None, False),
     ("b_srcv", [1, P], "b_srcv", None, False),
     ("b_tgt", [P, 1], "b_tgt", None, False),
     ("b_out0", [1, P], "b_out0", None, False)],
    [("w_gate", [P, 8], "L0_ffn_W_gate", None, False),
     ("b_gate", [1, 8], "b_gate", None, False),
     ("w1_0", [P, 8, P], "W1T", None, False),
     ("w2_0", [P, 8, P], "W2T", None, False),
     ("b1_0", [P, 8], "b1T", None, False),
     ("b2_0", [8, P], "L0_ffn_b2", None, False)],
    [("w_in", [P, P], "w_inT", None, False),
     ("g_res", [P, 1], "g_res", None, False),
     ("b_in", [1, P], "b_in", None, False),
     ("g_init", [P, P], "g_init", None, True),
     ("iota_row", [P, P], "c_iota", None, True),
     ("iota_col", [P, 1], "c_iota_col", None, False)],
    [("router1", [P, 16], "L1_ffn_router_w", None, False),
     ("wg1", [P, 5, P], "wg1", None, False),
     ("wu1", [P, 5, P], "wu1", None, False),
     ("wd1", [P, 5, P], "wd1", None, False),
     ("spread", [16, 4, P], "c_spread", None, False)],
    [("wq2", [P, 8, P], "wq2", None, False),
     ("wkv2", [P, 2, 2048], "L2_xattn_Wkv", "(c p) o -> p c o", False),
     ("wout2", [P, 8, P], "L2_xattn_Wout", "(c p) o -> p c o", False),
     ("nullk", [P, 1], "nullk", None, False),
     ("nullv", [P, 1], "nullv", None, False),
     ("nullv_row", [P, 64], "nullv_row", None, True),
     ("ln_scale", [P, P], "ln_scale", None, True),
     ("ln_bias", [P, P], "ln_bias", None, True)],
    [("router2", [P, P], "router2", None, True),
     ("router2_b", [P, 1], "router2_b", None, True),
     ("token", [P, 1], "c_iota_col", None, False),
     ("inv_freq", [P, 4], "c_inv_freq", None, True),
     ("block", [P, P], "c_block", None, False),
     ("off_block", [P, P], "c_off_block", None, False),
     ("eye8", [P, 8, 8], "c_eye8", None, True),
     ("head8", [P, 16], "c_head8", None, False),
     ("wqkv2", [P, 3 * P], "wqkv2", None, False),
     ("ln1", [P, 1], "ln1", None, False),
     ("ln2", [P, 1], "ln2", None, False),
     ("wo2", [P, P], "L2_ffn_wo", None, False),
     ("w1_2", [P, 512], "L2_ffn_w1", None, False),
     ("w2_2", [P, 4, P], "L2_ffn_w2", "(c p) o -> p c o", False)],
    [],
    [("up_rows", [P, 2, 512], "up_rows", None, False),
     ("up_bias", [P, 4], "up_bias", None, False),
     ("b_con", [1, P], "b_con", None, False),
     ("down_bias", [1, P], "down_bias", None, False),
     ("down_rows", [P, 1, 512], "down_rows", None, False)],
]


def clear_semaphores(nc):
    free = sorted(int(s) for s in nc.released_uncleared_semaphores)
    with nc.Block() as block:
        @block.gpsimd
        def _(pool):
            first = free[0]
            for i, s in enumerate(free):
                if i + 1 == len(free) or free[i + 1] != s + 1:
                    pool.sem_clear(range(first, s + 1))
                    if i + 1 < len(free):
                        first = free[i + 1]


def program(nc, A, out):
    with ExitStack() as c:
        def sb(name, shape, dt=F32):
            return c.enter_context(nc.sbuf_tensor(name, shape, dt))

        def ps(name):
            return c.enter_context(nc.psum_tensor(name, [P, 2, 512], F32))

        def sem(name):
            return c.enter_context(nc.semaphore(name))

        early = ExitStack()
        short_lived = {name for group in WEIGHTS[:5] for name, *_ in group} - {"ident"}
        shapes = {name: shape for group in WEIGHTS for name, shape, *_ in group}
        weights = {name: sb("w_" + name, shape) for name, shape in shapes.items() if name not in short_lived}
        K = Buffers()
        K.ctx, K.ctx_loaded = sb("ctx", [P, NB, DC]), sem("context_loaded")
        K.x, K.st6 = sb("x", [P, NB, D]), sb("st6", [P, NB, 6])
        K.plug, K.hot = sb("plug", [P, NB]), sb("hot", [P, NB, P], BF16)
        K.st6c = sb("st6c", [P, NB, 6])
        K.mean, K.var, K.rstd = sb("mean", [P, NB]), sb("var", [P, NB]), sb("rstd", [P, NB])
        K.lna, K.lnb = sb("lna", [P, NB]), sb("lnb", [P, NB])
        K.tg, K.neg_half = sb("tg", [P, 8]), sb("neg_half", [P, NB])
        K.ones_row, K.ones_bf, K.ones_f = sb("ones_row", [1, P]), sb("ones_bf", [P, P], BF16), sb("ones_f", [P, P])
        K.neg32, K.part32 = sb("neg32", [NB, P], BF16), sb("part32", [NB, 3, P], BF16)
        K.S, K.T, K.O, K.J = ps("S"), ps("T"), ps("O"), ps("J")
        K.gates_ready = sem("gates_ready")
        K.w_loaded = [sem(f"weights{i}_loaded") for i in range(len(WEIGHTS))]
        K.w_count = [16 * len(w) for w in WEIGHTS]
        weights.update({name: early.enter_context(nc.sbuf_tensor("w_" + name, shapes[name], F32)) for name in shapes
                        if name in short_lived})
        K.w = weights

        def load_weights(engine, i):
            for name, shape, source, order, spread in WEIGHTS[i]:
                src = A[source] if not order else A[source].rearrange(order, p=P)
                if spread:
                    src = bc(src, shape)
                dst = weights[name]
                engine.dma_start(dst[tuple(slice(None) for _ in shape)], src).then_inc(K.w_loaded[i], 16)
        K.load_weights = load_weights
        setup_block(nc, K, A)
        layer0_attention(nc, K, A)
        layer0_ffn(nc, K, A)
        layer1_attention(nc, K, A)
        layer1_ffn(nc, K, A)
        clear_semaphores(nc)
        layer2_attention(nc, K, A)
        early.close()
        clear_semaphores(nc)
        K.kbias_rows, K.kbias_moved = sb("kbias_rows", [3, NB * P], BF16), sem("kbias_moved")
        layer2_ffn(nc, K, A)
        layer3_attention(nc, K, A)
        layer3_ffn(nc, K, A, out)




def laid_out(inputs):
    import numpy as np
    f = {n: np.asarray(v) for n, v in inputs.items()}
    d = {}
    for n in ("x", "g_xattn", "g_ffn", "mask_BxS2_fk1", "itok_Bx1_68_817", "L3_xattn_b"):
        d[n] = f[n]
    ctx = f["ctx_2048"]
    d["ctxT"] = ctx.transpose(0, 2, 1)
    d["maskT"] = f["mask_BxS2_fk1"].T
    d["w_srcT"] = f["L0_xattn_W_src"].T
    d["w_tgtT"] = f["L0_xattn_W_tgt"].T
    d["w_out0T"] = f["L0_xattn_W_out"].T
    d["b_srck"] = f["L0_xattn_b_src"][:D, None]
    d["b_srcv"] = f["L0_xattn_b_src"][None, D:]
    d["b_tgt"] = f["L0_xattn_b_tgt"][:, None]
    d["b_out0"] = f["L0_xattn_b_out"][None, :]
    d["L0_ffn_W_gate"] = f["L0_ffn_W_gate"]
    d["b_gate"] = f["L0_ffn_b_gate"][None, :]
    d["W1T"] = f["L0_ffn_W1"].transpose(1, 0, 2)
    d["W2T"] = f["L0_ffn_W2"].transpose(1, 0, 2)
    d["b1T"] = f["L0_ffn_b1"].T
    d["L0_ffn_b2"] = f["L0_ffn_b2"]
    d["up_w"] = f["L3_ffn_up_weights"].transpose(0, 2, 3, 1)[None]
    d["up_rows"] = np.concatenate([f["L3_ffn_W_exp"][:, None, :], np.broadcast_to(f["L3_ffn_b_exp"], (P, 1, 512))], axis=1)
    d["w_inT"] = f["L1_xattn_W_in"].T
    d["g_res"] = f["L1_xattn_g_res"][:, None]
    d["b_in"] = f["L1_xattn_b_in"][None, :]
    d["g_init"] = f["L1_xattn_g_init"][None, :D]
    d["ctx_2048"] = ctx
    d["lensT"] = f["mask_BxS2_if0"].T
    d["c_upto"] = (np.arange(P)[:, None] <= np.arange(P)[None, :]).astype(np.float32)
    d["c_iota_col"] = np.arange(P, dtype=np.float32)[:, None]
    d["L1_ffn_router_w"] = f["L1_ffn_router_w"]
    for g in "gu":
        shared, routed = f[f"L1_ffn_w{g}_s"], f[f"L1_ffn_w{g}_r"]
        d[f"w{g}1"] = np.concatenate([shared.transpose(1, 0, 2).reshape(P, 1, P),
                                      routed.transpose(1, 0, 2).reshape(P, 4, P)], axis=1)
    d["wd1"] = np.concatenate([f["L1_ffn_wd_s"].reshape(1, P, P), f["L1_ffn_wd_r"].reshape(4, P, P)]).transpose(1, 0, 2)
    d["c_spread"] = (np.arange(16)[:, None, None] == 4 * np.arange(4)[None, :, None] + np.arange(P)[None, None, :] // 32)\
        .astype(np.float32)
    d["down_w"] = f["L3_ffn_down_weights"].transpose(0, 2, 3, 1)[None]
    d["down_rows"] = f["L3_ffn_W_con"].T[:, None, :]
    d["wq2"] = f["L2_xattn_Wq"].reshape(P, 8, P)
    d["L2_xattn_Wkv"] = f["L2_xattn_Wkv"]
    d["L2_xattn_Wout"] = f["L2_xattn_Wout"]
    null = f["L2_xattn_null_kv"]
    d["nullk"] = np.concatenate([null[0], null[0]])[:, None]
    d["nullv"] = np.concatenate([null[1], null[1]])[:, None]
    d["nullv_row"] = null[1:2]
    d["ln_scale"] = f["L2_xattn_ln_scale"][None]
    d["ln_bias"] = f["L2_xattn_ln_bias"][None]
    d["c_head8"] = (np.arange(P)[:, None] // 8 == np.arange(16)[None, :]).astype(np.float32)
    d["up_bias"] = f["L3_ffn_up_bias"].reshape(4, P).T
    d["b_con"] = f["L3_ffn_b_con"][None]
    d["down_bias"] = f["L3_ffn_down_bias"][None]
    d["router2"] = f["L2_ffn_router_w"].T
    d["router2_b"] = f["L2_ffn_router_b"][None]
    d["wqkv2"] = np.concatenate([f["L2_ffn_wq"], f["L2_ffn_wk"], f["L2_ffn_wv"]], axis=1)
    d["ln1"], d["ln2"] = f["L2_ffn_ln1"][:, None], f["L2_ffn_ln2"][:, None]
    for n in ("L2_ffn_wo", "L2_ffn_w1", "L2_ffn_w2", "L2_ffn_attention_mask"):
        d[n] = f[n]
    d["posT"] = f["L2_ffn_position_ids"][:, :P].T
    d["c_inv_freq"] = (np.float32(1.0) / np.float32(10000.0) ** (np.arange(0, 8, 2, dtype=np.float32) / np.float32(8)))\
        .astype(np.float32)[None]
    row = np.arange(P)
    own = (row[:, None] // SEL == row[None, :] // SEL) & (row[None, :] % SEL != SEL - 1)
    d["c_block"] = own.astype(np.float32)
    d["c_off_block"] = np.where(own, 0.0, -BIG).astype(np.float32)
    d["c_eye8"] = np.eye(8, dtype=np.float32)[None]
    d["c_iota"] = np.arange(P, dtype=np.float32)[None, :]
    d["c_ident"] = np.eye(P, dtype=np.float32)
    d["c_head16"] = (np.arange(P)[:, None] // 16 == np.arange(8)[None, :]).astype(np.float32)
    return {n: np.ascontiguousarray(v) for n, v in d.items()}


def kernel(**inputs):
    import concourse.bacc as _bacc
    from concourse import mybir as _mybir
    from concourse.bass_utils import run_bass_kernel_spmd as _run

    nc = _bacc.Bacc("TRN2", target_bir_lowering=False, num_devices=1)
    arrays, A = {}, {}
    for name, a in laid_out(inputs).items():
        arrays[f"in_{name}"] = a
        A[name] = nc.dram_tensor(f"in_{name}", a.shape, _mybir.dt.from_np(a.dtype), kind="ExternalInput").ap()
    out = nc.dram_tensor("out_0", (NB, P, D), _mybir.dt.float32, kind="ExternalOutput").ap()
    program(nc, A, out)
    r = _run(nc, [arrays], core_ids=[0])
    return r.results[0]["out_0"]
```
